# Optimizing a Trainium2 kernel written in Bass

```python
import numpy as np
import jax
import jax.numpy as jnp

def _softmax(x, axis=-1):
    return jax.nn.softmax(x, axis=axis)

def _gelu(x):
    return jax.nn.gelu(x, approximate=True)

def _silu(x):
    return jax.nn.silu(x)

def _sigmoid(x):
    return jax.nn.sigmoid(x)

def _layernorm(x, axis=-1, eps=1e-05):
    m = jnp.mean(x, axis=axis, keepdims=True)
    v = jnp.var(x, axis=axis, keepdims=True)
    return (x - m) / jnp.sqrt(v + eps)

def _scatter_add(tgt, idx, src, axis=0):
    return tgt.at[idx].add(src)

def _segment_sum(src, seg, n):
    return jax.ops.segment_sum(src, seg, n)
kernel_name = 'mk_metaformer_d2_conv_nchw128_r4_d44d09'

def setup_inputs(seed: int=0):
    np.random.seed(seed)
    _w = jnp.asarray

    def _rec_inputs():
        import jax
        import jax.numpy as jnp
        _gk = jax.random.key(seed)
        x = 1.648e-05 + 1 * jax.random.normal(jax.random.fold_in(_gk, 1), (8, 32, 24, 24), jnp.float32)
        return x
    x = _rec_inputs()

    def _L0_conv_setup():
        import jax, jax.numpy as jnp
        import numpy as np
        import math
        HEAD = 4

        def _neighbors3x3(t):
            b, g, d, h, w = t.shape
            tp = jnp.pad(t, ((0, 0), (0, 0), (0, 0), (1, 1), (1, 1)))
            patches = [tp[:, :, :, dy:dy + h, dx:dx + w] for dy in range(3) for dx in range(3)]
            return jnp.stack(patches, axis=3)
        key = jax.random.key(seed)
        k1, k2 = jax.random.split(key)
        x = jax.random.normal(k1, (8, 32, 24, 24), dtype=jnp.float32)
        W_trans = jax.random.normal(k2, (96, 32), dtype=jnp.float32) * 0.05
        return {'x': x, 'W_trans': W_trans}
    _L0_conv_all = _L0_conv_setup()
    _L0_conv_in = {k: v for k, v in _L0_conv_all.items() if k in ('W_trans',)}
    del _L0_conv_all

    def _L0_ffn_setup():
        import jax, jax.numpy as jnp
        import numpy as np
        B, S, D, E, H, O, K = (128, 512, 32, 16, 128, 32, 8)
        key = jax.random.key(seed)
        k0, k1, k2, k3 = jax.random.split(key, 4)
        x = jax.random.normal(k0, (B, S, D), dtype=jnp.float32)
        gate_w = jax.random.normal(k1, (E, D), dtype=jnp.float32) * (1.0 / np.sqrt(D))
        gate_b = jnp.zeros((E,), dtype=jnp.float32)
        weight1 = jax.random.uniform(k2, (E, D + 1, H), dtype=jnp.float32, minval=-1.0, maxval=1.0) * (1.0 / np.sqrt(D + 1))
        weight2 = jax.random.uniform(k3, (E, H + 1, O), dtype=jnp.float32, minval=-1.0, maxval=1.0) * (1.0 / np.sqrt(H + 1))
        return {'x': x, 'gate_w': gate_w, 'gate_b': gate_b, 'weight1': weight1, 'weight2': weight2}
    _L0_ffn_all = _L0_ffn_setup()
    _L0_ffn_in = {k: v for k, v in _L0_ffn_all.items() if k in ('gate_w', 'gate_b', 'weight1', 'weight2')}
    del _L0_ffn_all

    def _L1_conv_setup():
        import jax, jax.numpy as jnp
        import numpy as np
        R = 9
        key = jax.random.key(seed)
        ks = jax.random.split(key, 9)
        B, Cin, Cout, H, W = (4, 32, 32, 90, 90)
        r2 = R * R
        x = jax.random.normal(ks[0], (B, Cin, H, W), dtype=jnp.float32)
        Wconv = jax.random.normal(ks[1], (Cout, Cin), dtype=jnp.float32) * 0.05
        bconv = jax.random.normal(ks[2], (Cout,), dtype=jnp.float32) * 0.05
        Wa = jax.random.normal(ks[3], (r2, r2), dtype=jnp.float32) * 0.05
        ba = jax.random.normal(ks[4], (r2,), dtype=jnp.float32) * 0.05
        Wb = jax.random.normal(ks[5], (r2, r2), dtype=jnp.float32) * 0.05
        bb = jax.random.normal(ks[6], (r2,), dtype=jnp.float32) * 0.05
        Wc = jax.random.normal(ks[7], (r2, r2), dtype=jnp.float32) * 0.05
        bc = jax.random.normal(ks[8], (r2,), dtype=jnp.float32) * 0.05
        return {'x': x, 'Wconv': Wconv, 'bconv': bconv, 'Wa': Wa, 'ba': ba, 'Wb': Wb, 'bb': bb, 'Wc': Wc, 'bc': bc}
    _L1_conv_all = _L1_conv_setup()
    _L1_conv_in = {k: v for k, v in _L1_conv_all.items() if k in ('Wconv', 'bconv', 'Wa', 'ba', 'Wb', 'bb', 'Wc', 'bc')}
    del _L1_conv_all

    def _L1_ffn_setup():
        import jax, jax.numpy as jnp
        import numpy as np
        NB, NOPS = (33, 19)
        D, H = (32, 128)
        B, S = (8, 256)
        CARRY_OPS = [0, 1, 2, 10, 11, 12, 13]

        def _build_masks():
            am = np.zeros((NB, NOPS), dtype=bool)
            fm = np.zeros((NB, NOPS), dtype=bool)
            fm[0, :] = True
            for b in range(1, 8):
                am[b, CARRY_OPS] = True
                fm[b, CARRY_OPS] = True
            am[8, [14, 15, 8, 9]] = True
            fm[8, [14, 15, 8, 9]] = True
            for b in range(16, 32):
                fm[b, [3, 4]] = True
            am[32, [10, 11, 12, 13]] = True
            fm[32, [5, 6, 7, 2, 4, 10, 11, 12, 13]] = True
            return (jnp.asarray(am), jnp.asarray(fm))
        key = jax.random.key(seed)
        ks = jax.random.split(key, 9)
        sd = 1.0 / np.sqrt(D)
        sh = 1.0 / np.sqrt(H)
        am, fm = _build_masks()
        return {'x': jax.random.normal(ks[0], (B, S, D), jnp.float32), 'ffn_w1': jax.random.normal(ks[1], (NB, NOPS, D, H), jnp.float32) * sd, 'ffn_b1': jnp.zeros((NB, NOPS, H), jnp.float32), 'ffn_w2': jax.random.normal(ks[2], (NB, NOPS, H, D), jnp.float32) * sh, 'ffn_b2': jnp.zeros((NB, NOPS, D), jnp.float32), 'wq': jax.random.normal(ks[3], (NB, NOPS, D, D), jnp.float32) * sd, 'wk': jax.random.normal(ks[4], (NB, NOPS, D, D), jnp.float32) * sd, 'wv': jax.random.normal(ks[5], (NB, NOPS, D, D), jnp.float32) * sd, 'wo': jax.random.normal(ks[6], (NB, NOPS, D, D), jnp.float32) * sd, 'attn_mask': am, 'ffn_mask': fm}
    _L1_ffn_all = _L1_ffn_setup()
    _L1_ffn_in = {k: v for k, v in _L1_ffn_all.items() if k in ('ffn_w1', 'ffn_b1', 'ffn_w2', 'ffn_b2', 'wq', 'wk', 'wv', 'wo', 'attn_mask', 'ffn_mask')}
    del _L1_ffn_all
    return {'x': x, 'L0_conv_W_trans': _L0_conv_in['W_trans'], 'L0_ffn_gate_w': _L0_ffn_in['gate_w'], 'L0_ffn_gate_b': _L0_ffn_in['gate_b'], 'L0_ffn_weight1': _L0_ffn_in['weight1'], 'L0_ffn_weight2': _L0_ffn_in['weight2'], 'L1_conv_Wconv': _L1_conv_in['Wconv'], 'L1_conv_bconv': _L1_conv_in['bconv'], 'L1_conv_Wa': _L1_conv_in['Wa'], 'L1_conv_ba': _L1_conv_in['ba'], 'L1_conv_Wb': _L1_conv_in['Wb'], 'L1_conv_bb': _L1_conv_in['bb'], 'L1_conv_Wc': _L1_conv_in['Wc'], 'L1_conv_bc': _L1_conv_in['bc'], 'L1_ffn_ffn_w1': _L1_ffn_in['ffn_w1'], 'L1_ffn_ffn_b1': _L1_ffn_in['ffn_b1'], 'L1_ffn_ffn_w2': _L1_ffn_in['ffn_w2'], 'L1_ffn_ffn_b2': _L1_ffn_in['ffn_b2'], 'L1_ffn_wq': _L1_ffn_in['wq'], 'L1_ffn_wk': _L1_ffn_in['wk'], 'L1_ffn_wv': _L1_ffn_in['wv'], 'L1_ffn_wo': _L1_ffn_in['wo'], 'L1_ffn_attn_mask': _L1_ffn_in['attn_mask'], 'L1_ffn_ffn_mask': _L1_ffn_in['ffn_mask']}

def reference(x, L0_conv_W_trans, L0_ffn_gate_w, L0_ffn_gate_b, L0_ffn_weight1, L0_ffn_weight2, L1_conv_Wconv, L1_conv_bconv, L1_conv_Wa, L1_conv_ba, L1_conv_Wb, L1_conv_bb, L1_conv_Wc, L1_conv_bc, L1_ffn_ffn_w1, L1_ffn_ffn_b1, L1_ffn_ffn_w2, L1_ffn_ffn_b2, L1_ffn_wq, L1_ffn_wk, L1_ffn_wv, L1_ffn_wo, L1_ffn_attn_mask, L1_ffn_ffn_mask):
    import jax
    import jax.numpy as jnp

    def _L0_conv_ref(x, W_trans):
        import jax, jax.numpy as jnp
        import numpy as np
        import math
        HEAD = 4

        def _neighbors3x3(t):
            b, g, d, h, w = t.shape
            tp = jnp.pad(t, ((0, 0), (0, 0), (0, 0), (1, 1), (1, 1)))
            patches = [tp[:, :, :, dy:dy + h, dx:dx + w] for dy in range(3) for dx in range(3)]
            return jnp.stack(patches, axis=3)
        b, cin, h, w = x.shape
        t = jnp.einsum('bchw,oc->bohw', x, W_trans)
        q, k, v = jnp.split(t, 3, axis=1)
        C = q.shape[1]
        d = C // HEAD
        q = q.reshape(b, HEAD, d, h, w)
        k = k.reshape(b, HEAD, d, h, w)
        v = v.reshape(b, HEAD, d, h, w)
        kn = _neighbors3x3(k)
        vn = _neighbors3x3(v)
        att = jnp.einsum('bgdhw,bgdnhw->bgnhw', q, kn) / math.sqrt(d)
        att = jax.nn.softmax(att, axis=2)
        out = jnp.einsum('bgnhw,bgdnhw->bgdhw', att, vn)
        return out.reshape(b, C, h, w)

    def _L0_ffn_ref(x, gate_w, gate_b, weight1, weight2):
        import jax, jax.numpy as jnp
        import numpy as np
        B, S, D, E, H, O, K = (128, 512, 32, 16, 128, 32, 8)
        Bn, Sn, Dn = x.shape
        logits = jnp.einsum('bsd,ed->bse', x, gate_w) + gate_b
        probs = jax.nn.softmax(logits, axis=1)
        vals, idx = jax.lax.top_k(probs.transpose(0, 2, 1), K)
        topv = vals.transpose(0, 2, 1)
        topi = idx.transpose(0, 2, 1)
        flat_idx = topi.reshape(Bn, K * E)
        gathered = jnp.take_along_axis(x, flat_idx[:, :, None], axis=1)
        gathered = gathered.reshape(Bn, K, E, Dn)
        pooled = jnp.einsum('bked,bke->bed', gathered, topv)
        ones = jnp.ones((E, Bn, 1), dtype=x.dtype)
        h = jnp.concatenate([pooled.transpose(1, 0, 2), ones], axis=-1)
        h = jax.nn.gelu(jnp.einsum('ebd,edh->ebh', h, weight1), approximate=False)
        h = jnp.concatenate([h, ones], axis=-1)
        out = jnp.einsum('ebh,eho->ebo', h, weight2)
        out = out.transpose(1, 0, 2)
        weighted = jnp.einsum('beo,bke->bkeo', out, topv).reshape(Bn, K * E, O)
        outputs = jnp.zeros((Bn, Sn, O), dtype=x.dtype)
        outputs = outputs.at[jnp.arange(Bn)[:, None], flat_idx].add(weighted)
        return outputs

    def _L1_conv_ref(x, Wconv, bconv, Wa, ba, Wb, bb, Wc, bc):
        import jax, jax.numpy as jnp
        import numpy as np
        R = 9
        r = R
        x = jnp.einsum('bchw,oc->bohw', x, Wconv) + bconv[None, :, None, None]
        B, C, H, W = x.shape
        padh = -H % r
        padw = -W % r
        x = jnp.pad(x, ((0, 0), (0, 0), (0, padh), (0, padw)))
        Hp, Wp = (H + padh, W + padw)
        h, w = (Hp // r, Wp // r)
        x = x.reshape(B, C, r, h, r, w).transpose(0, 1, 3, 5, 2, 4).reshape(B, C, h * w, r * r)
        a = x @ Wa.T + ba
        b = x @ Wb.T + bb
        c = x @ Wc.T + bc
        y = a @ (jnp.swapaxes(b, -1, -2) @ c) / r
        y = y.reshape(B, C, h, w, r, r).transpose(0, 1, 4, 2, 5, 3).reshape(B, C, Hp, Wp)
        return y[:, :, :Hp - padh, :Wp - padw]

    def _L1_ffn_ref(x, ffn_w1, ffn_b1, ffn_w2, ffn_b2, wq, wk, wv, wo, attn_mask, ffn_mask):
        import jax, jax.numpy as jnp
        import numpy as np
        NB, NOPS = (33, 19)
        D, H = (32, 128)
        B, S = (8, 256)
        CARRY_OPS = [0, 1, 2, 10, 11, 12, 13]

        def _build_masks():
            am = np.zeros((NB, NOPS), dtype=bool)
            fm = np.zeros((NB, NOPS), dtype=bool)
            fm[0, :] = True
            for b in range(1, 8):
                am[b, CARRY_OPS] = True
                fm[b, CARRY_OPS] = True
            am[8, [14, 15, 8, 9]] = True
            fm[8, [14, 15, 8, 9]] = True
            for b in range(16, 32):
                fm[b, [3, 4]] = True
            am[32, [10, 11, 12, 13]] = True
            fm[32, [5, 6, 7, 2, 4, 10, 11, 12, 13]] = True
            return (jnp.asarray(am), jnp.asarray(fm))
        scale = jnp.asarray(1.0 / np.sqrt(D), x.dtype)

        def step(h, p):
            op = jnp.argmax(h[0, 0, :NOPS])
            q = h @ p['wq'][op]
            k = h @ p['wk'][op]
            v = h @ p['wv'][op]
            attn = jax.nn.softmax(jnp.einsum('bqd,bkd->bqk', q, k) * scale, axis=-1)
            y = jnp.einsum('bqk,bkd->bqd', attn, v) @ p['wo'][op]
            h = jnp.where(p['am'][op], y, h)
            z = jax.nn.relu(h @ p['w1'][op] + p['b1'][op]) @ p['w2'][op] + p['b2'][op]
            h = jnp.where(p['fm'][op], z, h)
            return (h, None)
        xs = {'w1': ffn_w1, 'b1': ffn_b1, 'w2': ffn_w2, 'b2': ffn_b2, 'wq': wq, 'wk': wk, 'wv': wv, 'wo': wo, 'am': attn_mask, 'fm': ffn_mask}
        out, _ = jax.lax.scan(step, x, xs)
        return out

    def _gn(v, G=32, eps=1e-05):
        B_, C_, H_, W_ = v.shape
        g = v.reshape(B_, G, C_ // G, H_, W_)
        m = jnp.mean(g, axis=(2, 3, 4), keepdims=True)
        s = jnp.var(g, axis=(2, 3, 4), keepdims=True)
        return ((g - m) / jnp.sqrt(s + eps)).reshape(v.shape)

    def _ln_c(v, eps=1e-06):
        m = jnp.mean(v, axis=1, keepdims=True)
        s = jnp.var(v, axis=1, keepdims=True)
        return (v - m) / jnp.sqrt(s + eps)

    def _ln_t(v, eps=1e-05):
        m = jnp.mean(v, axis=-1, keepdims=True)
        s = jnp.var(v, axis=-1, keepdims=True)
        return (v - m) / jnp.sqrt(s + eps)

    def _to_tokens(v):
        B_, C_, H_, W_ = v.shape
        return v.reshape(B_, C_, H_ * W_).transpose(0, 2, 1)

    def _from_tokens(t, like):
        B_, C_, H_, W_ = like.shape
        return t.transpose(0, 2, 1).reshape(B_, C_, H_, W_)
    x = x + _L0_conv_ref(_ln_c(x), L0_conv_W_trans)
    t = _to_tokens(x)
    t = t + _L0_ffn_ref(_ln_t(t), L0_ffn_gate_w, L0_ffn_gate_b, L0_ffn_weight1, L0_ffn_weight2)
    x = _from_tokens(t, x)
    x = x + _L1_conv_ref(_ln_c(x), L1_conv_Wconv, L1_conv_bconv, L1_conv_Wa, L1_conv_ba, L1_conv_Wb, L1_conv_bb, L1_conv_Wc, L1_conv_bc)
    t = _to_tokens(x)
    t = t + _L1_ffn_ref(_ln_t(t), L1_ffn_ffn_w1, L1_ffn_ffn_b1, L1_ffn_ffn_w2, L1_ffn_ffn_b2, L1_ffn_wq, L1_ffn_wk, L1_ffn_wv, L1_ffn_wo, L1_ffn_attn_mask, L1_ffn_ffn_mask)
    x = _from_tokens(t, x)
    return x

_drawn_inputs = setup_inputs


def setup_inputs(seed=0):
    import zlib

    import numpy as np

    out = dict(_drawn_inputs(seed))
    spreads = {'L0_ffn_gate_b': (0.0, 2.0), 'L1_ffn_ffn_b1': (0.0, 0.8), 'L1_ffn_ffn_b2': (0.0, 0.8)}
    factors = {'L0_ffn_gate_w': 8.0,
     'L0_ffn_weight1': 8.0,
     'L0_ffn_weight2': 8.0,
     'L1_conv_Wconv': 6.748,
     'L1_conv_bconv': 8.0,
     'L1_conv_Wa': 7.107,
     'L1_conv_ba': 8.0,
     'L1_conv_Wb': 8.0,
     'L1_conv_bb': 8.0,
     'L1_conv_Wc': 7.995,
     'L1_conv_bc': 8.0,
     'L1_ffn_ffn_w1': 8.0,
     'L1_ffn_ffn_w2': 8.0}
    for name, (base, spread) in spreads.items():
        noise = np.random.default_rng([zlib.crc32(name.encode()), seed]).standard_normal(out[name].shape)
        drawn = base * np.exp(spread * noise) if base else spread * noise
        out[name] = jnp.asarray(drawn.astype(out[name].dtype))
    for name, factor in factors.items():
        out[name] = (out[name] * factor).astype(out[name].dtype)
    return out
```

```python
from contextlib import ExitStack

import concourse.bass as bass
import numpy as np
from concourse import mybir

B, C, HH, WW = 8, 32, 24, 24
S = HH * WW
P = 128
TB = P // C
T = B // TB
HS = S // 2
HEADS, HD, NBR = 4, C // 4, 9
PW = WW + 2
QS = S // 4
TRI = 3
E_, H1, K_ = 16, 128, 8
SC_, NCH = 96, S // 96
R, NP = 9, 3
R2, NPT = R * R, NP * NP
RV = HH // NP
V2 = RV * RV
BAND = NP * V2
GRP = P // NPT
NGRP = -(-B * C // GRP)
GW = GRP * NPT
NB_, NOPS = 33, 19
MWORDS = -(-NB_ * NOPS // 4)
NONE = 4 * 100
INV = 1.0 / R

_COLS = [("idn", P), ("cen", P), ("mean", T * 32), ("heads", T * P), ("hsum", T * 32), ("own", TB), ("blk", GW),
         ("ebias", P), ("obias", P), ("iop", NOPS), ("istep", NB_)]
OFF, _o = {}, 0
for _n, _w in _COLS:
    OFF[_n] = (_o, _o + _w)
    _o += _w
NCST = _o


def constant_table():
    t = np.zeros((P, NCST), np.float32)
    p = np.arange(P)

    def put(name, a):
        t[:a.shape[0], OFF[name][0]:OFF[name][0] + a.shape[1]] = a

    same = (p[:, None] // C == p[None, :] // C).astype(np.float32)
    put("idn", np.eye(P, dtype=np.float32))
    put("cen", np.eye(P, dtype=np.float32) - same / C)
    bg = p // HD
    for t_ in range(T):
        a = np.zeros((P, 32), np.float32)
        for g in range(HEADS):
            a[p, (t_ * TB + p // C) * HEADS + g] = np.float32(1 / C)
        t[:, OFF["mean"][0] + 32 * t_:OFF["mean"][0] + 32 * (t_ + 1)] = a
        a = np.zeros((P, 32), np.float32)
        a[p, t_ * TB * HEADS + bg] = 1
        t[:, OFF["hsum"][0] + 32 * t_:OFF["hsum"][0] + 32 * (t_ + 1)] = a
        b = np.zeros((P, P), np.float32)
        for q in range(4):
            b[32 * q + t_ * TB * HEADS + bg, p] = 1
        t[:, OFF["heads"][0] + P * t_:OFF["heads"][0] + P * (t_ + 1)] = b
    put("own", ((p[:, None] // E_) % TB == np.arange(TB)).astype(np.float32))
    g = np.arange(GW)
    put("blk", (g[:, None] // NPT == g[None, :] // NPT).astype(np.float32) * np.float32(INV))
    e = np.arange(E_)
    put("ebias", (e[:, None] == p[None, :] // B).astype(np.float32))
    put("obias", (e[:, None] == p[None, :] % E_).astype(np.float32))
    put("iop", np.arange(NOPS, dtype=np.float32)[None, :])
    put("istep", 4 * np.arange(NB_, dtype=np.float32)[None, :])
    return t


def metaformer(nc, x, L0_conv_W_trans, L0_ffn_gate_w, L0_ffn_gate_b, L0_ffn_weight1, L0_ffn_weight2,
               L1_conv_Wconv, L1_conv_bconv, L1_conv_Wa, L1_conv_ba, L1_conv_Wb, L1_conv_bb, L1_conv_Wc,
               L1_conv_bc, L1_ffn_ffn_w1, L1_ffn_ffn_b1, L1_ffn_ffn_w2, L1_ffn_ffn_b2, L1_ffn_wq, L1_ffn_wk,
               L1_ffn_wv, L1_ffn_wo, L1_ffn_attn_mask, L1_ffn_ffn_mask, consts, out, dbg=None):
    f32, i32, u32, u8 = mybir.dt.float32, mybir.dt.int32, mybir.dt.uint32, mybir.dt.uint8
    ALU, ACT, AX = mybir.AluOpType, mybir.ActivationFunctionType, mybir.AxisListType

    ctx = ExitStack()
    with ctx:
        def sb(name, shape, dt=f32):
            return ctx.enter_context(nc.sbuf_tensor(name, shape, dt))

        def sem(name):
            return ctx.enter_context(nc.semaphore(name))

        cst = sb("cst", [P, NCST])

        def con(name, rows=P, first=0):
            return cst[first:first + rows, OFF[name][0]:OFF[name][1]]

        idn = con("idn")
        prods = sb("prods", [P, T, NBR + 1, S])
        x_in = prods[:, :, NBR, :]
        xs = [None] + [sb(f"x{i}", [P, T, S]) for i in (1, 2, 3)]
        sq = sb("sq", [P, T, S])
        xc = sb("xc", [P, T, S])
        std = sb("std", [P, QS])
        rstd = sb("rstd", [P, QS])
        spread = sb("spread", [P, T, 4, P])
        y = sb("y", [P, T, S])
        q_sb = sb("q_sb", [P, T, S])
        kpad = sb("kpad", [P, T, HH + 2, PW])
        vpad = sb("vpad", [P, T, HH + 2, PW])
        w_nat = sb("w_nat", [96, C])
        gw_nat = sb("gw_nat", [E_, C])
        wc_nat = sb("wc_nat", [C, C])
        qkv_bd = sb("qkv_bd", [P, 3, P])
        gate_bd = sb("gate_bd", [P, TB * E_])
        conv_bd = sb("conv_bd", [P, P])
        att = sb("att", [P, NBR, QS])
        smax2 = sb("smax2", [P, 2, QS])
        smax = sb("smax", [P, QS])
        ssum = sb("ssum", [P, QS])
        srec = sb("srec", [P, QS])
        gb = sb("gb", [P, 1])
        logit = sb("logit", [P, S])
        rest = sb("rest", [P, S])
        ismine = sb("ismine", [P, S])
        prob = sb("prob", [P, S])
        pick = sb("pick", [P, S])
        top8 = sb("top8", [P, K_])
        ntop = sb("ntop", [P, 1])
        psum_ = sb("psum_", [P, 1])
        prec = sb("prec", [P, 1])
        yT = sb("yT", [SC_, NCH, T, P])
        pickT = sb("pickT", [SC_, NCH, P])
        pool_bd = sb("pool_bd", [P, TB, TB * B])
        ew1 = sb("ew1", [P, TB, H1])
        eb1 = sb("eb1", [E_, H1])
        ew2 = sb("ew2", [P, E_, C])
        eb2 = sb("eb2", [E_, C])
        hid = sb("hid", [P, H1])
        hidT = sb("hidT", [P, P])
        eoutT = sb("eoutT", [C, P])
        eout_bd = sb("eout_bd", [P, TB, C])
        wa = sb("wa", [R2, V2 + 1])
        wb = sb("wb", [R2, V2 + 1])
        wc = sb("wc", [R2, V2 + 1])
        wcT = sb("wcT", [V2 + 1, V2])
        mab = sb("mab", [V2 + 1, V2 + 1])
        bc_rows = sb("bc_rows", [V2, P])
        xT = sb("xT", [V2 + 1, B * C * NPT])
        uT = prods[0:V2 + 1, 0, 0:4, :].rearrange("k n s -> k (n s)")
        gram = sb("gram", [GW, NGRP, GW])
        cval = sb("cval", [GW, NGRP, V2])
        yvT = prods[0:V2, 0, 4:8, :].rearrange("k n s -> k (n s)")
        h = sb("h", [P, T, S])
        fw1 = sb("fw1", [P, TB, H1])
        fw2 = sb("fw2", [H1, C])
        fb1 = sb("fb1", [H1, 1])
        fb2 = sb("fb2", [P, 1])
        relu_h = prods[:, 0, 0:B, :]
        tab = sb("tab", [1, 1])
        eps5 = sb("eps5", [P, 1])
        eps6 = sb("eps6", [P, 1])
        mask32 = sb("mask32", [1, 2, MWORDS], i32)
        mask8 = mask32[:, :, :].bitcast(u8)
        maskf = sb("maskf", [1, 2, NB_ * NOPS])
        both = sb("both", [1, NB_ * NOPS])
        anyf = sb("anyf", [1, NB_ * NOPS])
        code = sb("code", [1, NB_, NOPS])
        row = sb("row", [1, C])
        rmax = sb("rmax", [1, 8])
        ridx = sb("ridx", [1, 8], u32)
        opf = sb("opf", [1, 1])
        hot = sb("hot", [1, NOPS])
        csel = sb("csel", [1, NB_, NOPS])
        cand = sb("cand", [1, NB_])
        late = sb("late", [1, NB_])
        cand2 = sb("cand2", [1, NB_])
        nextf = sb("nextf", [1, 1])
        ctrl = sb("ctrl", [1, 2], i32)
        h0 = prods[0:C, 1, 0:B, :]
        hb = sq[0:C, 0, 0:S]
        qT_ = sq[0:C, 1, 0:S]
        kT_ = prods[0:C, 0, 0, :]
        vk = q_sb[0:SC_, 0, 0:NCH * C].rearrange("k (c d) -> k c d", c=NCH)
        qi = sb("qi", [C, SC_])
        nmax = sb("nmax", [SC_, 2])
        prow = prods[0:SC_, 0, 1, :]
        arow = prods[0:SC_, 0, 2, :]
        rsum = sb("rsum", [SC_, 1])
        rrec = sb("rrec", [SC_, 1])
        aT = q_sb[0:SC_, 1, :].rearrange("k (c q) -> k c q", c=NCH)
        oT = prods[0:C, 0, 3, :]
        aw = sb("aw", [C, 4, C])

        PS = ctx.enter_context(nc.psum_tensor("PS", [P, 8, 512], f32))

        x_ld = [sem(f"x_ld{t}") for t in range(T)]
        c1_in, c2_in, w_ld, wconv_ld, ew_ld, mask_ld, out_st = (
            sem(n) for n in ("c1_in", "c2_in", "w_ld", "wconv_ld", "ew_ld", "mask_ld", "out_st"))
        border0, eps_set, bd_zero, xT_ones, code_st = (
            sem(n) for n in ("border0", "eps_set", "bd_zero", "xT_ones", "code_st"))
        wT_done, wT_copied, mab_done, mab_copied, spread_zero, spread_rdy = (
            sem(n) for n in ("wT_done", "wT_copied", "mab_done", "mab_copied", "spread_zero", "spread_rdy"))
        xc_rdy, xc_copied, sq_rdy, var_rdy, std_rdy, rstd_rdy, rwide_rdy, y_rdy = (
            sem(n) for n in ("xc_rdy", "xc_copied", "sq_rdy", "var_rdy", "std_rdy", "rstd_rdy", "rwide_rdy", "y_rdy"))
        qkv_done, qkv_rdy, prod_rdy, score_rdy, smax_rdy, sdiff_rdy, sexp_rdy, ssum_rdy, att_rdy = (
            sem(n) for n in ("qkv_done", "qkv_rdy", "prod_rdy", "score_rdy", "smax_rdy", "sdiff_rdy", "sexp_rdy",
                             "ssum_rdy", "att_rdy"))
        wide_rdy, wide_used, pair_rdy, trio_rdy, last_trio, acc_rdy, x1_rdy, x2_rdy, x3_rdy = (
            sem(n) for n in ("wide_rdy", "wide_used", "pair_rdy", "trio_rdy", "last_trio", "acc_rdy", "x1_rdy", "x2_rdy", "x3_rdy"))
        logit_done, logit_rdy, yT_done, yT_rdy, top_rdy, ntop_rdy, rest_rdy, mine_rdy, prob_rdy, prec_rdy = (
            sem(n) for n in ("logit_done", "logit_rdy", "yT_done", "yT_rdy", "top_rdy", "ntop_rdy", "rest_rdy",
                             "mine_rdy", "prob_rdy", "prec_rdy"))
        pick_rdy, pickT_done, pickT_rdy, pool_done, pool_dve, pool_act, hid_done, hid_rdy, hidT_done, hidT_rdy = (
            sem(n) for n in ("pick_rdy", "pickT_done", "pickT_rdy", "pool_done", "pool_dve", "pool_act", "hid_done",
                             "hid_rdy", "hidT_done", "hidT_rdy"))
        eo_done, eo_rdy, eoT_done, eobd_rdy, scat_done = (
            sem(n) for n in ("eo_done", "eo_rdy", "eoT_done", "eobd_rdy", "scat_done"))
        pT_done, xT_rdy, u_done, u_rdy, gram_done, gram_rdy, cval_rdy, yv_done, yv_rdy, back_done = (
            sem(n) for n in ("pT_done", "xT_rdy", "u_done", "u_rdy", "gram_done", "gram_rdy", "cval_rdy", "yv_done",
                             "yv_rdy", "back_done"))
        h_upd, row_done, row_rdy, ctl_step, ctrl_rdy, fw_ld, aw_ld = (
            sem(n) for n in ("h_upd", "row_done", "row_rdy", "ctl_step", "ctrl_rdy", "fw_ld", "aw_ld"))
        f1_done, f1_act, f1_dve, z_done, fin_rdy = (
            sem(n) for n in ("f1_done", "f1_act", "f1_dve", "z_done", "fin_rdy"))
        waited = sem("waited")
        at_pe, at_dve, at_act = (sem(n) for n in ("at_pe", "at_dve", "at_act"))

        def half(t, first=0):
            return PS[:, first + 2 * t:first + 2 * t + 2, 0:HS]

        def cut(a, t):
            return a[:, t, 0:S].rearrange("p (g s) -> p g s", g=2)

        def patches(a, i):
            return a.rearrange("p (r i c j) -> p i j r c", r=RV, i=NP, c=RV)[:, i, :, :, :]

        def band(first, i):
            return PS[:, first + i // 2, (i % 2) * BAND:(i % 2 + 1) * BAND].rearrange("p (j r c) -> p j r c", j=NP, r=RV)

        def rows24(a, t):
            return a.rearrange("p g (r c) -> p g r c", c=WW)

        def inner(a, t):
            return a[:, t, 1:1 + HH, 1:1 + WW].rearrange("p (g r) c -> p g r c", g=2)

        QKV = [(0, 0, 0), (1, 0, 4), (0, 1, 2), (1, 1, 6), (2, 0, 0), (2, 1, 2)]
        WIDE = T * NBR // TRI
        last_w = (B * C - (NGRP - 1) * GRP) * NPT
        QUADS = [(g, min(4, NGRP - g)) for g in range(0, NGRP, 4)]
        GRAM_BANK = [0, 1, 2, 3, 4]
        CVAL_BANK = [5, 6, 7, 0, 1]
        YV_BANK = [5, 6, 7, 2, 3]
        BACK_BANK = [0, 4]
        UCH = 384
        NU = B * C * NPT // UCH
        APE_I, ADVE_I, AACT_I = 3, 7, 1
        APE_B, ADVE_B, AACT_B = 2 + NCH * APE_I, 3 + NCH * ADVE_I, NCH * AACT_I
        FW_DMAS = 16 * (2 * TB + 2)
        ADVE_R = 1 + B * ADVE_B

        def pool_src(j, e):
            a = PS[j * C:(j + 1) * C, 3, 0:2 * TB * E_].rearrange("c (t b g e) -> c b e g t", t=T, b=TB, e=TB)
            return a[:, j, e, :, :]

        def pool_dst(j, e):
            a = pool_bd[e * C:(e + 1) * C, :, :].rearrange("c g (e t b) -> c e b g t", e=TB, t=T)
            return a[:, e, j, :, :]

        x_sem = (None, x1_rdy, x2_rdy, x3_rdy)
        y_sem = (y_rdy, y_rdy, y_rdy, h_upd)

        def gw_of(g):
            return GW if g < NGRP - 1 else last_w

        def wait_for(eng, signal, value):
            eng.wait_ge(signal, value)
            if not isinstance(value, int):
                eng.sem_inc(waited, 1)

        block = ctx.enter_context(nc.Block())

        @block.sync
        def _(sp):
            sp.dma_start(cst[:, 0:OFF["hsum"][0]], consts[:, 0:OFF["hsum"][0]]).then_inc(c1_in, 16)
            for t in range(T):
                sp.dma_start(x_in[:, t, :], x[t * TB:(t + 1) * TB].rearrange("b c h w -> (b c) (h w)")).then_inc(x_ld[t], 16)
            sp.dma_start(cst[:, OFF["hsum"][0]:], consts[:, OFF["hsum"][0]:]).then_inc(c2_in, 16)
            for i, (w, b) in enumerate(((L1_conv_Wa, L1_conv_ba), (L1_conv_Wb, L1_conv_bb), (L1_conv_Wc, L1_conv_bc))):
                dst = (wa, wb, wc)[i]
                sp.dma_start(dst[:, 0:V2].rearrange("o (r c) -> o r c", r=RV),
                             w.rearrange("o (r c) -> o r c", r=R)[:, 0:RV, 0:RV]).then_inc(wconv_ld, 16)
                sp.dma_start(dst[:, V2:V2 + 1], b.rearrange("(p o) -> p o", o=1)).then_inc(wconv_ld, 16)
            for j in range(TB):
                sp.dma_start(bc_rows[:, j * C:(j + 1) * C], L1_conv_bconv.partition_broadcast(V2)).then_inc(wconv_ld, 16)
            for e in range(TB):
                sp.dma_start(ew1[e * C:(e + 1) * C, :, :],
                             L0_ffn_weight1[e::TB, 0:C, :].rearrange("g c h -> c g h")).then_inc(ew_ld, 16)
            sp.dma_start(eb1[:, :], L0_ffn_weight1[:, C, :]).then_inc(ew_ld, 16)
            sp.dma_start(ew2[:, :, :], L0_ffn_weight2[:, 0:H1, :].rearrange("e h c -> h e c")).then_inc(ew_ld, 16)
            sp.dma_start(eb2[:, :], L0_ffn_weight2[:, H1, :]).then_inc(ew_ld, 16)

            steps, cr, row_no = (sp.alloc_register(n) for n in ("sp_steps", "sp_code", "sp_row"))
            sp.reg_mov(steps, 0)
            sp.wait_ge(ctrl_rdy, 1)
            sp.wait_ge(border0, 1)
            sp.reg_load(cr, ctrl[0:1, 0:1])
            with sp.While(lambda: sp.snap(cr) < NONE):
                c_ = sp.snap(cr, min_val=0, max_val=4 * NB_ - 1)
                o_ = sp.value_load(ctrl[0:1, 1:2], min_val=0, max_val=NOPS - 1)
                sp.reg_mov(row_no, (c_ >> 2) * NOPS + o_)
                rw = sp.snap(row_no, min_val=0, max_val=NB_ * NOPS - 1)

                def of_step(w):
                    if len(w.shape) == 4:
                        return w.rearrange("b o c d -> (b o) c d")[bass.ds(rw, 1), :, :].rearrange("o c d -> (o c) d")
                    return w.rearrange("b o c -> (b o) c")[bass.ds(rw, 1), :].rearrange("o c -> c o")

                with sp.If((c_ & 2) > 0):
                    for i, w in enumerate((L1_ffn_wq, L1_ffn_wk, L1_ffn_wv, L1_ffn_wo)):
                        sp.dma_start(aw[:, i, :], of_step(w)).then_inc(aw_ld, 16)
                with sp.If((c_ & 1) > 0):
                    for j in range(TB):
                        sp.dma_start(fw1[j * C:(j + 1) * C, j, :], of_step(L1_ffn_ffn_w1)).then_inc(fw_ld, 16)
                    sp.dma_start(fb1[:, :], of_step(L1_ffn_ffn_b1)).then_inc(fw_ld, 16)
                    sp.dma_start(fw2[:, :], of_step(L1_ffn_ffn_w2)).then_inc(fw_ld, 16)
                    for j in range(TB):
                        sp.dma_start(fb2[j * C:(j + 1) * C, :], of_step(L1_ffn_ffn_b2)).then_inc(fw_ld, 16)
                sp.reg_add(steps, steps, 1)
                wait_for(sp, ctrl_rdy, sp.snap(steps) + 1)
                sp.reg_load(cr, ctrl[0:1, 0:1])

            for t in range(T):
                sp.wait_ge(fin_rdy, t + 1)
                sp.dma_start(out[t * TB:(t + 1) * TB].rearrange("b c h w -> (b c) (h w)"), y[:, t, :]).then_inc(out_st, 16)
            sp.wait_ge(out_st, 16 * T)

        @block.gpsimd
        def _(pool):
            nc.gpsimd.memset(eps6[:, :], 1e-6)
            nc.gpsimd.memset(tab[:, :], 0.0)
            nc.gpsimd.memset(eps5[:, :], 1e-5).then_inc(eps_set, 1)
            nc.gpsimd.memset(qkv_bd[:, :, :], 0.0)
            nc.gpsimd.memset(gate_bd[:, :], 0.0)
            nc.gpsimd.memset(conv_bd[:, :], 0.0).then_inc(bd_zero, 1)
            nc.gpsimd.memset(kpad[:, :, :, :], 0.0)
            nc.gpsimd.memset(pool_bd[:, :, :], 0.0)
            nc.gpsimd.memset(fw1[:, :, :], 0.0)
            nc.gpsimd.memset(vpad[:, :, :, :], 0.0).then_inc(border0, 1)
            pool.wait_ge(border0, 1)
            nc.gpsimd.memset(xT[V2:V2 + 1, :], 1.0).then_inc(xT_ones, 1)
            pool.wait_ge(xT_ones, 1)
            pool.wait_ge(mask_ld, 32)
            pool.wait_ge(c2_in, 16)
            nc.gpsimd.tensor_copy(maskf[:, :, :], mask8[:, :, 0:NB_ * NOPS]).then_inc(code_st, 1)
            pool.wait_ge(code_st, 1)
            am, fm = maskf[:, 0, :], maskf[:, 1, :]
            nc.gpsimd.tensor_tensor(both[:, :], am, fm, ALU.mult)
            nc.gpsimd.tensor_tensor(anyf[:, :], am, fm, ALU.add).then_inc(code_st, 1)
            pool.wait_ge(code_st, 2)
            bits = code[:, :, :].rearrange("p b o -> p (b o)")
            nc.gpsimd.tensor_tensor(bits, anyf[:, :], am, ALU.add).then_inc(code_st, 1)
            pool.wait_ge(code_st, 3)
            nc.gpsimd.tensor_tensor(anyf[:, :], anyf[:, :], both[:, :], ALU.subtract).then_inc(code_st, 1)
            nc.gpsimd.tensor_tensor(code[:, :, :], code[:, :, :],
                                    con("istep", 1).unsqueeze(2).to_broadcast([1, NB_, NOPS]), ALU.add).then_inc(code_st, 1)
            pool.wait_ge(code_st, 5)
            nc.gpsimd.tensor_scalar(bits, bits, -float(NONE), None, ALU.add).then_inc(code_st, 1)
            pool.wait_ge(code_st, 6)
            nc.gpsimd.tensor_tensor(bits, bits, anyf[:, :], ALU.mult).then_inc(code_st, 1)
            pool.wait_ge(code_st, 7)
            nc.gpsimd.tensor_scalar(bits, bits, float(NONE), None, ALU.add).then_inc(code_st, 1)

            for u in range(WIDE - 1):
                t, m3 = divmod(u, NBR // TRI)
                a, c = prods[:, t, m3 * TRI, :], prods[:, t, m3 * TRI + 2, :]
                pool.wait_ge(pair_rdy, u + 1)
                nc.gpsimd.tensor_tensor(a, a, c, ALU.add).then_inc(trio_rdy, 1)
                pool.wait_ge(trio_rdy, u + 1)
                if m3 == NBR // TRI - 1:
                    nc.gpsimd.tensor_tensor(xs[1][:, t, :], x_in[:, t, :], a, ALU.add).then_inc(x1_rdy, 1)
                    pool.sem_inc(acc_rdy, 1)
                else:
                    nc.gpsimd.tensor_tensor(x_in[:, t, :], x_in[:, t, :], a, ALU.add).then_inc(acc_rdy, 1)
                    pool.wait_ge(acc_rdy, u + 1)

        @block.tensor
        def _(pe):
            def layernorm(i, src):
                for t in range(T):
                    pe.wait_ge(*((x_ld[t], 16) if i == 0 else (x_sem[i], t + 1)))
                    for g in range(2):
                        last = nc.tensor.matmul(PS[:, 2 * t + g, 0:HS], con("cen"), cut(src, t)[:, g, :], start=True, stop=True)
                    last.then_inc(xc_rdy, 1)
                mean = con("mean").rearrange("p (t m) -> p t m", t=T)
                for t in range(T):
                    pe.wait_ge(sq_rdy, T * i + t + 1)
                    for q in range(4):
                        last = nc.tensor.matmul(PS[32 * q:32 * q + 32, 4, 0:QS], mean[:, t, :], sq[:, t, q * QS:(q + 1) * QS],
                                                start=(t == 0), stop=(t == T - 1), skip_group_check=True)
                last.then_inc(var_rdy, 1)
                pe.wait_ge(rstd_rdy, i + 1)
                for t in range(T):
                    for q in range(4):
                        last = nc.tensor.matmul(PS[:, 4 + 2 * t + q // 2, (q % 2) * QS:(q % 2 + 1) * QS], spread[:, t, q, :],
                                                rstd[:, :], start=True, stop=True)
                    last.then_inc(rwide_rdy, 1)

            pe.wait_ge(c1_in, 16)
            pe.wait_ge(w_ld, 16 * 4)
            nc.tensor.transpose(PS[0:C, 7, 0:96], w_nat[:, :], idn[0:96, 0:96])
            nc.tensor.transpose(PS[0:C, 7, 96:96 + E_], gw_nat[:, :], idn[0:E_, 0:E_])
            nc.tensor.transpose(PS[0:C, 7, 112:112 + C], wc_nat[:, :], idn[0:C, 0:C]).then_inc(wT_done, 1)
            pe.wait_ge(wT_copied, 1)
            pe.wait_ge(spread_rdy, 1)
            layernorm(0, x_in)

            def qkv_product(i):
                w, t, bank = QKV[i]
                pe.wait_ge(y_rdy, t + 1)
                for g in range(2):
                    last = nc.tensor.matmul(PS[:, bank + g, 0:HS], qkv_bd[:, w, :], cut(y, t)[:, g, :], start=True, stop=True)
                last.then_inc(qkv_done, 1)

            for i in range(4):
                qkv_product(i)

            pe.wait_ge(c2_in, 16)
            pe.wait_ge(qkv_rdy, 2)
            hsum = con("hsum").rearrange("p (t m) -> p t m", t=T)
            for t in range(T):
                for n in range(NBR):
                    if t == 0 and n == 2 * TRI:
                        pe.wait_ge(qkv_rdy, 4)
                    pe.wait_ge(prod_rdy, NBR * t + n + 1)
                    for q in range(4):
                        last = nc.tensor.matmul(PS[32 * q:32 * q + 32, 4 + n // TRI, (n % TRI) * QS:(n % TRI + 1) * QS],
                                                hsum[:, t, :], prods[:, t, n, q * QS:(q + 1) * QS],
                                                start=(t == 0 and n % TRI == 0), stop=(t == T - 1), skip_group_check=True)
                    if t == T - 1 and n % TRI == TRI - 1:
                        last.then_inc(score_rdy, 1)
            qkv_product(4)
            qkv_product(5)

            pe.wait_ge(wconv_ld, 16 * 10)
            nc.tensor.matmul(PS[0:V2 + 1, 7, 0:V2 + 1], wa[:, :], wb[:, :], start=True, stop=True)
            nc.tensor.transpose(PS[0:V2 + 1, 7, 128:128 + R2], wc[:, :], idn[0:R2, 0:R2]).then_inc(mab_done, 1)

            pe.wait_ge(qkv_rdy, 6)
            pe.wait_ge(mab_copied, 1)
            for u in range(WIDE):
                t, m = divmod(u, NBR // TRI)
                if t == 0:
                    pe.wait_ge(att_rdy, m + 1)
                if u >= 2:
                    pe.wait_ge(wide_used, u - 1)
                for q in range(4):
                    last = nc.tensor.matmul(PS[:, 4 * (u % 2) + q, 0:TRI * QS], spread[:, t, q, :],
                                            att[:, m * TRI:(m + 1) * TRI, :], start=True, stop=True)
                last.then_inc(wide_rdy, 1)

            pe.wait_ge(wide_used, WIDE - 1)
            layernorm(1, xs[1])
            for t in range(T):
                pe.wait_ge(y_rdy, T + t + 1)
            for g in range(2):
                for t in range(T):
                    last = nc.tensor.matmul(PS[64 * t:64 * t + 64, 4 + g, 0:HS], gate_bd[:, :], cut(y, t)[:, g, :],
                                            start=True, stop=True)
            last.then_inc(logit_done, 1)
            for c in range(NCH):
                for t in range(T):
                    last = nc.tensor.transpose(PS[0:SC_, c // 2, ((c % 2) * T + t) * P:((c % 2) * T + t + 1) * P],
                                               y[:, t, c * SC_:(c + 1) * SC_], idn)
                if c % 2:
                    last.then_inc(yT_done, 1)
            pe.wait_ge(pick_rdy, 1)
            for c in range(NCH):
                last = nc.tensor.transpose(PS[0:SC_, 6 + c // 4, (c % 4) * P:(c % 4 + 1) * P], pick[:, c * SC_:(c + 1) * SC_], idn)
                if c in (3, NCH - 1):
                    last.then_inc(pickT_done, 1)
            pe.wait_ge(yT_rdy, 3)
            for t in range(T):
                for c in range(NCH):
                    pe.wait_ge(pickT_rdy, 1 + c // 4)
                    last = nc.tensor.matmul(PS[:, 3, 64 * t:64 * t + 64], yT[:, c, t, :], pickT[:, c, 64 * t:64 * t + 64],
                                            start=(c == 0), stop=(c == NCH - 1))
            last.then_inc(pool_done, 1)
            pe.wait_ge(ew_ld, 16 * 7)
            nc.tensor.matmul(PS[:, 0, 0:H1], con("ebias", E_), eb1[:, :], start=True, stop=False, skip_group_check=True)
            pe.wait_ge(pool_dve, 1)
            pe.wait_ge(pool_act, 1)
            for g in range(TB):
                last = nc.tensor.matmul(PS[32 * g:32 * g + 32, 0, 0:H1], pool_bd[:, g, :], ew1[:, g, :],
                                        start=False, stop=True, skip_group_check=True)
            last.then_inc(hid_done, 1)
            nc.tensor.matmul(PS[0:C, 2, 0:P], eb2[:, :], con("obias", E_), start=True, stop=False, skip_group_check=True)
            pe.wait_ge(hid_rdy, 1)
            nc.tensor.transpose(PS[:, 1, 0:P], hid[:, :], idn).then_inc(hidT_done, 1)
            pe.wait_ge(hidT_rdy, 1)
            for e in range(E_):
                last = nc.tensor.matmul(PS[0:C, 2, e:e + E_ * (B - 1) + 1:E_], ew2[:, e, :], hidT[:, e * B:(e + 1) * B],
                                        start=False, stop=True, skip_group_check=True)
            last.then_inc(eo_done, 1)
            pe.wait_ge(eo_rdy, 1)
            nc.tensor.transpose(PS[:, 3, 256:256 + C], eoutT[:, :], idn[0:C, 0:C]).then_inc(eoT_done, 1)
            pe.wait_ge(eobd_rdy, 1)
            for t in range(T):
                rows = slice(TB * E_ * t, TB * E_ * (t + 1))
                for i in range(NP):
                    last = nc.tensor.matmul(band(4 + 2 * t, i), eout_bd[rows, :, :], patches(pick[rows, :], i), start=True, stop=True)
                last.then_inc(scat_done, 1)

            layernorm(2, xs[2])
            for t in range(T):
                pe.wait_ge(y_rdy, 2 * T + t + 1)
            for p in range(NPT):
                for t in range(T):
                    last = nc.tensor.matmul(PS[0:V2, p // 2, ((p % 2) * T + t) * P:((p % 2) * T + t + 1) * P],
                                            y[:, t, p * V2:(p + 1) * V2], conv_bd[:, :],
                                            start=True, stop=True)
                if p % 2 or p == NPT - 1:
                    last.then_inc(pT_done, 1)
            pe.wait_ge(xT_rdy, 5)
            for i in range(NU):
                nc.tensor.matmul(PS[0:V2 + 1, (5 + i) % 8, 0:UCH], mab[:, :], xT[:, i * UCH:(i + 1) * UCH],
                                 start=True, stop=True).then_inc(u_done, 1)
            pe.wait_ge(u_rdy, NU)

            def gram_quad(k):
                g0, n = QUADS[k]
                for i in range(n):
                    w = gw_of(g0 + i)
                    cols = slice((g0 + i) * GW, (g0 + i) * GW + w)
                    nc.tensor.matmul(PS[0:w, GRAM_BANK[k], i * GW:i * GW + w], xT[:, cols], uT[:, cols], start=True, stop=True)
                    last = nc.tensor.matmul(PS[0:w, CVAL_BANK[k], i * V2:(i + 1) * V2], xT[:, cols], wcT[:, :],
                                            start=True, stop=True)
                last.then_inc(gram_done, 1)

            def yv_quad(k):
                g0, n = QUADS[k]
                pe.wait_ge(gram_rdy, k + 1)
                pe.wait_ge(cval_rdy, k + 1)
                for i in range(n):
                    w = gw_of(g0 + i)
                    last = nc.tensor.matmul(PS[0:V2, YV_BANK[k], i * GW:i * GW + w], cval[0:w, g0 + i, :],
                                            gram[0:w, g0 + i, 0:w], start=True, stop=True)
                last.then_inc(yv_done, 1)

            for k in range(3):
                gram_quad(k)
            yv_quad(0)
            gram_quad(3)
            yv_quad(1)
            gram_quad(4)
            for k in (2, 3, 4):
                yv_quad(k)
            pe.wait_ge(yv_rdy, 5)
            yv3 = yvT[:, :].rearrange("k (b p) -> k b p", p=NPT)
            for t in range(T):
                for p in range(NPT):
                    last = nc.tensor.transpose(PS[:, BACK_BANK[t] + p // 6, (p % 6) * V2:(p % 6 + 1) * V2],
                                               yv3[:, t * P:(t + 1) * P, p], idn[0:V2, 0:V2])
                last.then_inc(back_done, 1)

            layernorm(3, xs[3])

            def second(k, nf):
                t, j = divmod(k, TB)
                wait_for(pe, (f1_act, f1_dve)[k % 2], nf * (B // 2) + k // 2 + 1)
                for g in range(2):
                    last = nc.tensor.matmul(PS[j * C:(j + 1) * C, 4 + 2 * t + g, 0:HS], fw2[:, :],
                                            relu_h[:, k, g * HS:(g + 1) * HS], start=True, stop=True)
                if j == TB - 1:
                    last.then_inc(z_done, 1)

            runs_a, runs_f, steps = (pe.alloc_register(n) for n in ("pe_a", "pe_f", "pe_s"))
            cr = pe.alloc_register("pe_code")
            for r in (runs_a, runs_f, steps):
                pe.reg_mov(r, 0)
            pe.wait_ge(h_upd, T)
            nc.tensor.transpose(PS[0:1, 7, 0:C], h[0:C, 0, 0:1], idn[0:C, 0:C]).then_inc(row_done, 1)
            pe.wait_ge(ctrl_rdy, 1)
            pe.reg_load(cr, ctrl[0:1, 0:1])
            with pe.While(lambda: pe.snap(cr) < NONE):
                c_ = pe.snap(cr, min_val=0, max_val=4 * NB_ - 1)
                with pe.If((c_ & 2) > 0):
                    na = pe.snap(runs_a, min_val=0, max_val=NB_)
                    wait_for(pe, aw_ld, na * 64 + 64)
                    with pe.Fori(0, B) as b:
                        d0 = na * ADVE_R + b * ADVE_B + 1
                        wait_for(pe, at_dve, d0 + 1)
                        for g in range(2):
                            for i in range(2):
                                nc.tensor.matmul(PS[0:C, 2 * i + g, 0:HS], aw[:, i, :], hb[:, g * HS:(g + 1) * HS], start=True, stop=True)
                        for c in range(NCH):
                            last = nc.tensor.matmul(PS[0:SC_, 4, c * C:(c + 1) * C], hb[:, c * SC_:(c + 1) * SC_], aw[:, 2, :],
                                                    start=True, stop=True)
                        last.then_inc(at_pe, 1)
                        with pe.Fori(0, NCH) as i:
                            di = d0 + i * ADVE_I + 2
                            wait_for(pe, at_dve, di + 1)
                            for g in range(2):
                                last = nc.tensor.matmul(PS[0:SC_, g, 0:HS], qi[:, :], kT_[:, g * HS:(g + 1) * HS], start=True, stop=True)
                            last.then_inc(at_pe, 1)
                            wait_for(pe, at_dve, di + 5)
                            for c in range(NCH):
                                last = nc.tensor.transpose(PS[0:SC_, 2 + c // 3, (c % 3) * SC_:(c % 3 + 1) * SC_],
                                                           arow[:, c * SC_:(c + 1) * SC_], idn[0:SC_, 0:SC_])
                            last.then_inc(at_pe, 1)
                            wait_for(pe, at_dve, di + 6)
                            for c in range(NCH):
                                last = nc.tensor.matmul(PS[0:C, 5, 0:SC_], vk[:, c, :], aT[:, c, :], start=(c == 0), stop=(c == NCH - 1))
                            last.then_inc(at_pe, 1)
                        wait_for(pe, at_dve, d0 + 2 + NCH * ADVE_I)
                        for g in range(2):
                            last = nc.tensor.matmul(PS[0:C, 6 + g, 0:HS], aw[:, 3, :], oT[:, g * HS:(g + 1) * HS], start=True, stop=True)
                        last.then_inc(at_pe, 1)
                    pe.reg_add(runs_a, runs_a, 1)
                with pe.If((c_ & 1) > 0):
                    na = pe.snap(runs_a, min_val=0, max_val=NB_)
                    nf = pe.snap(runs_f, min_val=0, max_val=NB_)
                    wait_for(pe, fw_ld, nf * FW_DMAS + FW_DMAS)
                    wait_for(pe, h_upd, na * T + nf * T + T)
                    for t in range(T):
                        for j in range(TB):
                            k = t * TB + j
                            if k >= 2:
                                wait_for(pe, (f1_act, f1_dve)[k % 2], nf * 4 + k // 2)
                            for g in range(2):
                                last = nc.tensor.matmul(PS[:, 2 * (k % 2) + g, 0:HS], fw1[:, j, :], cut(h, t)[:, g, :], start=True, stop=True)
                            last.then_inc(f1_done, 1)
                            if k >= 1:
                                second(k - 1, nf)
                    second(B - 1, nf)
                    pe.reg_add(runs_f, runs_f, 1)
                pe.reg_add(steps, steps, 1)
                st = pe.snap(steps, min_val=1, max_val=NB_)
                na = pe.snap(runs_a, min_val=0, max_val=NB_)
                nf = pe.snap(runs_f, min_val=0, max_val=NB_)
                wait_for(pe, h_upd, na * T + nf * T + T)
                nc.tensor.transpose(PS[0:1, 7, 0:C], h[0:C, 0, 0:1], idn[0:C, 0:C]).then_inc(row_done, 1)
                wait_for(pe, ctrl_rdy, st + 1)
                pe.reg_load(cr, ctrl[0:1, 0:1])

        @block.scalar
        def _(act):
            act.dma_start(w_nat[:, :], L0_conv_W_trans).then_inc(w_ld, 16)
            act.dma_start(gw_nat[:, :], L0_ffn_gate_w).then_inc(w_ld, 16)
            act.dma_start(wc_nat[:, :], L1_conv_Wconv).then_inc(w_ld, 16)
            act.dma_start(gb[:, :], L0_ffn_gate_b.rearrange("(o e) -> o e", o=1).to_broadcast([B, E_]).unsqueeze(2)).then_inc(w_ld, 16)
            act.dma_start(mask32[0:1, 0, :], L1_ffn_attn_mask).then_inc(mask_ld, 16)
            act.dma_start(mask32[0:1, 1, :], L1_ffn_ffn_mask).then_inc(mask_ld, 16)

            def layernorm(i, eps):
                for t in range(T):
                    act.wait_ge(xc_rdy, T * i + t + 1)
                    nc.scalar.activation(cut(sq, t), half(t), ACT.Square).then_inc(sq_rdy, 1)
                for t in range(T):
                    nc.scalar.copy(cut(xc, t), half(t)).then_inc(xc_copied, 1)
                act.wait_ge(var_rdy, i + 1)
                nc.scalar.activation(std[:, :], PS[:, 4, 0:QS], ACT.Sqrt, bias=eps[:, :]).then_inc(std_rdy, 1)

            def load_table(f):
                nc.scalar.activation(tab[:, :], tab[:, :], f)

            act.wait_ge(eps_set, 1)
            load_table(ACT.Sqrt)
            layernorm(0, eps6)
            load_table(ACT.Exp)
            act.wait_ge(border0, 1)
            for i, (w, t, bank) in enumerate(QKV):
                act.wait_ge(qkv_done, i + 1)
                src = PS[:, bank:bank + 2, 0:HS]
                if w == 0:
                    nc.scalar.copy(cut(q_sb, t), src).then_inc(qkv_rdy, 1)
                else:
                    nc.scalar.copy(inner((kpad, vpad)[w - 1], t), rows24(src, t)).then_inc(qkv_rdy, 1)
            for m in range(NBR // TRI):
                act.wait_ge(sdiff_rdy, m + 1)
                nc.scalar.activation(att[:, m * TRI:(m + 1) * TRI, :], att[:, m * TRI:(m + 1) * TRI, :], ACT.Exp,
                                     scale=HD ** -0.5).then_inc(sexp_rdy, 1)
            load_table(ACT.Sqrt)

            layernorm(1, eps5)
            load_table(ACT.Exp)
            act.wait_ge(logit_done, 1)
            act.wait_ge(w_ld, 64)
            nc.scalar.activation(logit[:, :].rearrange("p (g s) -> p g s", g=2), PS[:, 4:6, 0:HS], ACT.Identity,
                                 bias=gb[:, :]).then_inc(logit_rdy, 1)
            act.wait_ge(ntop_rdy, 1)
            nc.scalar.activation(prob[:, :], logit[:, :], ACT.Exp, bias=ntop[:, :], accum_out=psum_[:, :]).then_inc(prob_rdy, 1)
            for i in range(NCH // 2):
                act.wait_ge(yT_done, i + 1)
                nc.scalar.copy(yT[:, 2 * i:2 * i + 2, :, :].rearrange("k c t p -> k (c t p)"), PS[0:SC_, i, :]).then_inc(yT_rdy, 1)
            load_table(ACT.Gelu)
            act.wait_ge(pool_done, 1)
            act.wait_ge(border0, 1)
            for j in (2, 3):
                for e in range(TB):
                    last = nc.scalar.copy(pool_dst(j, e), pool_src(j, e))
            last.then_inc(pool_act, 1)
            act.wait_ge(hid_done, 1)
            nc.scalar.activation(hid[:, :], PS[:, 0, 0:H1], ACT.Gelu).then_inc(hid_rdy, 1)
            load_table(ACT.Sqrt)

            layernorm(2, eps6)
            for i in range(NU):
                act.wait_ge(u_done, i + 1)
                nc.scalar.copy(uT[:, i * UCH:(i + 1) * UCH], PS[0:V2 + 1, (5 + i) % 8, 0:UCH]).then_inc(u_rdy, 1)

            def cval_quad(k):
                g0, n = QUADS[k]
                act.wait_ge(gram_done, k + 1)
                full = n if g0 + n < NGRP else n - 1
                last = nc.scalar.copy(cval[:, g0:g0 + full, :],
                                      PS[0:GW, CVAL_BANK[k], 0:full * V2].rearrange("p (g c) -> p g c", c=V2))
                if full < n:
                    last = nc.scalar.copy(cval[0:last_w, NGRP - 1, :], PS[0:last_w, CVAL_BANK[k], full * V2:n * V2])
                last.then_inc(cval_rdy, 1)

            def yv_copy(k):
                g0, n = QUADS[k]
                act.wait_ge(yv_done, k + 1)
                w = (n - 1) * GW + gw_of(g0 + n - 1)
                nc.scalar.copy(yvT[:, g0 * GW:g0 * GW + w], PS[0:V2, YV_BANK[k], 0:w]).then_inc(yv_rdy, 1)

            for k in range(4):
                cval_quad(k)
            yv_copy(0)
            cval_quad(4)
            for k in range(1, 5):
                yv_copy(k)

            layernorm(3, eps5)
            runs_a, runs_f, steps, cr = (act.alloc_register(n) for n in ("act_a", "act_f", "act_steps", "act_code"))
            for r in (runs_a, runs_f, steps):
                act.reg_mov(r, 0)
            act.wait_ge(ctrl_rdy, 1)
            act.reg_load(cr, ctrl[0:1, 0:1])
            with act.While(lambda: act.snap(cr) < NONE):
                c_ = act.snap(cr, min_val=0, max_val=4 * NB_ - 1)
                with act.If((c_ & 2) > 0):
                    na = act.snap(runs_a, min_val=0, max_val=NB_)
                    with act.Fori(0, B) as b:
                        with act.Fori(0, NCH) as i:
                            wait_for(act, at_dve, na * ADVE_R + 1 + b * ADVE_B + 2 + i * ADVE_I + 3)
                            nc.scalar.activation(prow[:, :].rearrange("p (g s) -> p g s", g=2), PS[0:SC_, 0:2, 0:HS], ACT.Exp,
                                                 scale=C ** -0.5, bias=nmax[:, 1:2], accum_out=rsum[:, :]).then_inc(at_act, 1)
                    act.reg_add(runs_a, runs_a, 1)
                with act.If((c_ & 1) > 0):
                    nf = act.snap(runs_f, min_val=0, max_val=NB_)
                    wait_for(act, fw_ld, nf * FW_DMAS + FW_DMAS)
                    for k in range(0, B, 2):
                        wait_for(act, f1_done, nf * B + k + 1)
                        nc.scalar.activation(relu_h[:, k, :].rearrange("p (g s) -> p g s", g=2), PS[:, 0:2, 0:HS], ACT.Relu,
                                             bias=fb1[:, :]).then_inc(f1_act, 1)
                    act.reg_add(runs_f, runs_f, 1)
                act.reg_add(steps, steps, 1)
                wait_for(act, ctrl_rdy, act.snap(steps, min_val=1, max_val=NB_) + 1)
                act.reg_load(cr, ctrl[0:1, 0:1])

        @block.vector
        def _(dve):
            dve.wait_ge(c1_in, 16)
            nc.vector.memset(spread[:, :, :, :], 0.0).then_inc(spread_zero, 1)
            dve.wait_ge(spread_zero, 1)
            for q in range(4):
                rows = slice(32 * q, 32 * q + 32)
                last = nc.vector.tensor_copy(spread[rows, :, q, :], con("heads", 32, 32 * q).rearrange("p (t m) -> p t m", t=T))
            last.then_inc(spread_rdy, 1)
            dve.wait_ge(bd_zero, 1)
            dve.wait_ge(wT_done, 1)
            for j in range(TB):
                rows = slice(j * C, (j + 1) * C)
                nc.vector.tensor_copy(qkv_bd[rows, :, j * C:(j + 1) * C], PS[0:C, 7, 0:96].rearrange("p (s o) -> p s o", s=3))
                nc.vector.tensor_copy(gate_bd[rows, j * E_:(j + 1) * E_], PS[0:C, 7, 96:96 + E_])
                last = nc.vector.tensor_copy(conv_bd[rows, j * C:(j + 1) * C], PS[0:C, 7, 112:112 + C])
            last.then_inc(wT_copied, 1)

            def layernorm(i, dst):
                dve.wait_ge(std_rdy, i + 1)
                nc.vector.reciprocal(rstd[:, :], std[:, :]).then_inc(rstd_rdy, 1)
                dve.wait_ge(xc_copied, T * (i + 1))
                for t in range(T):
                    dve.wait_ge(rwide_rdy, T * i + t + 1)
                    nc.vector.tensor_tensor(cut(dst, t), half(t, 4), cut(xc, t), ALU.mult).then_inc(y_sem[i], 1)

            layernorm(0, y)

            for t in range(T):
                for n in range(NBR):
                    dy, dx = divmod(n, 3)
                    if n == 0:
                        dve.wait_ge(qkv_rdy, 2 * t + 2)
                    nc.vector.tensor_tensor(prods[:, t, n, :].rearrange("p (r c) -> p r c", c=WW),
                                            q_sb[:, t, :].rearrange("p (r c) -> p r c", c=WW),
                                            kpad[:, t, dy:dy + HH, dx:dx + WW], ALU.mult).then_inc(prod_rdy, 1)
            dve.wait_ge(score_rdy, 2)
            nc.vector.tensor_reduce(smax2[:, 0, :], PS[:, 4:6, 0:TRI * QS].rearrange("p b (m s) -> p s b m", s=QS), AX.XY, ALU.max)
            dve.wait_ge(score_rdy, 3)
            nc.vector.tensor_reduce(smax2[:, 1, :], PS[:, 6, 0:TRI * QS].rearrange("p (m s) -> p s m", s=QS), AX.X,
                                    ALU.max).then_inc(smax_rdy, 1)
            dve.wait_ge(smax_rdy, 1)
            nc.vector.tensor_tensor(smax[:, :], smax2[:, 0, :], smax2[:, 1, :], ALU.max).then_inc(smax_rdy, 1)
            dve.wait_ge(smax_rdy, 2)
            part = [P, TRI, QS]
            for m in range(NBR // TRI):
                nc.vector.tensor_tensor(att[:, m * TRI:(m + 1) * TRI, :], PS[:, 4 + m, 0:TRI * QS].rearrange("p (m s) -> p m s", s=QS),
                                        smax[:, :].unsqueeze(1).to_broadcast(part), ALU.subtract).then_inc(sdiff_rdy, 1)
            dve.wait_ge(sexp_rdy, 3)
            nc.vector.tensor_reduce(ssum[:, :], att[:, :, :].rearrange("p n s -> p s n"), AX.X, ALU.add).then_inc(ssum_rdy, 1)
            dve.wait_ge(ssum_rdy, 1)
            nc.vector.reciprocal(srec[:, :], ssum[:, :]).then_inc(ssum_rdy, 1)
            dve.wait_ge(ssum_rdy, 2)
            for m in range(NBR // TRI):
                nc.vector.tensor_tensor(att[:, m * TRI:(m + 1) * TRI, :], att[:, m * TRI:(m + 1) * TRI, :],
                                        srec[:, :].unsqueeze(1).to_broadcast(part), ALU.mult).then_inc(att_rdy, 1)
            dve.wait_ge(mab_done, 1)
            nc.vector.tensor_copy(mab[:, :], PS[0:V2 + 1, 7, 0:V2 + 1])
            nc.vector.tensor_copy(wcT[:, :].rearrange("k (r c) -> k r c", r=RV),
                                  PS[0:V2 + 1, 7, 128:128 + R2].rearrange("k (r c) -> k r c", r=R)[:, 0:RV, 0:RV]).then_inc(mab_copied, 1)
            for u in range(WIDE):
                t, m3 = divmod(u, NBR // TRI)
                dve.wait_ge(wide_rdy, u + 1)
                for m in range(TRI):
                    dy, dx = divmod(m3 * TRI + m, 3)
                    last = nc.vector.tensor_tensor(
                        prods[:, t, m3 * TRI + m, :].rearrange("p (q r c) -> p q r c", q=4, c=WW),
                        PS[:, 4 * (u % 2):4 * (u % 2) + 4, m * QS:(m + 1) * QS].rearrange("p q (r c) -> p q r c", c=WW),
                        vpad[:, t, dy:dy + HH, dx:dx + WW].rearrange("p (q r) c -> p q r c", q=4), ALU.mult)
                last.then_inc(wide_used, 1)
                dve.wait_ge(wide_used, u + 1)
                a, b, c = (prods[:, t, m3 * TRI + m, :] for m in range(TRI))
                nc.vector.tensor_tensor(a, a, b, ALU.add).then_inc(pair_rdy, 1)
            dve.wait_ge(pair_rdy, WIDE)
            nc.vector.tensor_tensor(a, a, c, ALU.add).then_inc(last_trio, 1)
            dve.wait_ge(last_trio, 1)
            dve.wait_ge(acc_rdy, WIDE - 1)
            nc.vector.tensor_tensor(xs[1][:, T - 1, :], x_in[:, T - 1, :], a, ALU.add).then_inc(x1_rdy, 1)

            layernorm(1, y)
            dve.wait_ge(logit_rdy, 1)
            nc.vector.max(top8[:, :], logit[:, :]).then_inc(top_rdy, 1)
            dve.wait_ge(top_rdy, 1)
            nc.vector.tensor_scalar(ntop[:, :], top8[:, 0:1], -1.0, None, ALU.mult).then_inc(ntop_rdy, 1)
            nc.vector.match_replace(rest[:, :], top8[:, :], logit[:, :], -3e38).then_inc(rest_rdy, 1)
            dve.wait_ge(rest_rdy, 1)
            nc.vector.tensor_tensor(ismine[:, :], logit[:, :], rest[:, :], ALU.not_equal).then_inc(mine_rdy, 1)
            dve.wait_ge(prob_rdy, 1)
            nc.vector.reciprocal(prec[:, :], psum_[:, :]).then_inc(prec_rdy, 1)
            dve.wait_ge(prec_rdy, 1)
            dve.wait_ge(mine_rdy, 1)
            nc.vector.scalar_tensor_tensor(pick[:, :], prob[:, :], prec[:, :], ismine[:, :], ALU.mult, ALU.mult).then_inc(pick_rdy, 1)
            for i, n in enumerate((4, NCH - 4)):
                dve.wait_ge(pickT_done, i + 1)
                nc.vector.tensor_copy(pickT[:, 4 * i:4 * i + n, :].rearrange("k c p -> k (c p)"), PS[0:SC_, 6 + i, 0:n * P]).then_inc(pickT_rdy, 1)
            dve.wait_ge(border0, 1)
            dve.wait_ge(pool_done, 1)
            for j in (0, 1):
                for e in range(TB):
                    last = nc.vector.tensor_copy(pool_dst(j, e), pool_src(j, e))
            last.then_inc(pool_dve, 1)
            dve.wait_ge(hidT_done, 1)
            nc.vector.tensor_copy(hidT[:, :], PS[:, 1, 0:P]).then_inc(hidT_rdy, 1)
            dve.wait_ge(eo_done, 1)
            nc.vector.tensor_copy(eoutT[:, :], PS[0:C, 2, 0:P]).then_inc(eo_rdy, 1)
            dve.wait_ge(eoT_done, 1)
            nc.vector.tensor_tensor(eout_bd[:, :, :], PS[:, 3, 256:256 + C].unsqueeze(1).to_broadcast([P, TB, C]),
                                    con("own").unsqueeze(2).to_broadcast([P, TB, C]), ALU.mult).then_inc(eobd_rdy, 1)
            for t in range(T):
                dve.wait_ge(scat_done, t + 1)
                for i in range(NP):
                    last = nc.vector.tensor_tensor(xs[2][:, t, i * BAND:(i + 1) * BAND].rearrange("p (j r c) -> p j r c", j=NP, r=RV),
                                                   band(4 + 2 * t, i), patches(xs[1][:, t, :], i), ALU.add)
                last.then_inc(x2_rdy, 1)

            layernorm(2, y)
            xT4 = xT[0:V2, :].rearrange("k (t b p) -> k p t b", t=T, p=NPT)
            dve.wait_ge(wconv_ld, 16 * 10)
            dve.wait_ge(xT_ones, 1)
            for i in range(5):
                dve.wait_ge(pT_done, i + 1)
                n = min(2, NPT - 2 * i)
                nc.vector.tensor_tensor(xT4[:, 2 * i:2 * i + n, :, :],
                                        PS[0:V2, i, 0:n * T * P].rearrange("k (p t b) -> k p t b", p=n, t=T),
                                        bc_rows[:, :].unsqueeze(1).unsqueeze(1).to_broadcast([V2, n, T, P]), ALU.add).then_inc(xT_rdy, 1)
            for k, (g0, n) in enumerate(QUADS):
                dve.wait_ge(gram_done, k + 1)
                full = n if g0 + n < NGRP else n - 1
                last = nc.vector.tensor_tensor(gram[:, g0:g0 + full, :],
                                               PS[0:GW, GRAM_BANK[k], 0:full * GW].rearrange("p (g c) -> p g c", c=GW),
                                               con("blk", GW).unsqueeze(1).to_broadcast([GW, full, GW]), ALU.mult)
                if full < n:
                    last = nc.vector.tensor_tensor(gram[0:last_w, NGRP - 1, 0:last_w],
                                                   PS[0:last_w, GRAM_BANK[k], full * GW:full * GW + last_w],
                                                   con("blk", last_w)[:, 0:last_w], ALU.mult)
                last.then_inc(gram_rdy, 1)
            for t in range(T):
                dve.wait_ge(back_done, t + 1)
                for b, n in ((0, 2 * BAND), (1, BAND)):
                    px = slice(2 * BAND * b, 2 * BAND * b + n)
                    last = nc.vector.tensor_tensor(xs[3][:, t, px], PS[:, BACK_BANK[t] + b, 0:n], xs[2][:, t, px], ALU.add)
                last.then_inc(x3_rdy, 1)

            layernorm(3, h)
            dve.wait_ge(code_st, 8)
            nc.vector.memset(nextf[:, :], -1.0).then_inc(ctl_step, 1)
            runs_a, runs_f, steps, cr = (dve.alloc_register(n) for n in ("dve_a", "dve_f", "dve_steps", "dve_code"))
            for r in (runs_a, runs_f, steps):
                dve.reg_mov(r, 0)

            CTL = 9

            def choose(n):
                base = n * CTL + 1
                wait_for(dve, row_done, n + 1)
                nc.vector.tensor_copy(row[:, :], PS[0:1, 7, 0:C]).then_inc(row_rdy, 1)
                wait_for(dve, row_rdy, n + 1)
                nc.vector.max(rmax[:, :], row[:, 0:NOPS]).then_inc(ctl_step, 1)
                wait_for(dve, ctl_step, base + 1)
                nc.vector.max_index(ridx[:, :], rmax[:, :], row[:, 0:NOPS]).then_inc(ctl_step, 1)
                wait_for(dve, ctl_step, base + 2)
                nc.vector.tensor_copy(opf[:, :], ridx[:, 0:1])
                nc.vector.tensor_copy(ctrl[:, 1:2], ridx[:, 0:1]).then_inc(ctl_step, 1)
                wait_for(dve, ctl_step, base + 3)
                nc.vector.tensor_scalar(hot[:, :], con("iop", 1), opf[:, :], None, ALU.is_equal).then_inc(ctl_step, 1)
                nc.vector.tensor_scalar(late[:, :], con("istep", 1), nextf[:, :], float(NONE), ALU.is_le, ALU.mult).then_inc(ctl_step, 1)
                wait_for(dve, ctl_step, base + 5)
                nc.vector.tensor_tensor(csel[:, :, :], code[:, :, :], hot[:, :].unsqueeze(1).to_broadcast([1, NB_, NOPS]),
                                        ALU.mult).then_inc(ctl_step, 1)
                wait_for(dve, ctl_step, base + 6)
                nc.vector.tensor_reduce(cand[:, :], csel[:, :, :], AX.X, ALU.add).then_inc(ctl_step, 1)
                wait_for(dve, ctl_step, base + 7)
                nc.vector.tensor_tensor(cand2[:, :], cand[:, :], late[:, :], ALU.add).then_inc(ctl_step, 1)
                wait_for(dve, ctl_step, base + 8)
                nc.vector.tensor_reduce(nextf[:, :], cand2[:, :], AX.X, ALU.min).then_inc(ctl_step, 1)
                wait_for(dve, ctl_step, base + 9)
                nc.vector.tensor_copy(ctrl[:, 0:1], nextf[:, :]).then_inc(ctrl_rdy, 1)
                wait_for(dve, ctrl_rdy, n + 1)
                dve.reg_load(cr, ctrl[0:1, 0:1])

            choose(0)
            with dve.While(lambda: dve.snap(cr) < NONE):
                c_ = dve.snap(cr, min_val=0, max_val=4 * NB_ - 1)
                with dve.If((c_ & 2) > 0):
                    na = dve.snap(runs_a, min_val=0, max_val=NB_)
                    for j in range(TB):
                        last = nc.vector.tensor_copy(h0[:, j::TB, :], h[j * C:(j + 1) * C, :, :])
                    last.then_inc(at_dve, 1)
                    with dve.Fori(0, B) as b:
                        d0 = na * ADVE_R + 1 + b * ADVE_B
                        p0 = na * (B * APE_B) + b * APE_B
                        wait_for(dve, at_dve, d0)
                        nc.vector.tensor_copy(hb[:, :], h0[:, bass.ds(b, 1), :].rearrange("c b s -> c (b s)")).then_inc(at_dve, 1)
                        wait_for(dve, at_pe, p0 + 1)
                        nc.vector.tensor_copy(qT_[:, :].rearrange("p (g s) -> p g s", g=2), PS[0:C, 0:2, 0:HS])
                        nc.vector.tensor_copy(kT_[:, :].rearrange("p (g s) -> p g s", g=2), PS[0:C, 2:4, 0:HS])
                        nc.vector.tensor_copy(vk[:, :, :].rearrange("k c d -> k (c d)"), PS[0:SC_, 4, 0:NCH * C]).then_inc(at_dve, 1)
                        with dve.Fori(0, NCH) as i:
                            di = d0 + 2 + i * ADVE_I
                            pi = p0 + 1 + i * APE_I
                            wait_for(dve, at_dve, di)
                            nc.vector.tensor_copy(qi[:, :], qT_[:, bass.ds(i * SC_, SC_)]).then_inc(at_dve, 1)
                            wait_for(dve, at_pe, pi + 1)
                            nc.vector.tensor_reduce(nmax[:, 0:1], PS[0:SC_, 0:2, 0:HS], AX.XY, ALU.max, negate=True).then_inc(at_dve, 1)
                            wait_for(dve, at_dve, di + 2)
                            nc.vector.tensor_scalar(nmax[:, 1:2], nmax[:, 0:1], C ** -0.5, None, ALU.mult).then_inc(at_dve, 1)
                            wait_for(dve, at_act, (na * B + b) * AACT_B + i + 1)
                            nc.vector.reciprocal(rrec[:, :], rsum[:, :]).then_inc(at_dve, 1)
                            wait_for(dve, at_dve, di + 4)
                            nc.vector.tensor_scalar(arow[:, :], prow[:, :], rrec[:, :], None, ALU.mult).then_inc(at_dve, 1)
                            wait_for(dve, at_pe, pi + 2)
                            nc.vector.tensor_copy(aT[:, :, :].rearrange("k (g c) q -> k g (c q)", g=2), PS[0:SC_, 2:4, 0:HS]).then_inc(at_dve, 1)
                            wait_for(dve, at_pe, pi + 3)
                            nc.vector.tensor_copy(oT[:, bass.ds(i * SC_, SC_)], PS[0:C, 5, 0:SC_]).then_inc(at_dve, 1)
                        wait_for(dve, at_pe, p0 + APE_B)
                        nc.vector.tensor_copy(h0[:, bass.ds(b, 1), :].rearrange("c b (g s) -> c (b g) s", g=2), PS[0:C, 6:8, 0:HS]).then_inc(at_dve, 1)
                    wait_for(dve, at_dve, na * ADVE_R + ADVE_R)
                    for j in range(TB):
                        last = nc.vector.tensor_copy(h[j * C:(j + 1) * C, :, :], h0[:, j::TB, :])
                    last.then_inc(h_upd, T)
                    dve.reg_add(runs_a, runs_a, 1)
                with dve.If((c_ & 1) > 0):
                    nf = dve.snap(runs_f, min_val=0, max_val=NB_)
                    wait_for(dve, fw_ld, nf * FW_DMAS + FW_DMAS)
                    for k in range(1, B, 2):
                        wait_for(dve, f1_done, nf * B + k + 1)
                        nc.vector.tensor_scalar(relu_h[:, k, :].rearrange("p (g s) -> p g s", g=2), PS[:, 2:4, 0:HS],
                                                fb1[:, :], 0.0, ALU.add, ALU.max).then_inc(f1_dve, 1)
                    for t in range(T):
                        wait_for(dve, z_done, nf * T + t + 1)
                        nc.vector.tensor_scalar(cut(h, t), half(t, 4), fb2[:, :], None, ALU.add).then_inc(h_upd, 1)
                    dve.reg_add(runs_f, runs_f, 1)
                dve.reg_add(steps, steps, 1)
                choose(dve.snap(steps, min_val=1, max_val=NB_))
            na = dve.snap(runs_a, min_val=0, max_val=NB_)
            nf = dve.snap(runs_f, min_val=0, max_val=NB_)
            wait_for(dve, h_upd, na * T + nf * T + T)
            for t in range(T):
                for i in range(NP):
                    px = slice(i * BAND, (i + 1) * BAND)
                    last = nc.vector.tensor_tensor(patches(y[:, t, :], i), xs[3][:, t, px].rearrange("p (j r c) -> p j r c", j=NP, r=RV),
                                                   h[:, t, px].rearrange("p (j r c) -> p j r c", j=NP, r=RV), ALU.add)
                last.then_inc(fin_rdy, 1)


def kernel(**inputs):
    from concourse import bacc
    from concourse.bass_utils import run_bass_kernel_spmd

    nc = bacc.Bacc("TRN2", target_bir_lowering=False, num_devices=1)
    arrays, args = {}, {}
    for name, a in inputs.items():
        a = np.ascontiguousarray(a)
        if a.dtype == np.bool_:
            padded = np.zeros((1, 4 * MWORDS), np.bool_)
            padded[0, :a.size] = a.ravel()
            a = padded.view(np.int32)
        arrays["in_" + name] = a
        args[name] = nc.dram_tensor("in_" + name, a.shape, mybir.dt.from_np(a.dtype), kind="ExternalInput").ap()
    arrays["consts"] = constant_table()
    args["consts"] = nc.dram_tensor("consts", (P, NCST), mybir.dt.float32, kind="ExternalInput").ap()
    args["out"] = nc.dram_tensor("result", (B, C, HH, WW), mybir.dt.float32, kind="ExternalOutput").ap()
    metaformer(nc, **args)
    return run_bass_kernel_spmd(nc, [arrays], core_ids=[0]).results[0]["result"]
```

```python
from contextlib import ExitStack

import concourse.bass as bass
import numpy as np
from concourse import mybir

B, C, HH, WW = 8, 32, 24, 24
S = HH * WW
P = 128
TB = P // C
T = B // TB
HS = S // 2
HEADS, HD, NBR = 4, C // 4, 9
PW = WW + 2
QS = S // 4
TRI = 3
E_, H1, K_ = 16, 128, 8
SC_, NCH = 96, S // 96
R, NP = 9, 3
R2, NPT = R * R, NP * NP
RV = HH // NP
V2 = RV * RV
BAND = NP * V2
GRP = P // NPT
NGRP = -(-B * C // GRP)
GW = GRP * NPT
NB_, NOPS = 33, 19
MWORDS = -(-NB_ * NOPS // 4)
NONE = 4 * 1000
INV = 1.0 / R

_COLS = [("idn", P), ("cen", P), ("mean", T * 32), ("heads", T * P), ("hsum", T * 32), ("own", TB), ("blk", GW),
         ("ebias", P), ("obias", P), ("iop", NOPS), ("istep", NB_)]
OFF, _o = {}, 0
for _n, _w in _COLS:
    OFF[_n] = (_o, _o + _w)
    _o += _w
NCST = _o


def constant_table():
    t = np.zeros((P, NCST), np.float32)
    p = np.arange(P)

    def put(name, a):
        t[:a.shape[0], OFF[name][0]:OFF[name][0] + a.shape[1]] = a

    same = (p[:, None] // C == p[None, :] // C).astype(np.float32)
    put("idn", np.eye(P, dtype=np.float32))
    put("cen", np.eye(P, dtype=np.float32) - same / C)
    bg = p // HD
    for t_ in range(T):
        a = np.zeros((P, 32), np.float32)
        for g in range(HEADS):
            a[p, (t_ * TB + p // C) * HEADS + g] = np.float32(1 / C)
        t[:, OFF["mean"][0] + 32 * t_:OFF["mean"][0] + 32 * (t_ + 1)] = a
        a = np.zeros((P, 32), np.float32)
        a[p, t_ * TB * HEADS + bg] = 1
        t[:, OFF["hsum"][0] + 32 * t_:OFF["hsum"][0] + 32 * (t_ + 1)] = a
        b = np.zeros((P, P), np.float32)
        for q in range(4):
            b[32 * q + t_ * TB * HEADS + bg, p] = 1
        t[:, OFF["heads"][0] + P * t_:OFF["heads"][0] + P * (t_ + 1)] = b
    put("own", ((p[:, None] // E_) % TB == np.arange(TB)).astype(np.float32))
    g = np.arange(GW)
    put("blk", (g[:, None] // NPT == g[None, :] // NPT).astype(np.float32) * np.float32(INV))
    e = np.arange(E_)
    put("ebias", (e[:, None] == p[None, :] // B).astype(np.float32))
    put("obias", (e[:, None] == p[None, :] % E_).astype(np.float32))
    put("iop", np.arange(NOPS, dtype=np.float32)[None, :])
    put("istep", 4 * NOPS * np.arange(NB_, dtype=np.float32)[None, :])
    return t


def row_table():
    return 4 * np.arange(NB_ * NOPS, dtype=np.float32)[None, :]


def metaformer(nc, x, L0_conv_W_trans, L0_ffn_gate_w, L0_ffn_gate_b, L0_ffn_weight1, L0_ffn_weight2,
               L1_conv_Wconv, L1_conv_bconv, L1_conv_Wa, L1_conv_ba, L1_conv_Wb, L1_conv_bb, L1_conv_Wc,
               L1_conv_bc, L1_ffn_ffn_w1, L1_ffn_ffn_b1, L1_ffn_ffn_w2, L1_ffn_ffn_b2, L1_ffn_wq, L1_ffn_wk,
               L1_ffn_wv, L1_ffn_wo, L1_ffn_attn_mask, L1_ffn_ffn_mask, consts, row_codes, out, dbg=None):
    f32, i32, u32, u8 = mybir.dt.float32, mybir.dt.int32, mybir.dt.uint32, mybir.dt.uint8
    ALU, ACT, AX = mybir.AluOpType, mybir.ActivationFunctionType, mybir.AxisListType

    ctx = ExitStack()
    with ctx:
        def sb(name, shape, dt=f32):
            return ctx.enter_context(nc.sbuf_tensor(name, shape, dt))

        def sem(name):
            return ctx.enter_context(nc.semaphore(name))

        cst = sb("cst", [P, NCST])

        def con(name, rows=P, first=0):
            return cst[first:first + rows, OFF[name][0]:OFF[name][1]]

        idn = con("idn")
        prods = sb("prods", [P, T, NBR + 1, S])
        x_in = prods[:, :, NBR, :]
        xs = [None] + [sb(f"x{i}", [P, T, S]) for i in (1, 2, 3)]
        sq = sb("sq", [P, T, S])
        xc = sb("xc", [P, T, S])
        std = sb("std", [P, QS])
        rstd = sb("rstd", [P, QS])
        spread = sb("spread", [P, T, 4, P])
        y = sb("y", [P, T, S])
        q_sb = sb("q_sb", [P, T, S])
        kpad = sb("kpad", [P, T, HH + 2, PW])
        vpad = sb("vpad", [P, T, HH + 2, PW])
        w_nat = sb("w_nat", [96, C])
        gw_nat = sb("gw_nat", [E_, C])
        wc_nat = sb("wc_nat", [C, C])
        qkv_bd = sb("qkv_bd", [P, 3, P])
        gate_bd = sb("gate_bd", [P, TB * E_])
        conv_bd = sb("conv_bd", [P, P])
        att = sb("att", [P, NBR, QS])
        smax2 = sb("smax2", [P, 2, QS])
        smax = sb("smax", [P, QS])
        ssum = sb("ssum", [P, QS])
        srec = sb("srec", [P, QS])
        gb = sb("gb", [P, 1])
        logit = sb("logit", [P, S])
        rest = sb("rest", [P, S])
        ismine = sb("ismine", [P, S])
        prob = sb("prob", [P, S])
        pick = sb("pick", [P, S])
        top8 = sb("top8", [P, K_])
        ntop = sb("ntop", [P, 1])
        psum_ = sb("psum_", [P, 1])
        prec = sb("prec", [P, 1])
        yT = sb("yT", [SC_, NCH, T, P])
        pickT = sb("pickT", [SC_, NCH, P])
        pool_bd = sb("pool_bd", [P, TB, TB * B])
        ew1 = sb("ew1", [P, TB, H1])
        eb1 = sb("eb1", [E_, H1])
        ew2 = sb("ew2", [P, E_, C])
        eb2 = sb("eb2", [E_, C])
        hid = sb("hid", [P, H1])
        hidT = sb("hidT", [P, P])
        eoutT = sb("eoutT", [C, P])
        eout_bd = sb("eout_bd", [P, TB, C])
        wa = sb("wa", [R2, V2 + 1])
        wb = sb("wb", [R2, V2 + 1])
        wc = sb("wc", [R2, V2 + 1])
        wcT = sb("wcT", [P, V2])
        mab = sb("mab", [P, P])
        bc_rows = sb("bc_rows", [V2, P])
        xT = sb("xT", [P, B * C * NPT])
        uT = prods[:, 0, 0:4, :].rearrange("k n s -> k (n s)")
        gram = sb("gram", [GW, NGRP, GW])
        cval = sb("cval", [GW, NGRP, V2])
        yvT = prods[0:V2, 0, 4:8, :].rearrange("k n s -> k (n s)")
        h = sb("h", [P, T, S])
        fw1 = sb("fw1", [P, TB, H1])
        fw2 = sb("fw2", [H1, C])
        fb1 = sb("fb1", [H1, 1])
        fb2 = sb("fb2", [P, 1])
        relu_h = prods[:, 0, 0:B, :]
        tab = sb("tab", [1, 1])
        eps5 = sb("eps5", [P, 1])
        eps6 = sb("eps6", [P, 1])
        mask32 = sb("mask32", [1, 2, MWORDS], i32)
        mask8 = mask32[:, :, :].bitcast(u8)
        maskf = sb("maskf", [1, 2, NB_ * NOPS])
        both = sb("both", [1, NB_ * NOPS])
        anyf = sb("anyf", [1, NB_ * NOPS])
        rowc = sb("rowc", [1, NB_ * NOPS])
        code = sb("code", [1, NB_, NOPS])
        row = sb("row", [1, C])
        rmax = sb("rmax", [1, 8])
        ridx = sb("ridx", [1, 8], u32)
        opf = sb("opf", [1, 1])
        hot = sb("hot", [1, NOPS])
        csel = sb("csel", [1, NB_, NOPS])
        cand = sb("cand", [1, NB_])
        late = sb("late", [1, NB_])
        nextf = sb("nextf", [1, 1])
        ctrl = sb("ctrl", [1, 1], i32)
        h0 = prods[0:C, 1, 0:B, :]
        hb = xc[0:C, 0, 0:S]
        qT_ = xc[0:C, 1, 0:S]
        kT_ = prods[0:C, 0, 0, :]
        vk = q_sb[0:SC_, 0, 0:NCH * C].rearrange("k (c d) -> k c d", c=NCH)
        qi = sb("qi", [C, SC_])
        nmax = sb("nmax", [SC_, 2])
        prow = prods[0:SC_, 0, 1, :]
        arow = prods[0:SC_, 0, 2, :]
        rsum = sb("rsum", [SC_, 1])
        rrec = sb("rrec", [SC_, 1])
        aT = q_sb[0:SC_, 1, :].rearrange("k (c q) -> k c q", c=NCH)
        oT = prods[0:C, 0, 3, :]
        aw = sb("aw", [C, 4, C])

        PS = ctx.enter_context(nc.psum_tensor("PS", [P, 8, 512], f32))

        x_ld = [sem(f"x_ld{t}") for t in range(T)]
        c0_in, c1_in, c2_in, gb_ld, w_ld, wconv_ld, ew_ld, mask_ld, out_st = (
            sem(n) for n in ("c0_in", "c1_in", "c2_in", "gb_ld", "w_ld", "wconv_ld", "ew_ld", "mask_ld", "out_st"))
        border0, sq_set, eps_set, bd_zero, xT_ones, code_st = (
            sem(n) for n in ("border0", "sq_set", "eps_set", "bd_zero", "xT_ones", "code_st"))
        wT_done, wT_copied, mab_done, mab_copied, spread_zero, spread_rdy = (
            sem(n) for n in ("wT_done", "wT_copied", "mab_done", "mab_copied", "spread_zero", "spread_rdy"))
        xc_rdy, xc_copied, sq_rdy, var_rdy, std_rdy, rstd_rdy, rwide_rdy, y_rdy = (
            sem(n) for n in ("xc_rdy", "xc_copied", "sq_rdy", "var_rdy", "std_rdy", "rstd_rdy", "rwide_rdy", "y_rdy"))
        qkv_done, qkv_rdy, prod_rdy, gprod_rdy, score_rdy, smax_rdy, sdiff_rdy, sexp_rdy, ssum_rdy, att_rdy = (
            sem(n) for n in ("qkv_done", "qkv_rdy", "prod_rdy", "gprod_rdy", "score_rdy", "smax_rdy", "sdiff_rdy", "sexp_rdy",
                             "ssum_rdy", "att_rdy"))
        wide_rdy, wide_used, pair_rdy, trio_rdy, last_trio, acc_rdy, x1_rdy, x2_rdy, x3_rdy = (
            sem(n) for n in ("wide_rdy", "wide_used", "pair_rdy", "trio_rdy", "last_trio", "acc_rdy", "x1_rdy", "x2_rdy", "x3_rdy"))
        logit_done, logit_rdy, yT_done, yT_rdy, top_rdy, ntop_rdy, rest_rdy, mine_rdy, prob_rdy, prec_rdy = (
            sem(n) for n in ("logit_done", "logit_rdy", "yT_done", "yT_rdy", "top_rdy", "ntop_rdy", "rest_rdy",
                             "mine_rdy", "prob_rdy", "prec_rdy"))
        pick_rdy, pickT_done, pickT_rdy, pool_done, pool_dve, pool_act, hid_done, hid_rdy, hidT_done, hidT_rdy = (
            sem(n) for n in ("pick_rdy", "pickT_done", "pickT_rdy", "pool_done", "pool_dve", "pool_act", "hid_done",
                             "hid_rdy", "hidT_done", "hidT_rdy"))
        eo_done, eo_rdy, eoT_done, eobd_rdy, scat_done = (
            sem(n) for n in ("eo_done", "eo_rdy", "eoT_done", "eobd_rdy", "scat_done"))
        pT_done, xT_rdy, u_done, u_rdy, gram_done, gram_rdy, cval_rdy, yv_done, yv_rdy, back_done = (
            sem(n) for n in ("pT_done", "xT_rdy", "u_done", "u_rdy", "gram_done", "gram_rdy", "cval_rdy", "yv_done",
                             "yv_rdy", "back_done"))
        late_rdy, next_rdy, h_upd, row_done, row_rdy, ctl_step, ctrl_rdy, fw_ld, aw_ld = (
            sem(n) for n in ("late_rdy", "next_rdy", "h_upd", "row_done", "row_rdy", "ctl_step", "ctrl_rdy", "fw_ld", "aw_ld"))
        fw1_ld, fw_free, f1_done, relu_rdy, z_done, fin_rdy = (
            sem(n) for n in ("fw1_ld", "fw_free", "f1_done", "relu_rdy", "z_done", "fin_rdy"))
        waited = sem("waited")
        at_pe, at_dve, at_act = (sem(n) for n in ("at_pe", "at_dve", "at_act"))

        def half(t, first=0):
            return PS[:, first + 2 * t:first + 2 * t + 2, 0:HS]

        def cut(a, t):
            return a[:, t, 0:S].rearrange("p (g s) -> p g s", g=2)

        def patches(a, i):
            return a.rearrange("p (r i c j) -> p i j r c", r=RV, i=NP, c=RV)[:, i, :, :, :]

        def band(first, i):
            return PS[:, first + i // 2, (i % 2) * BAND:(i % 2 + 1) * BAND].rearrange("p (j r c) -> p j r c", j=NP, r=RV)

        def rows24(a, t):
            return a.rearrange("p g (r c) -> p g r c", c=WW)

        def inner(a, t):
            return a[:, t, 1:1 + HH, 1:1 + WW].rearrange("p (g r) c -> p g r c", g=2)

        QKV = [(0, 0, 0), (1, 0, 4), (0, 1, 2), (1, 1, 6), (2, 0, 0), (2, 1, 2)]
        NDVE = 6
        WIDE = T * NBR // TRI
        last_w = (B * C - (NGRP - 1) * GRP) * NPT
        QUADS = [(g, min(4, NGRP - g)) for g in range(0, NGRP, 4)]
        GRAM_BANK = [0, 1, 2, 3, 4]
        CVAL_BANK = [5, 6, 7, 0, 1]
        YV_BANK = [5, 6, 7, 2, 3]
        BACK_BANK = [0, 4]
        PAIRS = -(-NPT // 2)
        APE_I, ADVE_I, AACT_I = 3, 7, 1
        APE_B, ADVE_B, AACT_B = 2 + NCH * APE_I, 3 + NCH * ADVE_I, NCH * AACT_I
        FW_DMAS = 16 * 3
        ADVE_R = 1 + B * ADVE_B

        def pool_src(j, e):
            a = PS[j * C:(j + 1) * C, 3, 0:2 * TB * E_].rearrange("c (t b g e) -> c b e g t", t=T, b=TB, e=TB)
            return a[:, j, e, :, :]

        def pool_dst(j, e):
            a = pool_bd[e * C:(e + 1) * C, :, :].rearrange("c g (e t b) -> c e b g t", e=TB, t=T)
            return a[:, e, j, :, :]

        x_sem = (None, x1_rdy, x2_rdy, x3_rdy)
        y_sem = (y_rdy, y_rdy, y_rdy, h_upd)

        def patch_pair(a, i):
            n = min(2, NPT - 2 * i)
            return a.rearrange("k (b p) -> k p b", p=NPT)[:, 2 * i:2 * i + n, :]

        def gw_of(g):
            return GW if g < NGRP - 1 else last_w

        def wait_for(eng, signal, value):
            eng.wait_ge(signal, value)
            if not isinstance(value, int):
                eng.sem_inc(waited, 1)

        def band_add(vec, t, i):
            px = slice(i * BAND, (i + 1) * BAND)
            return vec.tensor_tensor(patches(y[:, t, :], i), xs[3][:, t, px].rearrange("p (j r c) -> p j r c", j=NP, r=RV),
                                     h[:, t, px].rearrange("p (j r c) -> p j r c", j=NP, r=RV), ALU.add)

        def final_add(vec, t):
            for i in range(NP):
                last = band_add(vec, t, i)
            last.then_inc(fin_rdy, 1)

        block = ctx.enter_context(nc.Block())

        @block.sync
        def _(sp):
            sp.dma_start(x_in[:, 0, :], x[0:TB].rearrange("b c h w -> (b c) (h w)")).then_inc(x_ld[0], 16)
            sp.dma_start(cst[:, 0:OFF["mean"][0]], consts[:, 0:OFF["mean"][0]]).then_inc(c0_in, 16)
            sp.dma_start(cst[:, OFF["mean"][0]:OFF["hsum"][0]], consts[:, OFF["mean"][0]:OFF["hsum"][0]]).then_inc(c1_in, 16)
            sp.dma_start(cst[:, OFF["hsum"][0]:], consts[:, OFF["hsum"][0]:]).then_inc(c2_in, 16)
            sp.dma_start(gb[:, :], L0_ffn_gate_b.rearrange("(o e) -> o e", o=1).to_broadcast([B, E_]).unsqueeze(2)).then_inc(gb_ld, 16)
            sp.dma_start(mask32[0:1, 0, :], L1_ffn_attn_mask).then_inc(mask_ld, 16)
            sp.dma_start(mask32[0:1, 1, :], L1_ffn_ffn_mask).then_inc(mask_ld, 16)
            sp.dma_start(rowc[:, :], row_codes).then_inc(mask_ld, 16)
            for i, (w, b) in enumerate(((L1_conv_Wa, L1_conv_ba), (L1_conv_Wb, L1_conv_bb), (L1_conv_Wc, L1_conv_bc))):
                dst = (wa, wb, wc)[i]
                sp.dma_start(dst[:, 0:V2].rearrange("o (r c) -> o r c", r=RV),
                             w.rearrange("o (r c) -> o r c", r=R)[:, 0:RV, 0:RV]).then_inc(wconv_ld, 16)
                sp.dma_start(dst[:, V2:V2 + 1], b.rearrange("(p o) -> p o", o=1)).then_inc(wconv_ld, 16)
            for j in range(TB):
                sp.dma_start(bc_rows[:, j * C:(j + 1) * C], L1_conv_bconv.partition_broadcast(V2)).then_inc(wconv_ld, 16)
            for e in range(TB):
                sp.dma_start(ew1[e * C:(e + 1) * C, :, :],
                             L0_ffn_weight1[e::TB, 0:C, :].rearrange("g c h -> c g h")).then_inc(ew_ld, 16)
            sp.dma_start(eb1[:, :], L0_ffn_weight1[:, C, :]).then_inc(ew_ld, 16)
            sp.dma_start(ew2[:, :, :], L0_ffn_weight2[:, 0:H1, :].rearrange("e h c -> h e c")).then_inc(ew_ld, 16)
            sp.dma_start(eb2[:, :], L0_ffn_weight2[:, H1, :]).then_inc(ew_ld, 16)

            steps, runs_a, runs_f, cr, row_no = (
                sp.alloc_register(n) for n in ("sp_steps", "sp_a", "sp_f", "sp_code", "sp_row"))
            for r in (steps, runs_a, runs_f):
                sp.reg_mov(r, 0)
            sp.wait_ge(border0, 1)
            sp.wait_ge(ctrl_rdy, 1)
            sp.reg_load(cr, ctrl[0:1, 0:1])
            with sp.While(lambda: sp.snap(cr) < NONE):
                c_ = sp.snap(cr, min_val=0, max_val=4 * NB_ * NOPS - 1)
                sp.reg_mov(row_no, c_ >> 2)
                rw = sp.snap(row_no, min_val=0, max_val=NB_ * NOPS - 1)

                def of_step(w):
                    if len(w.shape) == 4:
                        return w.rearrange("b o c d -> (b o) c d")[bass.ds(rw, 1), :, :].rearrange("o c d -> (o c) d")
                    return w.rearrange("b o c -> (b o) c")[bass.ds(rw, 1), :].rearrange("o c -> c o")

                with sp.If((c_ & 2) > 0):
                    for i, w in enumerate((L1_ffn_wq, L1_ffn_wk, L1_ffn_wv, L1_ffn_wo)):
                        sp.dma_start(aw[:, i, :], of_step(w)).then_inc(aw_ld, 16)
                    sp.reg_add(runs_a, runs_a, 1)
                with sp.If((c_ & 1) > 0):
                    wait_for(sp, fw_free, sp.snap(steps, min_val=0, max_val=NB_) + 1)
                    for j in range(TB):
                        sp.dma_start(fw1[j * C:(j + 1) * C, j, :], of_step(L1_ffn_ffn_w1)).then_inc(fw1_ld, 16)
                    sp.dma_start(fb1[:, :], of_step(L1_ffn_ffn_b1)).then_inc(fw_ld, 16)
                    sp.dma_start(fw2[:, :], of_step(L1_ffn_ffn_w2)).then_inc(fw_ld, 16)
                    sp.dma_start(fb2[:, :], of_step(L1_ffn_ffn_b2).unsqueeze(0).to_broadcast([TB, C, 1])).then_inc(fw_ld, 16)
                    sp.reg_add(runs_f, runs_f, 1)
                sp.reg_add(steps, steps, 1)
                wait_for(sp, ctrl_rdy, sp.snap(steps) + 1)
                sp.reg_load(cr, ctrl[0:1, 0:1])

            done = T * sp.snap(steps, min_val=0, max_val=NB_)
            for t in range(T):
                wait_for(sp, fin_rdy, done + t + 1)
                sp.dma_start(out[t * TB:(t + 1) * TB].rearrange("b c h w -> (b c) (h w)"), y[:, t, :]).then_inc(out_st, 16)
            sp.wait_ge(out_st, 16 * T)

        @block.gpsimd
        def _(pool):
            nc.gpsimd.memset(sq[:, 0, 0:HS], 0.0).then_inc(sq_set, 1)
            nc.gpsimd.memset(eps6[:, :], 1e-6)
            nc.gpsimd.memset(tab[:, :], 0.0)
            nc.gpsimd.memset(eps5[:, :], 1e-5).then_inc(eps_set, 1)
            nc.gpsimd.memset(qkv_bd[:, :, :], 0.0)
            nc.gpsimd.memset(gate_bd[:, :], 0.0)
            nc.gpsimd.memset(conv_bd[:, :], 0.0).then_inc(bd_zero, 1)
            nc.gpsimd.memset(kpad[:, :, :, :], 0.0)
            nc.gpsimd.memset(pool_bd[:, :, :], 0.0)
            nc.gpsimd.memset(fw1[:, :, :], 0.0)
            nc.gpsimd.memset(vpad[:, :, :, :], 0.0).then_inc(border0, 1)
            pool.wait_ge(border0, 1)
            nc.gpsimd.memset(mab[:, :], 0.0)
            nc.gpsimd.memset(wcT[:, :], 0.0).then_inc(xT_ones, 1)
            pool.wait_ge(xT_ones, 1)
            nc.gpsimd.memset(xT[V2:P, :], 0.0).then_inc(xT_ones, 1)
            pool.wait_ge(xT_ones, 2)
            nc.gpsimd.memset(xT[V2:V2 + 1, :], 1.0).then_inc(xT_ones, 1)
            pool.wait_ge(xT_ones, 3)
            for t in range(T):
                pool.wait_ge(qkv_rdy, 2 * t + 2)
                for n in range(NDVE, NBR):
                    dy, dx = divmod(n, 3)
                    nc.gpsimd.tensor_tensor(prods[:, t, n, :].rearrange("p (r c) -> p r c", c=WW),
                                            q_sb[:, t, :].rearrange("p (r c) -> p r c", c=WW),
                                            kpad[:, t, dy:dy + HH, dx:dx + WW], ALU.mult).then_inc(gprod_rdy, 1)
            for u in range(WIDE - 1):
                t, m3 = divmod(u, NBR // TRI)
                a, c = prods[:, t, m3 * TRI, :], prods[:, t, m3 * TRI + 2, :]
                pool.wait_ge(pair_rdy, u + 1)
                nc.gpsimd.tensor_tensor(a, a, c, ALU.add).then_inc(trio_rdy, 1)
                pool.wait_ge(trio_rdy, u + 1)
                if m3 == NBR // TRI - 1:
                    nc.gpsimd.tensor_tensor(xs[1][:, t, :], x_in[:, t, :], a, ALU.add).then_inc(x1_rdy, 1)
                    pool.sem_inc(acc_rdy, 1)
                else:
                    nc.gpsimd.tensor_tensor(x_in[:, t, :], x_in[:, t, :], a, ALU.add).then_inc(acc_rdy, 1)
                    pool.wait_ge(acc_rdy, u + 1)

            pool.wait_ge(mask_ld, 16 * 3)
            nc.gpsimd.tensor_copy(maskf[:, :, :], mask8[:, :, 0:NB_ * NOPS]).then_inc(code_st, 1)
            pool.wait_ge(code_st, 1)
            am, fm = maskf[:, 0, :], maskf[:, 1, :]
            nc.gpsimd.tensor_tensor(both[:, :], am, fm, ALU.mult)
            nc.gpsimd.tensor_tensor(anyf[:, :], am, fm, ALU.add).then_inc(code_st, 1)
            pool.wait_ge(code_st, 2)
            bits = code[:, :, :].rearrange("p b o -> p (b o)")
            nc.gpsimd.tensor_tensor(bits, anyf[:, :], am, ALU.add).then_inc(code_st, 1)
            pool.wait_ge(code_st, 3)
            nc.gpsimd.tensor_tensor(anyf[:, :], anyf[:, :], both[:, :], ALU.subtract).then_inc(code_st, 1)
            nc.gpsimd.tensor_tensor(bits, bits, rowc[:, :], ALU.add).then_inc(code_st, 1)
            pool.wait_ge(code_st, 5)
            nc.gpsimd.tensor_scalar(bits, bits, -float(NONE), None, ALU.add).then_inc(code_st, 1)
            pool.wait_ge(code_st, 6)
            nc.gpsimd.tensor_tensor(bits, bits, anyf[:, :], ALU.mult).then_inc(code_st, 1)
            pool.wait_ge(code_st, 7)
            nc.gpsimd.tensor_scalar(bits, bits, float(NONE), None, ALU.add).then_inc(code_st, 1)

            for t in range(T):
                pool.wait_ge(h_upd, t + 1)
                pool.wait_ge(x3_rdy, t + 1)
                final_add(nc.gpsimd, t)

        @block.tensor
        def _(pe):
            def keep_clock(n, bank):
                for i in range(n):
                    nc.tensor.matmul(PS[:, bank, 0:HS], sq[:, 0, 0:P], sq[:, 0, 0:HS], start=True, stop=True)

            def centre(i, src, t):
                pe.wait_ge(*((x_ld[t], 16) if i == 0 else (x_sem[i], t + 1)))
                for g in range(2):
                    last = nc.tensor.matmul(PS[:, 2 * t + g, 0:HS], con("cen"), cut(src, t)[:, g, :], start=True, stop=True)
                last.then_inc(xc_rdy, 1)

            def deviation(i):
                mean = con("mean").rearrange("p (t m) -> p t m", t=T)
                for t in range(T):
                    pe.wait_ge(sq_rdy, T * i + t + 1)
                    for q in range(4):
                        last = nc.tensor.matmul(PS[32 * q:32 * q + 32, 4, 0:QS], mean[:, t, :], sq[:, t, q * QS:(q + 1) * QS],
                                                start=(t == 0), stop=(t == T - 1), skip_group_check=True)
                last.then_inc(var_rdy, 1)
                keep_clock(2, 5)
                pe.wait_ge(rstd_rdy, i + 1)
                if i == 0:
                    pe.wait_ge(spread_rdy, 1)
                    pe.wait_ge(wT_copied, 1)
                for t in range(T):
                    for q in range(4):
                        last = nc.tensor.matmul(PS[:, 4 + 2 * t + q // 2, (q % 2) * QS:(q % 2 + 1) * QS], spread[:, t, q, :],
                                                rstd[:, :], start=True, stop=True)
                    last.then_inc(rwide_rdy, 1)

            def layernorm(i, src):
                for t in range(T):
                    centre(i, src, t)
                deviation(i)

            pe.wait_ge(sq_set, 1)
            keep_clock(3, 7)
            pe.wait_ge(c0_in, 16)
            centre(0, x_in, 0)
            centre(0, x_in, 1)
            pe.wait_ge(w_ld, 16 * 3)
            nc.tensor.transpose(PS[0:C, 7, 0:96], w_nat[:, :], idn[0:96, 0:96])
            nc.tensor.transpose(PS[0:C, 7, 96:96 + E_], gw_nat[:, :], idn[0:E_, 0:E_])
            nc.tensor.transpose(PS[0:C, 7, 112:112 + C], wc_nat[:, :], idn[0:C, 0:C]).then_inc(wT_done, 1)
            pe.wait_ge(c1_in, 16)
            deviation(0)

            def qkv_product(i):
                w, t, bank = QKV[i]
                pe.wait_ge(y_rdy, t + 1)
                for g in range(2):
                    last = nc.tensor.matmul(PS[:, bank + g, 0:HS], qkv_bd[:, w, :], cut(y, t)[:, g, :], start=True, stop=True)
                last.then_inc(qkv_done, 1)

            for i in range(4):
                qkv_product(i)

            pe.wait_ge(c2_in, 16)
            pe.wait_ge(qkv_rdy, 2)
            hsum = con("hsum").rearrange("p (t m) -> p t m", t=T)
            for t in range(T):
                for n in range(NBR):
                    if t == 0 and n == 2 * TRI:
                        pe.wait_ge(qkv_rdy, 4)
                    if n < NDVE:
                        pe.wait_ge(prod_rdy, NDVE * t + n + 1)
                    else:
                        pe.wait_ge(gprod_rdy, (NBR - NDVE) * t + n - NDVE + 1)
                    for q in range(4):
                        last = nc.tensor.matmul(PS[32 * q:32 * q + 32, 4 + n // TRI, (n % TRI) * QS:(n % TRI + 1) * QS],
                                                hsum[:, t, :], prods[:, t, n, q * QS:(q + 1) * QS],
                                                start=(t == 0 and n % TRI == 0), stop=(t == T - 1), skip_group_check=True)
                    if t == T - 1 and n % TRI == TRI - 1:
                        last.then_inc(score_rdy, 1)
            qkv_product(4)
            qkv_product(5)

            pe.wait_ge(wconv_ld, 16 * 10)
            nc.tensor.matmul(PS[0:V2 + 1, 7, 0:V2 + 1], wa[:, :], wb[:, :], start=True, stop=True)
            nc.tensor.transpose(PS[0:V2 + 1, 7, 128:128 + R2], wc[:, :], idn[0:R2, 0:R2]).then_inc(mab_done, 1)

            pe.wait_ge(mab_copied, 1)
            keep_clock(5, 7)
            pe.wait_ge(qkv_rdy, 6)
            for u in range(WIDE):
                t, m = divmod(u, NBR // TRI)
                if t == 0:
                    pe.wait_ge(att_rdy, m + 1)
                if u >= 2:
                    pe.wait_ge(wide_used, u - 1)
                for q in range(4):
                    last = nc.tensor.matmul(PS[:, 4 * (u % 2) + q, 0:TRI * QS], spread[:, t, q, :],
                                            att[:, m * TRI:(m + 1) * TRI, :], start=True, stop=True)
                last.then_inc(wide_rdy, 1)

            pe.wait_ge(wide_used, WIDE - 1)
            layernorm(1, xs[1])
            for t in range(T):
                pe.wait_ge(y_rdy, T + t + 1)
            for g in range(2):
                for t in range(T):
                    last = nc.tensor.matmul(PS[64 * t:64 * t + 64, 4 + g, 0:HS], gate_bd[:, :], cut(y, t)[:, g, :],
                                            start=True, stop=True)
            last.then_inc(logit_done, 1)
            for c in range(NCH):
                for t in range(T):
                    last = nc.tensor.transpose(PS[0:SC_, c // 2, ((c % 2) * T + t) * P:((c % 2) * T + t + 1) * P],
                                               y[:, t, c * SC_:(c + 1) * SC_], idn)
                if c % 2:
                    last.then_inc(yT_done, 1)
            keep_clock(3, 7)
            pe.wait_ge(pick_rdy, 1)
            for c in range(NCH):
                last = nc.tensor.transpose(PS[0:SC_, 6 + c // 4, (c % 4) * P:(c % 4 + 1) * P], pick[:, c * SC_:(c + 1) * SC_], idn)
                if c in (3, NCH - 1):
                    last.then_inc(pickT_done, 1)
            keep_clock(1, 3)
            pe.wait_ge(yT_rdy, 3)
            for t in range(T):
                for c in range(NCH):
                    pe.wait_ge(pickT_rdy, 1 + c // 4)
                    last = nc.tensor.matmul(PS[:, 3, 64 * t:64 * t + 64], yT[:, c, t, :], pickT[:, c, 64 * t:64 * t + 64],
                                            start=(c == 0), stop=(c == NCH - 1))
            last.then_inc(pool_done, 1)
            pe.wait_ge(ew_ld, 16 * 7)
            nc.tensor.matmul(PS[:, 0, 0:H1], con("ebias", E_), eb1[:, :], start=True, stop=False, skip_group_check=True)
            keep_clock(1, 4)
            pe.wait_ge(pool_dve, 1)
            pe.wait_ge(pool_act, 1)
            for g in range(TB):
                last = nc.tensor.matmul(PS[32 * g:32 * g + 32, 0, 0:H1], pool_bd[:, g, :], ew1[:, g, :],
                                        start=False, stop=True, skip_group_check=True)
            last.then_inc(hid_done, 1)
            nc.tensor.matmul(PS[0:C, 2, 0:P], eb2[:, :], con("obias", E_), start=True, stop=False, skip_group_check=True)
            keep_clock(1, 4)
            pe.wait_ge(hid_rdy, 1)
            nc.tensor.transpose(PS[:, 1, 0:P], hid[:, :], idn).then_inc(hidT_done, 1)
            keep_clock(1, 4)
            pe.wait_ge(hidT_rdy, 1)
            for e in range(E_):
                last = nc.tensor.matmul(PS[0:C, 2, e:e + E_ * (B - 1) + 1:E_], ew2[:, e, :], hidT[:, e * B:(e + 1) * B],
                                        start=False, stop=True, skip_group_check=True)
            last.then_inc(eo_done, 1)
            keep_clock(1, 4)
            pe.wait_ge(eo_rdy, 1)
            nc.tensor.transpose(PS[:, 3, 256:256 + C], eoutT[:, :], idn[0:C, 0:C]).then_inc(eoT_done, 1)
            keep_clock(1, 4)
            pe.wait_ge(eobd_rdy, 1)
            for t in range(T):
                rows = slice(TB * E_ * t, TB * E_ * (t + 1))
                for i in range(NP):
                    last = nc.tensor.matmul(band(4 + 2 * t, i), eout_bd[rows, :, :], patches(pick[rows, :], i), start=True, stop=True)
                last.then_inc(scat_done, 1)

            layernorm(2, xs[2])
            def pixels_out(i):
                for t in range(T):
                    pe.wait_ge(y_rdy, 2 * T + t + 1)
                    for p in range(2 * i, min(2 * i + 2, NPT)):
                        last = nc.tensor.matmul(PS[0:V2, i, ((p % 2) * T + t) * P:((p % 2) * T + t + 1) * P],
                                                y[:, t, p * V2:(p + 1) * V2], conv_bd[:, :],
                                                start=True, stop=True, skip_group_check=True)
                last.then_inc(pT_done, 1)

            def mab_product(i):
                pe.wait_ge(xT_rdy, i + 1)
                n = min(2, NPT - 2 * i)
                nc.tensor.matmul(PS[:, (5 + i) % 8, 0:n * T * P], mab[:, :], patch_pair(xT, i), start=True, stop=True).then_inc(u_done, 1)

            pixels_out(0)
            for i in range(1, PAIRS):
                pixels_out(i)
                mab_product(i - 1)
            mab_product(PAIRS - 1)

            def cval_products(k):
                g0, n = QUADS[k]
                for i in range(n):
                    w = gw_of(g0 + i)
                    cols = slice((g0 + i) * GW, (g0 + i) * GW + w)
                    nc.tensor.matmul(PS[0:w, CVAL_BANK[k], i * V2:(i + 1) * V2], xT[:, cols], wcT[:, :], start=True, stop=True)

            def gram_products(k):
                g0, n = QUADS[k]
                for i in range(n):
                    w = gw_of(g0 + i)
                    cols = slice((g0 + i) * GW, (g0 + i) * GW + w)
                    last = nc.tensor.matmul(PS[0:w, GRAM_BANK[k], i * GW:i * GW + w], xT[:, cols], uT[:, cols], start=True, stop=True)
                last.then_inc(gram_done, 1)

            def gram_quad(k):
                cval_products(k)
                gram_products(k)

            def yv_quad(k):
                g0, n = QUADS[k]
                pe.wait_ge(gram_rdy, k + 1)
                pe.wait_ge(cval_rdy, k + 1)
                for i in range(n):
                    w = gw_of(g0 + i)
                    last = nc.tensor.matmul(PS[0:V2, YV_BANK[k], i * GW:i * GW + w], cval[0:w, g0 + i, :],
                                            gram[0:w, g0 + i, 0:w], start=True, stop=True)
                last.then_inc(yv_done, 1)

            pe.wait_ge(u_rdy, 1)
            cval_products(0)
            pe.wait_ge(u_rdy, PAIRS)
            gram_products(0)
            for k in (1, 2):
                gram_quad(k)
            yv_quad(0)
            gram_quad(3)
            yv_quad(1)
            gram_quad(4)
            for k in (2, 3, 4):
                yv_quad(k)
            pe.wait_ge(yv_rdy, 5)
            yv3 = yvT[:, :].rearrange("k (b p) -> k b p", p=NPT)
            for t in range(T):
                for p in range(NPT):
                    last = nc.tensor.transpose(PS[:, BACK_BANK[t] + p // 6, (p % 6) * V2:(p % 6 + 1) * V2],
                                               yv3[:, t * P:(t + 1) * P, p], idn[0:V2, 0:V2])
                last.then_inc(back_done, 1)
            keep_clock(2, 7)

            def first_token(h_, bank):
                nc.tensor.transpose(PS[0:1, bank, 0:C], h_[0:C, 0, 0:1], idn[0:C, 0:C]).then_inc(row_done, 1)

            pe.wait_ge(x3_rdy, 1)
            first_token(xs[3], 6)
            pe.wait_ge(row_rdy, 1)
            layernorm(3, xs[3])

            def second(t, nf):
                wait_for(pe, relu_rdy, nf * B + (t + 1) * TB)
                for g in range(2):
                    for j in range(TB):
                        last = nc.tensor.matmul(PS[j * C:(j + 1) * C, 4 + 2 * t + g, 0:HS], fw2[:, :],
                                                relu_h[:, t * TB + j, g * HS:(g + 1) * HS], start=True, stop=True)
                last.then_inc(z_done, 1)

            runs_a, runs_f, steps = (pe.alloc_register(n) for n in ("pe_a", "pe_f", "pe_s"))
            cr = pe.alloc_register("pe_code")
            for r in (runs_a, runs_f, steps):
                pe.reg_mov(r, 0)
            keep_clock(1, 1)
            pe.wait_ge(xc_copied, 4 * T)
            pe.wait_ge(ctrl_rdy, 1)
            pe.reg_load(cr, ctrl[0:1, 0:1])
            with pe.While(lambda: pe.snap(cr) < NONE):
                c_ = pe.snap(cr, min_val=0, max_val=4 * NB_ * NOPS - 1)
                with pe.If((c_ & 2) > 0):
                    na = pe.snap(runs_a, min_val=0, max_val=NB_)
                    wait_for(pe, aw_ld, na * 64 + 64)
                    with pe.Fori(0, B) as b:
                        d0 = na * ADVE_R + b * ADVE_B + 1
                        wait_for(pe, at_dve, d0 + 1)
                        for g in range(2):
                            for i in range(2):
                                nc.tensor.matmul(PS[0:C, 2 * i + g, 0:HS], aw[:, i, :], hb[:, g * HS:(g + 1) * HS], start=True, stop=True)
                        for c in range(NCH):
                            last = nc.tensor.matmul(PS[0:SC_, 4, c * C:(c + 1) * C], hb[:, c * SC_:(c + 1) * SC_], aw[:, 2, :],
                                                    start=True, stop=True)
                        last.then_inc(at_pe, 1)
                        with pe.Fori(0, NCH) as i:
                            di = d0 + i * ADVE_I + 2
                            wait_for(pe, at_dve, di + 1)
                            for g in range(2):
                                last = nc.tensor.matmul(PS[0:SC_, g, 0:HS], qi[:, :], kT_[:, g * HS:(g + 1) * HS], start=True, stop=True)
                            last.then_inc(at_pe, 1)
                            wait_for(pe, at_dve, di + 5)
                            for c in range(NCH):
                                last = nc.tensor.transpose(PS[0:SC_, 2 + c // 3, (c % 3) * SC_:(c % 3 + 1) * SC_],
                                                           arow[:, c * SC_:(c + 1) * SC_], idn[0:SC_, 0:SC_])
                            last.then_inc(at_pe, 1)
                            wait_for(pe, at_dve, di + 6)
                            for c in range(NCH):
                                last = nc.tensor.matmul(PS[0:C, 5, 0:SC_], vk[:, c, :], aT[:, c, :], start=(c == 0), stop=(c == NCH - 1))
                            last.then_inc(at_pe, 1)
                        wait_for(pe, at_dve, d0 + 2 + NCH * ADVE_I)
                        for g in range(2):
                            last = nc.tensor.matmul(PS[0:C, 6 + g, 0:HS], aw[:, 3, :], oT[:, g * HS:(g + 1) * HS], start=True, stop=True)
                        last.then_inc(at_pe, 1)
                    pe.reg_add(runs_a, runs_a, 1)
                with pe.If((c_ & 1) > 0):
                    na = pe.snap(runs_a, min_val=0, max_val=NB_)
                    nf = pe.snap(runs_f, min_val=0, max_val=NB_)
                    wait_for(pe, fw1_ld, nf * 16 * TB + 16 * TB)
                    for t in range(T):
                        wait_for(pe, h_upd, na * T + nf * T + t + 1)
                        for j in range(TB):
                            k = t * TB + j
                            if k >= 2:
                                wait_for(pe, relu_rdy, nf * B + k - 1)
                            for g in range(2):
                                last = nc.tensor.matmul(PS[:, 2 * (k % 2) + g, 0:HS], fw1[:, j, :], cut(h, t)[:, g, :], start=True, stop=True)
                            last.then_inc(f1_done, 1)
                            if k == TB:
                                wait_for(pe, fw_ld, nf * FW_DMAS + FW_DMAS)
                                second(0, nf)
                            if k == TB + 1:
                                wait_for(pe, h_upd, na * T + nf * T + T + 1)
                                first_token(h, 4)
                    second(1, nf)
                    pe.reg_add(runs_f, runs_f, 1)
                with pe.If((c_ & 1) < 1):
                    na = pe.snap(runs_a, min_val=0, max_val=NB_)
                    nf = pe.snap(runs_f, min_val=0, max_val=NB_)
                    wait_for(pe, h_upd, na * T + nf * T + T)
                    first_token(h, 4)
                pe.reg_add(steps, steps, 1)
                st = pe.snap(steps, min_val=1, max_val=NB_)
                wait_for(pe, ctrl_rdy, st + 1)
                pe.reg_load(cr, ctrl[0:1, 0:1])

        @block.scalar
        def _(act):
            act.dma_start(x_in[:, 1, :], x[TB:B].rearrange("b c h w -> (b c) (h w)")).then_inc(x_ld[1], 16)
            act.dma_start(w_nat[:, :], L0_conv_W_trans).then_inc(w_ld, 16)
            act.dma_start(gw_nat[:, :], L0_ffn_gate_w).then_inc(w_ld, 16)
            act.dma_start(wc_nat[:, :], L1_conv_Wconv).then_inc(w_ld, 16)
            def layernorm(i, eps):
                def squares(t):
                    act.wait_ge(xc_rdy, T * i + t + 1)
                    nc.scalar.activation(cut(sq, t), half(t), ACT.Square).then_inc(sq_rdy, 1)

                def keep(t):
                    nc.scalar.copy(cut(xc, t), half(t)).then_inc(xc_copied, 1)

                squares(0)
                keep(0)
                squares(1)
                act.wait_ge(var_rdy, i + 1)
                nc.scalar.activation(std[:, :], PS[:, 4, 0:QS], ACT.Sqrt, bias=eps[:, :]).then_inc(std_rdy, 1)
                keep(1)

            def load_table(f):
                nc.scalar.activation(tab[:, :], tab[:, :], f)

            act.wait_ge(eps_set, 1)
            load_table(ACT.Sqrt)
            layernorm(0, eps6)
            load_table(ACT.Exp)
            act.wait_ge(border0, 1)
            def qkv_out(i):
                w, t, bank = QKV[i]
                act.wait_ge(qkv_done, i + 1)
                src = PS[:, bank:bank + 2, 0:HS]
                if w == 0:
                    nc.scalar.copy(cut(q_sb, t), src).then_inc(qkv_rdy, 1)
                else:
                    nc.scalar.copy(inner((kpad, vpad)[w - 1], t), rows24(src, t)).then_inc(qkv_rdy, 1)

            for i in range(4):
                qkv_out(i)
            for m in range(NBR // TRI):
                act.wait_ge(sdiff_rdy, m + 1)
                nc.scalar.activation(att[:, m * TRI:(m + 1) * TRI, :], att[:, m * TRI:(m + 1) * TRI, :], ACT.Exp,
                                     scale=HD ** -0.5).then_inc(sexp_rdy, 1)
            qkv_out(4)
            qkv_out(5)
            load_table(ACT.Sqrt)

            layernorm(1, eps5)
            load_table(ACT.Exp)
            act.wait_ge(logit_done, 1)
            act.wait_ge(gb_ld, 16)
            nc.scalar.activation(logit[:, :].rearrange("p (g s) -> p g s", g=2), PS[:, 4:6, 0:HS], ACT.Identity,
                                 bias=gb[:, :]).then_inc(logit_rdy, 1)
            act.wait_ge(ntop_rdy, 1)
            nc.scalar.activation(prob[:, :], logit[:, :], ACT.Exp, bias=ntop[:, :], accum_out=psum_[:, :]).then_inc(prob_rdy, 1)
            for i in range(NCH // 2):
                act.wait_ge(yT_done, i + 1)
                nc.scalar.copy(yT[:, 2 * i:2 * i + 2, :, :].rearrange("k c t p -> k (c t p)"), PS[0:SC_, i, :]).then_inc(yT_rdy, 1)
            load_table(ACT.Gelu)
            act.wait_ge(pool_done, 1)
            act.wait_ge(border0, 1)
            for j in (2, 3):
                for e in range(TB):
                    last = nc.scalar.copy(pool_dst(j, e), pool_src(j, e))
            last.then_inc(pool_act, 1)
            act.wait_ge(hid_done, 1)
            nc.scalar.activation(hid[:, :], PS[:, 0, 0:H1], ACT.Gelu).then_inc(hid_rdy, 1)
            load_table(ACT.Sqrt)

            layernorm(2, eps6)
            for i in range(PAIRS):
                act.wait_ge(u_done, i + 1)
                n = min(2, NPT - 2 * i)
                nc.scalar.copy(patch_pair(uT, i), PS[:, (5 + i) % 8, 0:n * T * P].rearrange("k (p b) -> k p b", p=n)).then_inc(u_rdy, 1)

            def cval_quad(k):
                g0, n = QUADS[k]
                act.wait_ge(gram_done, k + 1)
                full = n if g0 + n < NGRP else n - 1
                last = nc.scalar.copy(cval[:, g0:g0 + full, :],
                                      PS[0:GW, CVAL_BANK[k], 0:full * V2].rearrange("p (g c) -> p g c", c=V2))
                if full < n:
                    last = nc.scalar.copy(cval[0:last_w, NGRP - 1, :], PS[0:last_w, CVAL_BANK[k], full * V2:n * V2])
                last.then_inc(cval_rdy, 1)

            def yv_copy(k):
                g0, n = QUADS[k]
                act.wait_ge(yv_done, k + 1)
                w = (n - 1) * GW + gw_of(g0 + n - 1)
                nc.scalar.copy(yvT[:, g0 * GW:g0 * GW + w], PS[0:V2, YV_BANK[k], 0:w]).then_inc(yv_rdy, 1)

            for k in range(4):
                cval_quad(k)
            yv_copy(0)
            cval_quad(4)
            for k in range(1, 5):
                yv_copy(k)

            layernorm(3, eps5)
            runs_a, runs_f, steps, cr = (act.alloc_register(n) for n in ("act_a", "act_f", "act_steps", "act_code"))
            for r in (runs_a, runs_f, steps):
                act.reg_mov(r, 0)
            act.wait_ge(ctrl_rdy, 1)
            act.reg_load(cr, ctrl[0:1, 0:1])
            with act.While(lambda: act.snap(cr) < NONE):
                c_ = act.snap(cr, min_val=0, max_val=4 * NB_ * NOPS - 1)
                with act.If((c_ & 2) > 0):
                    na = act.snap(runs_a, min_val=0, max_val=NB_)
                    with act.Fori(0, B) as b:
                        with act.Fori(0, NCH) as i:
                            wait_for(act, at_dve, na * ADVE_R + 1 + b * ADVE_B + 2 + i * ADVE_I + 3)
                            nc.scalar.activation(prow[:, :].rearrange("p (g s) -> p g s", g=2), PS[0:SC_, 0:2, 0:HS], ACT.Exp,
                                                 scale=C ** -0.5, bias=nmax[:, 1:2], accum_out=rsum[:, :]).then_inc(at_act, 1)
                    act.reg_add(runs_a, runs_a, 1)
                with act.If((c_ & 1) > 0):
                    nf = act.snap(runs_f, min_val=0, max_val=NB_)
                    load_table(ACT.Relu)
                    wait_for(act, fw_ld, nf * FW_DMAS + FW_DMAS)
                    for k in range(B):
                        wait_for(act, f1_done, nf * B + k + 1)
                        nc.scalar.activation(relu_h[:, k, :].rearrange("p (g s) -> p g s", g=2),
                                             PS[:, 2 * (k % 2):2 * (k % 2) + 2, 0:HS], ACT.Relu, bias=fb1[:, :]).then_inc(relu_rdy, 1)
                    act.reg_add(runs_f, runs_f, 1)
                act.reg_add(steps, steps, 1)
                wait_for(act, ctrl_rdy, act.snap(steps, min_val=1, max_val=NB_) + 1)
                act.reg_load(cr, ctrl[0:1, 0:1])

        @block.vector
        def _(dve):
            nc.vector.memset(spread[:, :, :, :], 0.0).then_inc(spread_zero, 1)
            dve.wait_ge(spread_zero, 1)
            dve.wait_ge(c1_in, 16)
            for q in range(4):
                rows = slice(32 * q, 32 * q + 32)
                last = nc.vector.tensor_copy(spread[rows, :, q, :], con("heads", 32, 32 * q).rearrange("p (t m) -> p t m", t=T))
            last.then_inc(spread_rdy, 1)
            dve.wait_ge(bd_zero, 1)
            dve.wait_ge(wT_done, 1)
            for j in range(TB):
                rows = slice(j * C, (j + 1) * C)
                nc.vector.tensor_copy(qkv_bd[rows, :, j * C:(j + 1) * C], PS[0:C, 7, 0:96].rearrange("p (s o) -> p s o", s=3))
                nc.vector.tensor_copy(gate_bd[rows, j * E_:(j + 1) * E_], PS[0:C, 7, 96:96 + E_])
                last = nc.vector.tensor_copy(conv_bd[rows, j * C:(j + 1) * C], PS[0:C, 7, 112:112 + C])
            last.then_inc(wT_copied, 1)

            def layernorm(i, dst):
                dve.wait_ge(std_rdy, i + 1)
                nc.vector.reciprocal(rstd[:, :], std[:, :]).then_inc(rstd_rdy, 1)
                for t in range(T):
                    dve.wait_ge(xc_copied, T * i + t + 1)
                    dve.wait_ge(rwide_rdy, T * i + t + 1)
                    nc.vector.tensor_tensor(cut(dst, t), half(t, 4), cut(xc, t), ALU.mult).then_inc(y_sem[i], 1)

            layernorm(0, y)

            for t in range(T):
                for n in range(NDVE):
                    dy, dx = divmod(n, 3)
                    if n == 0:
                        dve.wait_ge(qkv_rdy, 2 * t + 2)
                    nc.vector.tensor_tensor(prods[:, t, n, :].rearrange("p (r c) -> p r c", c=WW),
                                            q_sb[:, t, :].rearrange("p (r c) -> p r c", c=WW),
                                            kpad[:, t, dy:dy + HH, dx:dx + WW], ALU.mult).then_inc(prod_rdy, 1)
            dve.wait_ge(score_rdy, 2)
            nc.vector.tensor_reduce(smax2[:, 0, :], PS[:, 4:6, 0:TRI * QS].rearrange("p b (m s) -> p s b m", s=QS), AX.XY, ALU.max)
            dve.wait_ge(score_rdy, 3)
            nc.vector.tensor_reduce(smax2[:, 1, :], PS[:, 6, 0:TRI * QS].rearrange("p (m s) -> p s m", s=QS), AX.X,
                                    ALU.max).then_inc(smax_rdy, 1)
            dve.wait_ge(smax_rdy, 1)
            nc.vector.tensor_tensor(smax[:, :], smax2[:, 0, :], smax2[:, 1, :], ALU.max).then_inc(smax_rdy, 1)
            dve.wait_ge(smax_rdy, 2)
            part = [P, TRI, QS]
            for m in range(NBR // TRI):
                nc.vector.tensor_tensor(att[:, m * TRI:(m + 1) * TRI, :], PS[:, 4 + m, 0:TRI * QS].rearrange("p (m s) -> p m s", s=QS),
                                        smax[:, :].unsqueeze(1).to_broadcast(part), ALU.subtract).then_inc(sdiff_rdy, 1)
            dve.wait_ge(mab_done, 1)
            dve.wait_ge(xT_ones, 2)
            nc.vector.tensor_copy(mab[0:V2 + 1, 0:V2 + 1], PS[0:V2 + 1, 7, 0:V2 + 1])
            nc.vector.tensor_copy(wcT[0:V2 + 1, :].rearrange("k (r c) -> k r c", r=RV),
                                  PS[0:V2 + 1, 7, 128:128 + R2].rearrange("k (r c) -> k r c", r=R)[:, 0:RV, 0:RV]).then_inc(mab_copied, 1)
            dve.wait_ge(sexp_rdy, 3)
            nc.vector.tensor_reduce(ssum[:, :], att[:, :, :].rearrange("p n s -> p s n"), AX.X, ALU.add).then_inc(ssum_rdy, 1)
            dve.wait_ge(ssum_rdy, 1)
            nc.vector.reciprocal(srec[:, :], ssum[:, :]).then_inc(ssum_rdy, 1)
            dve.wait_ge(ssum_rdy, 2)
            for m in range(NBR // TRI):
                nc.vector.tensor_tensor(att[:, m * TRI:(m + 1) * TRI, :], att[:, m * TRI:(m + 1) * TRI, :],
                                        srec[:, :].unsqueeze(1).to_broadcast(part), ALU.mult).then_inc(att_rdy, 1)
            for u in range(WIDE):
                t, m3 = divmod(u, NBR // TRI)
                dve.wait_ge(wide_rdy, u + 1)
                for m in range(TRI):
                    dy, dx = divmod(m3 * TRI + m, 3)
                    last = nc.vector.tensor_tensor(
                        prods[:, t, m3 * TRI + m, :].rearrange("p (q r c) -> p q r c", q=4, c=WW),
                        PS[:, 4 * (u % 2):4 * (u % 2) + 4, m * QS:(m + 1) * QS].rearrange("p q (r c) -> p q r c", c=WW),
                        vpad[:, t, dy:dy + HH, dx:dx + WW].rearrange("p (q r) c -> p q r c", q=4), ALU.mult)
                last.then_inc(wide_used, 1)
                dve.wait_ge(wide_used, u + 1)
                a, b, c = (prods[:, t, m3 * TRI + m, :] for m in range(TRI))
                nc.vector.tensor_tensor(a, a, b, ALU.add).then_inc(pair_rdy, 1)
            dve.wait_ge(pair_rdy, WIDE)
            nc.vector.tensor_tensor(a, a, c, ALU.add).then_inc(last_trio, 1)
            dve.wait_ge(last_trio, 1)
            dve.wait_ge(acc_rdy, WIDE - 1)
            nc.vector.tensor_tensor(xs[1][:, T - 1, :], x_in[:, T - 1, :], a, ALU.add).then_inc(x1_rdy, 1)

            layernorm(1, y)
            dve.wait_ge(logit_rdy, 1)
            nc.vector.max(top8[:, :], logit[:, :]).then_inc(top_rdy, 1)
            dve.wait_ge(top_rdy, 1)
            nc.vector.tensor_scalar(ntop[:, :], top8[:, 0:1], -1.0, None, ALU.mult).then_inc(ntop_rdy, 1)
            nc.vector.match_replace(rest[:, :], top8[:, :], logit[:, :], -3e38).then_inc(rest_rdy, 1)
            dve.wait_ge(rest_rdy, 1)
            nc.vector.tensor_tensor(ismine[:, :], logit[:, :], rest[:, :], ALU.not_equal).then_inc(mine_rdy, 1)
            dve.wait_ge(prob_rdy, 1)
            nc.vector.reciprocal(prec[:, :], psum_[:, :]).then_inc(prec_rdy, 1)
            dve.wait_ge(prec_rdy, 1)
            dve.wait_ge(mine_rdy, 1)
            nc.vector.scalar_tensor_tensor(pick[:, :], prob[:, :], prec[:, :], ismine[:, :], ALU.mult, ALU.mult).then_inc(pick_rdy, 1)
            for i, n in enumerate((4, NCH - 4)):
                dve.wait_ge(pickT_done, i + 1)
                nc.vector.tensor_copy(pickT[:, 4 * i:4 * i + n, :].rearrange("k c p -> k (c p)"), PS[0:SC_, 6 + i, 0:n * P]).then_inc(pickT_rdy, 1)
            dve.wait_ge(border0, 1)
            dve.wait_ge(pool_done, 1)
            for j in (0, 1):
                for e in range(TB):
                    last = nc.vector.tensor_copy(pool_dst(j, e), pool_src(j, e))
            last.then_inc(pool_dve, 1)
            dve.wait_ge(hidT_done, 1)
            nc.vector.tensor_copy(hidT[:, :], PS[:, 1, 0:P]).then_inc(hidT_rdy, 1)
            dve.wait_ge(eo_done, 1)
            nc.vector.tensor_copy(eoutT[:, :], PS[0:C, 2, 0:P]).then_inc(eo_rdy, 1)
            dve.wait_ge(eoT_done, 1)
            nc.vector.tensor_tensor(eout_bd[:, :, :], PS[:, 3, 256:256 + C].unsqueeze(1).to_broadcast([P, TB, C]),
                                    con("own").unsqueeze(2).to_broadcast([P, TB, C]), ALU.mult).then_inc(eobd_rdy, 1)
            for t in range(T):
                dve.wait_ge(scat_done, t + 1)
                for i in range(NP):
                    last = nc.vector.tensor_tensor(xs[2][:, t, i * BAND:(i + 1) * BAND].rearrange("p (j r c) -> p j r c", j=NP, r=RV),
                                                   band(4 + 2 * t, i), patches(xs[1][:, t, :], i), ALU.add)
                last.then_inc(x2_rdy, 1)

            layernorm(2, y)
            xT4 = xT[0:V2, :].rearrange("k (t b p) -> k p t b", t=T, p=NPT)
            dve.wait_ge(wconv_ld, 16 * 10)
            dve.wait_ge(xT_ones, 3)
            for i in range(5):
                dve.wait_ge(pT_done, i + 1)
                n = min(2, NPT - 2 * i)
                nc.vector.tensor_tensor(xT4[:, 2 * i:2 * i + n, :, :],
                                        PS[0:V2, i, 0:n * T * P].rearrange("k (p t b) -> k p t b", p=n, t=T),
                                        bc_rows[:, :].unsqueeze(1).unsqueeze(1).to_broadcast([V2, n, T, P]), ALU.add).then_inc(xT_rdy, 1)
            for k, (g0, n) in enumerate(QUADS):
                dve.wait_ge(gram_done, k + 1)
                full = n if g0 + n < NGRP else n - 1
                last = nc.vector.tensor_tensor(gram[:, g0:g0 + full, :],
                                               PS[0:GW, GRAM_BANK[k], 0:full * GW].rearrange("p (g c) -> p g c", c=GW),
                                               con("blk", GW).unsqueeze(1).to_broadcast([GW, full, GW]), ALU.mult)
                if full < n:
                    last = nc.vector.tensor_tensor(gram[0:last_w, NGRP - 1, 0:last_w],
                                                   PS[0:last_w, GRAM_BANK[k], full * GW:full * GW + last_w],
                                                   con("blk", last_w)[:, 0:last_w], ALU.mult)
                last.then_inc(gram_rdy, 1)
            for t in range(T):
                dve.wait_ge(back_done, t + 1)
                for b, n in ((0, 2 * BAND), (1, BAND)):
                    px = slice(2 * BAND * b, 2 * BAND * b + n)
                    last = nc.vector.tensor_tensor(xs[3][:, t, px], PS[:, BACK_BANK[t] + b, 0:n], xs[2][:, t, px], ALU.add)
                last.then_inc(x3_rdy, 1)

            dve.wait_ge(code_st, 8)
            runs_a, runs_f, steps, cr = (dve.alloc_register(n) for n in ("dve_a", "dve_f", "dve_steps", "dve_code"))
            for r in (runs_a, runs_f, steps):
                dve.reg_mov(r, 0)

            CTL = 6

            def choose(n, bank, add_tile0=False):
                base = n * CTL
                wait_for(dve, row_done, n + 1)
                nc.vector.tensor_copy(row[:, :], PS[0:1, bank, 0:C]).then_inc(row_rdy, 1)
                wait_for(dve, row_rdy, n + 1)
                nc.vector.max(rmax[:, :], row[:, 0:NOPS]).then_inc(ctl_step, 1)
                if add_tile0:
                    band_add(nc.vector, 0, 0)
                wait_for(dve, ctl_step, base + 1)
                nc.vector.max_index(ridx[:, :], rmax[:, :], row[:, 0:NOPS]).then_inc(ctl_step, 1)
                if add_tile0:
                    band_add(nc.vector, 0, 1)
                wait_for(dve, ctl_step, base + 2)
                nc.vector.tensor_copy(opf[:, :], ridx[:, 0:1]).then_inc(ctl_step, 1)
                if add_tile0:
                    band_add(nc.vector, 0, 2).then_inc(fin_rdy, 1)
                wait_for(dve, ctl_step, base + 3)
                nc.vector.tensor_scalar(hot[:, :], con("iop", 1), opf[:, :], None, ALU.is_equal).then_inc(ctl_step, 1)
                wait_for(dve, ctl_step, base + 4)
                nc.vector.tensor_tensor(csel[:, :, :], code[:, :, :], hot[:, :].unsqueeze(1).to_broadcast([1, NB_, NOPS]),
                                        ALU.mult).then_inc(ctl_step, 1)
                wait_for(dve, ctl_step, base + 5)
                nc.vector.tensor_reduce(cand[:, :], csel[:, :, :], AX.X, ALU.add).then_inc(ctl_step, 1)
                wait_for(dve, ctl_step, base + 6)
                nc.vector.tensor_reduce(nextf[:, :], cand[:, :], AX.X, ALU.min).then_inc(next_rdy, 1)
                wait_for(dve, next_rdy, n + 1)
                nc.vector.tensor_copy(ctrl[:, 0:1], nextf[:, :]).then_inc(ctrl_rdy, 1)

            def strike_out(n):
                nc.vector.tensor_scalar(late[:, :], con("istep", 1), nextf[:, :], float(NONE), ALU.is_le, ALU.mult).then_inc(late_rdy, 1)
                wait_for(dve, late_rdy, 2 * n + 1)
                nc.vector.tensor_tensor(code[:, :, :], code[:, :, :], late[:, :].unsqueeze(2).to_broadcast([1, NB_, NOPS]),
                                        ALU.add).then_inc(late_rdy, 1)
                wait_for(dve, late_rdy, 2 * n + 2)

            dve.sem_inc(fw_free, 1)
            choose(0, 6)
            dve.wait_ge(ctrl_rdy, 1)
            dve.reg_load(cr, ctrl[0:1, 0:1])
            layernorm(3, h)

            def new_h(t):
                nf = dve.snap(runs_f, min_val=0, max_val=NB_)
                if t == 0:
                    dve.wait_ge(fin_rdy, T)
                wait_for(dve, z_done, nf * T + t + 1)
                nc.vector.tensor_scalar(cut(h, t), half(t, 4), fb2[:, :], None, ALU.add).then_inc(h_upd, 1)

            with dve.While(lambda: dve.snap(cr) < NONE):
                strike_out(dve.snap(steps, min_val=0, max_val=NB_))
                c_ = dve.snap(cr, min_val=0, max_val=4 * NB_ * NOPS - 1)
                with dve.If((c_ & 2) > 0):
                    na = dve.snap(runs_a, min_val=0, max_val=NB_)
                    wait_for(dve, h_upd, na * T + dve.snap(runs_f, min_val=0, max_val=NB_) * T + T)
                    for j in range(TB):
                        last = nc.vector.tensor_copy(h0[:, j::TB, :], h[j * C:(j + 1) * C, :, :])
                    last.then_inc(at_dve, 1)
                    with dve.Fori(0, B) as b:
                        d0 = na * ADVE_R + 1 + b * ADVE_B
                        p0 = na * (B * APE_B) + b * APE_B
                        wait_for(dve, at_dve, d0)
                        nc.vector.tensor_copy(hb[:, :], h0[:, bass.ds(b, 1), :].rearrange("c b s -> c (b s)")).then_inc(at_dve, 1)
                        wait_for(dve, at_pe, p0 + 1)
                        nc.vector.tensor_copy(qT_[:, :].rearrange("p (g s) -> p g s", g=2), PS[0:C, 0:2, 0:HS])
                        nc.vector.tensor_copy(kT_[:, :].rearrange("p (g s) -> p g s", g=2), PS[0:C, 2:4, 0:HS])
                        nc.vector.tensor_copy(vk[:, :, :].rearrange("k c d -> k (c d)"), PS[0:SC_, 4, 0:NCH * C]).then_inc(at_dve, 1)
                        with dve.Fori(0, NCH) as i:
                            di = d0 + 2 + i * ADVE_I
                            pi = p0 + 1 + i * APE_I
                            wait_for(dve, at_dve, di)
                            nc.vector.tensor_copy(qi[:, :], qT_[:, bass.ds(i * SC_, SC_)]).then_inc(at_dve, 1)
                            wait_for(dve, at_pe, pi + 1)
                            nc.vector.tensor_reduce(nmax[:, 0:1], PS[0:SC_, 0:2, 0:HS], AX.XY, ALU.max, negate=True).then_inc(at_dve, 1)
                            wait_for(dve, at_dve, di + 2)
                            nc.vector.tensor_scalar(nmax[:, 1:2], nmax[:, 0:1], C ** -0.5, None, ALU.mult).then_inc(at_dve, 1)
                            wait_for(dve, at_act, (na * B + b) * AACT_B + i + 1)
                            nc.vector.reciprocal(rrec[:, :], rsum[:, :]).then_inc(at_dve, 1)
                            wait_for(dve, at_dve, di + 4)
                            nc.vector.tensor_scalar(arow[:, :], prow[:, :], rrec[:, :], None, ALU.mult).then_inc(at_dve, 1)
                            wait_for(dve, at_pe, pi + 2)
                            nc.vector.tensor_copy(aT[:, :, :].rearrange("k (g c) q -> k g (c q)", g=2), PS[0:SC_, 2:4, 0:HS]).then_inc(at_dve, 1)
                            wait_for(dve, at_pe, pi + 3)
                            nc.vector.tensor_copy(oT[:, bass.ds(i * SC_, SC_)], PS[0:C, 5, 0:SC_]).then_inc(at_dve, 1)
                        wait_for(dve, at_pe, p0 + APE_B)
                        nc.vector.tensor_copy(h0[:, bass.ds(b, 1), :].rearrange("c b (g s) -> c (b g) s", g=2), PS[0:C, 6:8, 0:HS]).then_inc(at_dve, 1)
                    dve.wait_ge(fin_rdy, T)
                    wait_for(dve, at_dve, na * ADVE_R + ADVE_R)
                    for j in range(TB):
                        last = nc.vector.tensor_copy(h[j * C:(j + 1) * C, :, :], h0[:, j::TB, :])
                    last.then_inc(h_upd, T)
                    dve.reg_add(runs_a, runs_a, 1)
                with dve.If((c_ & 1) > 0):
                    nf = dve.snap(runs_f, min_val=0, max_val=NB_)
                    wait_for(dve, fw_ld, nf * FW_DMAS + FW_DMAS)
                    new_h(0)
                dve.reg_add(steps, steps, 1)
                choose(dve.snap(steps, min_val=1, max_val=NB_), 4, add_tile0=True)
                with dve.If((c_ & 1) > 0):
                    new_h(1)
                    dve.reg_add(runs_f, runs_f, 1)
                wait_for(dve, h_upd, T * (dve.snap(runs_a, min_val=0, max_val=NB_) + dve.snap(runs_f, min_val=0, max_val=NB_)) + T)
                dve.sem_inc(fw_free, 1)
                final_add(nc.vector, 1)
                wait_for(dve, ctrl_rdy, dve.snap(steps, min_val=1, max_val=NB_) + 1)
                dve.reg_load(cr, ctrl[0:1, 0:1])


def kernel(**inputs):
    from concourse import bacc
    from concourse.bass_utils import run_bass_kernel_spmd

    nc = bacc.Bacc("TRN2", target_bir_lowering=False, num_devices=1)
    arrays, args = {}, {}
    for name, a in inputs.items():
        a = np.ascontiguousarray(a)
        if a.dtype == np.bool_:
            padded = np.zeros((1, 4 * MWORDS), np.bool_)
            padded[0, :a.size] = a.ravel()
            a = padded.view(np.int32)
        arrays["in_" + name] = a
        args[name] = nc.dram_tensor("in_" + name, a.shape, mybir.dt.from_np(a.dtype), kind="ExternalInput").ap()
    arrays["consts"] = constant_table()
    args["consts"] = nc.dram_tensor("consts", (P, NCST), mybir.dt.float32, kind="ExternalInput").ap()
    arrays["row_codes"] = row_table()
    args["row_codes"] = nc.dram_tensor("row_codes", (1, NB_ * NOPS), mybir.dt.float32, kind="ExternalInput").ap()
    args["out"] = nc.dram_tensor("result", (B, C, HH, WW), mybir.dt.float32, kind="ExternalOutput").ap()
    metaformer(nc, **args)
    return run_bass_kernel_spmd(nc, [arrays], core_ids=[0]).results[0]["result"]
```

```python
from contextlib import ExitStack

import concourse.bass as bass
import numpy as np
from concourse import mybir

B, C, HH, WW = 8, 32, 24, 24
S = HH * WW
P = 128
TB = P // C
T = B // TB
HS = S // 2
HEADS, HD, NBR = 4, C // 4, 9
PW = WW + 2
QS = S // 4
TRI = 3
E_, H1, K_ = 16, 128, 8
SC_, NCH = 96, S // 96
FULL, TAIL = S // P, S % P
R, NP = 9, 3
R2, NPT = R * R, NP * NP
RV = HH // NP
V2 = RV * RV
BAND = NP * V2
GRP = P // NPT
NGRP = -(-B * C // GRP)
GW = GRP * NPT
NB_, NOPS = 33, 19
MWORDS = -(-NB_ * NOPS // 4)
NONE = 4 * 1000
INV = 1.0 / R

_COLS = [("idn", P), ("cen", P), ("mean", T * 32), ("heads", T * P), ("hsum", T * 32), ("own", TB), ("blk", GW),
         ("ebias", P), ("obias", P), ("iop", NOPS), ("istep", NB_)]
OFF, _o = {}, 0
for _n, _w in _COLS:
    OFF[_n] = (_o, _o + _w)
    _o += _w
NCST = _o


def constant_table():
    t = np.zeros((P, NCST), np.float32)
    p = np.arange(P)

    def put(name, a):
        t[:a.shape[0], OFF[name][0]:OFF[name][0] + a.shape[1]] = a

    same = (p[:, None] // C == p[None, :] // C).astype(np.float32)
    put("idn", np.eye(P, dtype=np.float32))
    put("cen", np.eye(P, dtype=np.float32) - same / C)
    bg = p // HD
    for t_ in range(T):
        a = np.zeros((P, 32), np.float32)
        for g in range(HEADS):
            a[p, (t_ * TB + p // C) * HEADS + g] = np.float32(1 / C)
        t[:, OFF["mean"][0] + 32 * t_:OFF["mean"][0] + 32 * (t_ + 1)] = a
        a = np.zeros((P, 32), np.float32)
        a[p, t_ * TB * HEADS + bg] = 1
        t[:, OFF["hsum"][0] + 32 * t_:OFF["hsum"][0] + 32 * (t_ + 1)] = a
        b = np.zeros((P, P), np.float32)
        for q in range(4):
            b[32 * q + t_ * TB * HEADS + bg, p] = 1
        t[:, OFF["heads"][0] + P * t_:OFF["heads"][0] + P * (t_ + 1)] = b
    put("own", ((p[:, None] // E_) % TB == np.arange(TB)).astype(np.float32))
    g = np.arange(GW)
    put("blk", (g[:, None] // NPT == g[None, :] // NPT).astype(np.float32) * np.float32(INV))
    e = np.arange(E_)
    put("ebias", (e[:, None] == p[None, :] // B).astype(np.float32))
    put("obias", (e[:, None] == p[None, :] % E_).astype(np.float32))
    put("iop", np.arange(NOPS, dtype=np.float32)[None, :])
    put("istep", 4 * NOPS * np.arange(NB_, dtype=np.float32)[None, :])
    return t


def row_table():
    return 4 * np.arange(NB_ * NOPS, dtype=np.float32)[None, :]


def metaformer(nc, x, L0_conv_W_trans, L0_ffn_gate_w, L0_ffn_gate_b, L0_ffn_weight1, L0_ffn_weight2,
               L1_conv_Wconv, L1_conv_bconv, L1_conv_Wa, L1_conv_ba, L1_conv_Wb, L1_conv_bb, L1_conv_Wc,
               L1_conv_bc, L1_ffn_ffn_w1, L1_ffn_ffn_b1, L1_ffn_ffn_w2, L1_ffn_ffn_b2, L1_ffn_wq, L1_ffn_wk,
               L1_ffn_wv, L1_ffn_wo, L1_ffn_attn_mask, L1_ffn_ffn_mask, consts, row_codes, out):
    f32, i32, u32, u8 = mybir.dt.float32, mybir.dt.int32, mybir.dt.uint32, mybir.dt.uint8
    ALU, ACT, AX = mybir.AluOpType, mybir.ActivationFunctionType, mybir.AxisListType

    ctx = ExitStack()
    with ctx:
        def sb(name, shape, dt=f32):
            return ctx.enter_context(nc.sbuf_tensor(name, shape, dt))

        def sem(name):
            return ctx.enter_context(nc.semaphore(name))

        cst = sb("cst", [P, NCST])

        def con(name, rows=P, first=0):
            return cst[first:first + rows, OFF[name][0]:OFF[name][1]]

        idn = con("idn")
        prods = sb("prods", [P, T, NBR + 1, S])
        x_in = prods[:, :, NBR, :]
        xs = [None] + [sb(f"x{i}", [P, T, S]) for i in (1, 2, 3)]
        sq = sb("sq", [P, T, S])
        xc = sb("xc", [P, T, S])
        std = sb("std", [P, QS])
        rstd = sb("rstd", [P, QS])
        spread = sb("spread", [P, T, 4, P])
        y = sb("y", [P, T, S])
        q_sb = sb("q_sb", [P, T, S])
        kpad = sb("kpad", [P, T, HH + 2, PW])
        vpad = sb("vpad", [P, T, HH + 2, PW])
        w_nat = sb("w_nat", [96, C])
        gw_nat = sb("gw_nat", [E_, C])
        wc_nat = sb("wc_nat", [C, C])
        qkv_bd = sb("qkv_bd", [P, 3, P])
        gate_bd = sb("gate_bd", [P, TB * E_])
        conv_bd = sb("conv_bd", [P, P])
        att = sb("att", [P, NBR, QS])
        attn = sb("attn", [P, NBR, QS])
        rtile = sb("rtile", [P, 4, QS])
        smax2 = sb("smax2", [P, 2, QS])
        smax = sb("smax", [P, QS])
        ssum = sb("ssum", [P, QS])
        srec = sb("srec", [P, QS])
        gb = sb("gb", [P, 1])
        logit = sb("logit", [P, S])
        rest = sb("rest", [P, S])
        ismine = sb("ismine", [P, S])
        prob = sb("prob", [P, S])
        pick = sb("pick", [P, S])
        top8 = sb("top8", [P, K_])
        ntop = sb("ntop", [P, 1])
        psum_ = sb("psum_", [P, 1])
        prec = sb("prec", [P, 1])
        yT = sb("yT", [P, FULL + 1, T, P])
        pickT = sb("pickT", [P, FULL + 1, P])
        pool_bd = sb("pool_bd", [P, TB, TB * B])
        ew1 = sb("ew1", [P, TB, H1])
        eb1 = sb("eb1", [E_, H1])
        ew2 = sb("ew2", [P, E_, C])
        eb2 = sb("eb2", [E_, C])
        hid = sb("hid", [P, H1])
        hidT = sb("hidT", [P, P])
        eoutT = sb("eoutT", [C, P])
        eout_bd = sb("eout_bd", [P, TB, C])
        wa = sb("wa", [R2, V2 + 1])
        wb = sb("wb", [R2, V2 + 1])
        wc = sb("wc", [R2, V2 + 1])
        wcT = sb("wcT", [P, V2])
        mab = sb("mab", [P, P])
        bc_rows = sb("bc_rows", [V2, P])
        xT = sb("xT", [P, B * C * NPT])
        uT = prods[:, 0, 0:4, :].rearrange("k n s -> k (n s)")
        gram = sb("gram", [GW, NGRP, GW])
        cval = sb("cval", [GW, NGRP, V2])
        yvT = prods[0:V2, 0, 4:8, :].rearrange("k n s -> k (n s)")
        h = sb("h", [P, T, S])
        x3b = prob
        fw1 = sb("fw1", [P, TB, H1])
        fw2 = sb("fw2", [H1, C])
        fb1 = sb("fb1", [H1, 1])
        fb2 = sb("fb2", [P, 1])
        relu_h = prods[:, 0, 0:B, :]
        tab = sb("tab", [1, 1])
        eps5 = sb("eps5", [P, 1])
        eps6 = sb("eps6", [P, 1])
        mask32 = sb("mask32", [1, 2, MWORDS], i32)
        mask8 = mask32[:, :, :].bitcast(u8)
        maskf = sb("maskf", [1, 2, NB_ * NOPS])
        both = sb("both", [1, NB_ * NOPS])
        anyf = sb("anyf", [1, NB_ * NOPS])
        rowc = sb("rowc", [1, NB_ * NOPS])
        code = sb("code", [1, NB_, NOPS])
        rmax = sb("rmax", [1, 8])
        ridx = sb("ridx", [1, 8], u32)
        opf = sb("opf", [1, 1])
        hot = sb("hot", [1, NOPS])
        csel = sb("csel", [1, NB_, NOPS])
        cand = sb("cand", [1, NB_])
        late = sb("late", [1, NB_])
        nextf = sb("nextf", [1, 1])
        ctrl = sb("ctrl", [1, 1], i32)
        h0 = prods[0:C, 1, 0:B, :]
        hb = xc[0:C, 0, 0:S]
        qT_ = xc[0:C, 1, 0:S]
        kT_ = prods[0:C, 0, 0, :]
        vk = q_sb[0:SC_, 0, 0:NCH * C].rearrange("k (c d) -> k c d", c=NCH)
        qi = sb("qi", [C, SC_])
        nmax = sb("nmax", [SC_, 2])
        prow = prods[0:SC_, 0, 1, :]
        arow = prods[0:SC_, 0, 2, :]
        rsum = sb("rsum", [SC_, 1])
        rrec = sb("rrec", [SC_, 1])
        aT = q_sb[0:SC_, 1, :].rearrange("k (c q) -> k c q", c=NCH)
        oT = prods[0:C, 0, 3, :]
        aw = sb("aw", [C, 4, C])

        PS = ctx.enter_context(nc.psum_tensor("PS", [P, 8, 512], f32))

        x_ld = [sem(f"x_ld{i}") for i in range(3)]
        c0_in, c1_in, c2_in, gb_ld, w_ld, wconv_ld, ew_ld, mask_ld, out_st = (
            sem(n) for n in ("c0_in", "c1_in", "c2_in", "gb_ld", "w_ld", "wconv_ld", "ew_ld", "mask_ld", "out_st"))
        border0, sq_set, eps_set, bd_zero, xT_ones, code_st = (
            sem(n) for n in ("border0", "sq_set", "eps_set", "bd_zero", "xT_ones", "code_st"))
        wT_done, wT_copied, mab_done, mab_copied, spread_zero, spread_rdy = (
            sem(n) for n in ("wT_done", "wT_copied", "mab_done", "mab_copied", "spread_zero", "spread_rdy"))
        xc_rdy, xc_copied, sq_rdy, var_rdy, std_rdy, rstd_rdy, rwide_rdy, y_rdy = (
            sem(n) for n in ("xc_rdy", "xc_copied", "sq_rdy", "var_rdy", "std_rdy", "rstd_rdy", "rwide_rdy", "y_rdy"))
        qkv_done, qkv_rdy, prod_rdy, gprod_rdy, score_rdy, smax_rdy, sdiff_rdy, sexp_rdy, ssum_rdy = (
            sem(n) for n in ("qkv_done", "qkv_rdy", "prod_rdy", "gprod_rdy", "score_rdy", "smax_rdy", "sdiff_rdy", "sexp_rdy",
                             "ssum_rdy"))
        wide_rdy, wide_used, pair_rdy, trio_rdy, scaled_rdy, attn_rdy, tail_rdy = (
            sem(n) for n in ("wide_rdy", "wide_used", "pair_rdy", "trio_rdy", "scaled_rdy", "attn_rdy", "tail_rdy"))
        total_rdy, x1_half, acc_rdy, x1_rdy, x2_rdy, x3_rdy = (
            sem(n) for n in ("total_rdy", "x1_half", "acc_rdy", "x1_rdy", "x2_rdy", "x3_rdy"))
        logit_done, logit_rdy, yT_done, yT_rdy, top_rdy, ntop_rdy, rest_rdy, mine_rdy, prob_rdy, prec_rdy = (
            sem(n) for n in ("logit_done", "logit_rdy", "yT_done", "yT_rdy", "top_rdy", "ntop_rdy", "rest_rdy",
                             "mine_rdy", "prob_rdy", "prec_rdy"))
        pick_rdy, pickT_done, pickT_rdy, pool_done, pool_dve, pool_act, hid_done, hid_rdy, hidT_done, hidT_rdy = (
            sem(n) for n in ("pick_rdy", "pickT_done", "pickT_rdy", "pool_done", "pool_dve", "pool_act", "hid_done",
                             "hid_rdy", "hidT_done", "hidT_rdy"))
        eo_done, eo_rdy, eoT_done, eobd_rdy, scat_done = (
            sem(n) for n in ("eo_done", "eo_rdy", "eoT_done", "eobd_rdy", "scat_done"))
        pT_done, xT_rdy, u_done, u_rdy, gram_done, gram_rdy, cval_rdy, yv_done, yv_rdy, back_done = (
            sem(n) for n in ("pT_done", "xT_rdy", "u_done", "u_rdy", "gram_done", "gram_rdy", "cval_rdy", "yv_done",
                             "yv_rdy", "back_done"))
        late_rdy, next_rdy, h_upd, row_done, ctl_step, ctrl_rdy, fw_ld, aw_ld = (
            sem(n) for n in ("late_rdy", "next_rdy", "h_upd", "row_done", "ctl_step", "ctrl_rdy", "fw_ld", "aw_ld"))
        fw1_ld = [sem(f"fw1_ld{j}") for j in range(TB)]
        fb1_ld, x3b_rdy, fw_free, f1_done, relu_rdy, z_done, fin_rdy = (
            sem(n) for n in ("fb1_ld", "x3b_rdy", "fw_free", "f1_done", "relu_rdy", "z_done", "fin_rdy"))
        waited = sem("waited")
        at_pe, at_dve, at_act = (sem(n) for n in ("at_pe", "at_dve", "at_act"))

        def half(t, first=0):
            return PS[:, first + 2 * t:first + 2 * t + 2, 0:HS]

        XB, VB = (0, 4, 0, 0), (4, 0, 4, 4)

        def cut(a, t):
            return a[:, t, 0:S].rearrange("p (g s) -> p g s", g=2)

        def patches(a, i):
            return a.rearrange("p (r i c j) -> p i j r c", r=RV, i=NP, c=RV)[:, i, :, :, :]

        def band(first, i):
            return PS[:, first + i // 2, (i % 2) * BAND:(i % 2 + 1) * BAND].rearrange("p (j r c) -> p j r c", j=NP, r=RV)

        def rows24(a):
            return a.rearrange("p g (r c) -> p g r c", c=WW)

        def inner(a, t):
            return a[:, t, 1:1 + HH, 1:1 + WW].rearrange("p (g r) c -> p g r c", g=2)

        QKV = [(0, 0, 0), (1, 0, 4), (0, 1, 2), (1, 1, 6), (2, 0, 0), (2, 1, 2)]
        WIDE_BANK = (4, 0)
        NDVE = 6
        WIDE = T * NBR // TRI
        last_w = (B * C - (NGRP - 1) * GRP) * NPT
        QUADS = [(g, min(4, NGRP - g)) for g in range(0, NGRP, 4)]
        GRAM_BANK = [0, 1, 2, 3, 4]
        CVAL_BANK = [5, 6, 7, 0, 1]
        YV_BANK = [5, 6, 7, 2, 3]
        BACK_BANK = [0, 4]
        HID_BANK = (0, 2, 6)
        PAIRS = -(-NPT // 2)
        APE_I, ADVE_I, AACT_I = 3, 7, 1
        APE_B, ADVE_B, AACT_B = 2 + NCH * APE_I, 3 + NCH * ADVE_I, NCH * AACT_I
        FW_DMAS = 16 * 2
        ADVE_R = 1 + B * ADVE_B

        def pool_src(j, e):
            a = PS[j * C:(j + 1) * C, 3, 0:2 * TB * E_].rearrange("c (t b g e) -> c b e g t", t=T, b=TB, e=TB)
            return a[:, j, e, :, :]

        def pool_dst(j, e):
            a = pool_bd[e * C:(e + 1) * C, :, :].rearrange("c g (e t b) -> c e b g t", e=TB, t=T)
            return a[:, e, j, :, :]

        x_sem = (None, x1_rdy, x2_rdy, x3_rdy)
        y_sem = (y_rdy, y_rdy, y_rdy, h_upd)

        def patch_pair(a, i):
            n = min(2, NPT - 2 * i)
            return a.rearrange("k (b p) -> k p b", p=NPT)[:, 2 * i:2 * i + n, :]

        def gw_of(g):
            return GW if g < NGRP - 1 else last_w

        def wait_for(eng, signal, value):
            eng.wait_ge(signal, value)
            if not isinstance(value, int):
                eng.sem_inc(waited, 1)

        def band_add(vec, t, i):
            px = slice(i * BAND, (i + 1) * BAND)
            return vec.tensor_tensor(patches(y[:, t, :], i), xs[3][:, t, px].rearrange("p (j r c) -> p j r c", j=NP, r=RV),
                                     h[:, t, px].rearrange("p (j r c) -> p j r c", j=NP, r=RV), ALU.add)

        def final_add(vec, t):
            for i in range(NP):
                last = band_add(vec, t, i)
            last.then_inc(fin_rdy, 1)

        block = ctx.enter_context(nc.Block())

        @block.sync
        def _(sp):
            for g in range(2):
                sp.dma_start(cut(x_in, 0)[:, g, :], x[0:TB].rearrange("b c h w -> (b c) (h w)")[:, g * HS:(g + 1) * HS]).then_inc(x_ld[g], 16)
            sp.dma_start(w_nat[:, :], L0_conv_W_trans).then_inc(w_ld, 16)
            sp.dma_start(gw_nat[:, :], L0_ffn_gate_w).then_inc(w_ld, 16)
            sp.dma_start(wc_nat[:, :], L1_conv_Wconv).then_inc(w_ld, 16)
            sp.dma_start(cst[:, OFF["mean"][0]:OFF["hsum"][0]], consts[:, OFF["mean"][0]:OFF["hsum"][0]]).then_inc(c1_in, 16)
            sp.dma_start(cst[:, OFF["hsum"][0]:], consts[:, OFF["hsum"][0]:]).then_inc(c2_in, 16)
            sp.dma_start(gb[:, :], L0_ffn_gate_b.rearrange("(o e) -> o e", o=1).to_broadcast([B, E_]).unsqueeze(2)).then_inc(gb_ld, 16)
            sp.dma_start(mask32[0:1, 0, :], L1_ffn_attn_mask).then_inc(mask_ld, 16)
            sp.dma_start(mask32[0:1, 1, :], L1_ffn_ffn_mask).then_inc(mask_ld, 16)
            sp.dma_start(rowc[:, :], row_codes).then_inc(mask_ld, 16)
            for i, (w, b) in enumerate(((L1_conv_Wa, L1_conv_ba), (L1_conv_Wb, L1_conv_bb), (L1_conv_Wc, L1_conv_bc))):
                dst = (wa, wb, wc)[i]
                sp.dma_start(dst[:, 0:V2].rearrange("o (r c) -> o r c", r=RV),
                             w.rearrange("o (r c) -> o r c", r=R)[:, 0:RV, 0:RV]).then_inc(wconv_ld, 16)
                sp.dma_start(dst[:, V2:V2 + 1], b.rearrange("(p o) -> p o", o=1)).then_inc(wconv_ld, 16)
            for j in range(TB):
                sp.dma_start(bc_rows[:, j * C:(j + 1) * C], L1_conv_bconv.partition_broadcast(V2)).then_inc(wconv_ld, 16)
            for e in range(TB):
                sp.dma_start(ew1[e * C:(e + 1) * C, :, :],
                             L0_ffn_weight1[e::TB, 0:C, :].rearrange("g c h -> c g h")).then_inc(ew_ld, 16)
            sp.dma_start(eb1[:, :], L0_ffn_weight1[:, C, :]).then_inc(ew_ld, 16)
            sp.dma_start(ew2[:, :, :], L0_ffn_weight2[:, 0:H1, :].rearrange("e h c -> h e c")).then_inc(ew_ld, 16)
            sp.dma_start(eb2[:, :], L0_ffn_weight2[:, H1, :]).then_inc(ew_ld, 16)

            steps, cr, row_no = (sp.alloc_register(n) for n in ("sp_steps", "sp_code", "sp_row"))
            sp.reg_mov(steps, 0)
            sp.wait_ge(border0, 1)
            sp.wait_ge(ctrl_rdy, 1)
            sp.reg_load(cr, ctrl[0:1, 0:1])
            with sp.While(lambda: sp.snap(cr) < NONE):
                c_ = sp.snap(cr, min_val=0, max_val=4 * NB_ * NOPS - 1)
                sp.reg_mov(row_no, c_ >> 2)
                rw = sp.snap(row_no, min_val=0, max_val=NB_ * NOPS - 1)

                def of_step(w):
                    if len(w.shape) == 4:
                        return w.rearrange("b o c d -> (b o) c d")[bass.ds(rw, 1), :, :].rearrange("o c d -> (o c) d")
                    return w.rearrange("b o c -> (b o) c")[bass.ds(rw, 1), :].rearrange("o c -> c o")

                with sp.If((c_ & 2) > 0):
                    for i, w in enumerate((L1_ffn_wq, L1_ffn_wk, L1_ffn_wv, L1_ffn_wo)):
                        sp.dma_start(aw[:, i, :], of_step(w)).then_inc(aw_ld, 16)
                with sp.If((c_ & 1) > 0):
                    wait_for(sp, fw_free, sp.snap(steps, min_val=0, max_val=NB_) + 1)
                    for j in range(TB):
                        sp.dma_start(fw1[j * C:(j + 1) * C, j, :], of_step(L1_ffn_ffn_w1)).then_inc(fw1_ld[j], 16)
                        if j == 0:
                            sp.dma_start(fb1[:, :], of_step(L1_ffn_ffn_b1)).then_inc(fb1_ld, 16)
                    sp.dma_start(fw2[:, :], of_step(L1_ffn_ffn_w2)).then_inc(fw_ld, 16)
                    sp.dma_start(fb2[:, :], of_step(L1_ffn_ffn_b2).unsqueeze(0).to_broadcast([TB, C, 1])).then_inc(fw_ld, 16)
                sp.reg_add(steps, steps, 1)
                wait_for(sp, ctrl_rdy, sp.snap(steps) + 1)
                sp.reg_load(cr, ctrl[0:1, 0:1])

            done = T * sp.snap(steps, min_val=0, max_val=NB_)
            for t in range(T):
                wait_for(sp, fin_rdy, done + t + 1)
                sp.dma_start(out[t * TB:(t + 1) * TB].rearrange("b c h w -> (b c) (h w)"), y[:, t, :]).then_inc(out_st, 16)
            sp.wait_ge(out_st, 16 * T)

        @block.gpsimd
        def _(pool):
            nc.gpsimd.memset(sq[:, 0, 0:HS], 0.0).then_inc(sq_set, 1)
            nc.gpsimd.memset(eps6[:, :], 1e-6)
            nc.gpsimd.memset(tab[:, :], 0.0)
            nc.gpsimd.memset(eps5[:, :], 1e-5).then_inc(eps_set, 1)
            nc.gpsimd.memset(qkv_bd[:, :, :], 0.0)
            nc.gpsimd.memset(gate_bd[:, :], 0.0)
            nc.gpsimd.memset(conv_bd[:, :], 0.0).then_inc(bd_zero, 1)
            nc.gpsimd.memset(kpad[:, :, :, :], 0.0)
            nc.gpsimd.memset(pool_bd[:, :, :], 0.0)
            nc.gpsimd.memset(fw1[:, :, :], 0.0)
            nc.gpsimd.memset(vpad[:, :, :, :], 0.0).then_inc(border0, 1)
            pool.wait_ge(border0, 1)
            nc.gpsimd.memset(mab[:, :], 0.0)
            nc.gpsimd.memset(wcT[:, :], 0.0).then_inc(xT_ones, 1)
            pool.wait_ge(xT_ones, 1)
            nc.gpsimd.memset(xT[V2:P, :], 0.0).then_inc(xT_ones, 1)
            pool.wait_ge(xT_ones, 2)
            nc.gpsimd.memset(xT[V2:V2 + 1, :], 1.0).then_inc(xT_ones, 1)
            pool.wait_ge(xT_ones, 3)
            for t in range(T):
                pool.wait_ge(qkv_rdy, 2 * t + 2)
                for n in range(NDVE, NBR):
                    dy, dx = divmod(n, 3)
                    nc.gpsimd.tensor_tensor(prods[:, t, n, :].rearrange("p (r c) -> p r c", c=WW),
                                            q_sb[:, t, :].rearrange("p (r c) -> p r c", c=WW),
                                            kpad[:, t, dy:dy + HH, dx:dx + WW], ALU.mult).then_inc(gprod_rdy, 1)
            pool.wait_ge(ssum_rdy, 2)
            nc.gpsimd.tensor_tensor(attn[:, :, :], att[:, :, :], srec[:, :].unsqueeze(1).to_broadcast([P, NBR, QS]),
                                    ALU.mult).then_inc(attn_rdy, 1)

            def trio(u):
                t, m3 = divmod(u, NBR // TRI)
                a, c = prods[:, t, m3 * TRI, :], prods[:, t, m3 * TRI + 2, :]
                pool.wait_ge(pair_rdy, u + 1)
                nc.gpsimd.tensor_tensor(a, a, c, ALU.add).then_inc(trio_rdy, 1)
                pool.wait_ge(trio_rdy, u + 1)
                return a

            total = trio(0)
            for u in (1, 2):
                nc.gpsimd.tensor_tensor(total, total, trio(u), ALU.add).then_inc(acc_rdy, 1)
                pool.wait_ge(acc_rdy, u)
            nc.gpsimd.tensor_tensor(prods[:, 1, 1, :], trio(3), x_in[:, 1, :], ALU.add).then_inc(acc_rdy, 1)
            trio(4)
            pool.wait_ge(scaled_rdy, 1)
            nc.gpsimd.tensor_tensor(xs[1][:, 0, :], x_in[:, 0, :], total, ALU.add).then_inc(x1_half, 1)

            pool.wait_ge(mask_ld, 16 * 3)
            nc.gpsimd.tensor_copy(maskf[:, :, :], mask8[:, :, 0:NB_ * NOPS]).then_inc(code_st, 1)
            pool.wait_ge(code_st, 1)
            am, fm = maskf[:, 0, :], maskf[:, 1, :]
            nc.gpsimd.tensor_tensor(both[:, :], am, fm, ALU.mult)
            nc.gpsimd.tensor_tensor(anyf[:, :], am, fm, ALU.add).then_inc(code_st, 1)
            pool.wait_ge(code_st, 2)
            bits = code[:, :, :].rearrange("p b o -> p (b o)")
            nc.gpsimd.tensor_tensor(bits, anyf[:, :], am, ALU.add).then_inc(code_st, 1)
            pool.wait_ge(code_st, 3)
            nc.gpsimd.tensor_tensor(anyf[:, :], anyf[:, :], both[:, :], ALU.subtract).then_inc(code_st, 1)
            nc.gpsimd.tensor_tensor(bits, bits, rowc[:, :], ALU.add).then_inc(code_st, 1)
            pool.wait_ge(code_st, 5)
            nc.gpsimd.tensor_scalar(bits, bits, -float(NONE), None, ALU.add).then_inc(code_st, 1)
            pool.wait_ge(code_st, 6)
            nc.gpsimd.tensor_tensor(bits, bits, anyf[:, :], ALU.mult).then_inc(code_st, 1)
            pool.wait_ge(code_st, 7)
            nc.gpsimd.tensor_scalar(bits, bits, float(NONE), None, ALU.add).then_inc(code_st, 1)

            for t in range(T):
                pool.wait_ge(h_upd, t + 1)
                pool.wait_ge(x3_rdy, t + 1)
                final_add(nc.gpsimd, t)

        @block.tensor
        def _(pe):
            def keep_clock(n, bank):
                for i in range(n):
                    nc.tensor.matmul(PS[:, bank, 0:HS], sq[:, 0, 0:P], sq[:, 0, 0:HS], start=True, stop=True)

            def centre(i, src, t):
                for g in range(2):
                    pe.wait_ge(*((x_ld[(g, 2)[t]], 16) if i == 0 else (x_sem[i], t + 1)))
                    nc.tensor.matmul(PS[:, XB[i] + 2 * t + g, 0:HS], con("cen"), cut(src, t)[:, g, :],
                                     start=True, stop=True).then_inc(xc_rdy, 1)

            def variances(i):
                mean = con("mean").rearrange("p (t m) -> p t m", t=T)
                for t in range(T):
                    for q in range(4):
                        if q % 2 == 0:
                            pe.wait_ge(sq_rdy, 2 * (T * i + t) + q // 2 + 1)
                        last = nc.tensor.matmul(PS[32 * q:32 * q + 32, VB[i], 0:QS], mean[:, t, :], sq[:, t, q * QS:(q + 1) * QS],
                                                start=(t == 0), stop=(t == T - 1), skip_group_check=True)
                last.then_inc(var_rdy, 1)
                keep_clock(2, VB[i] + 1)

            def widen(i):
                pe.wait_ge(rstd_rdy, i + 1)
                if i == 0:
                    pe.wait_ge(spread_rdy, 1)
                for t in range(T):
                    for q in range(4):
                        if i == 0 and t == 1 and q == 2:
                            pe.wait_ge(wT_copied, 2)
                        last = nc.tensor.matmul(PS[:, VB[i] + 2 * t + q // 2, (q % 2) * QS:(q % 2 + 1) * QS], spread[:, t, q, :],
                                                rstd[:, :], start=True, stop=True)
                    last.then_inc(rwide_rdy, 1)

            def layernorm(i, src):
                for t in range(T):
                    centre(i, src, t)
                variances(i)
                widen(i)

            pe.wait_ge(sq_set, 1)
            keep_clock(3, 7)
            pe.wait_ge(c0_in, 16)
            centre(0, x_in, 0)
            centre(0, x_in, 1)
            pe.wait_ge(w_ld, 16 * 3)
            nc.tensor.transpose(PS[0:C, 7, 0:96], w_nat[:, :], idn[0:96, 0:96])
            nc.tensor.transpose(PS[0:C, 7, 96:96 + E_], gw_nat[:, :], idn[0:E_, 0:E_])
            nc.tensor.transpose(PS[0:C, 7, 112:112 + C], wc_nat[:, :], idn[0:C, 0:C]).then_inc(wT_done, 1)
            pe.wait_ge(c1_in, 16)
            variances(0)
            widen(0)

            def qkv_product(i):
                w, t, bank = QKV[i]
                pe.wait_ge(y_rdy, t + 1)
                for g in range(2):
                    last = nc.tensor.matmul(PS[:, bank + g, 0:HS], qkv_bd[:, w, :], cut(y, t)[:, g, :], start=True, stop=True)
                last.then_inc(qkv_done, 1)

            for i in range(4):
                qkv_product(i)

            pe.wait_ge(c2_in, 16)
            pe.wait_ge(qkv_rdy, 2)
            hsum = con("hsum").rearrange("p (t m) -> p t m", t=T)
            for t in range(T):
                if t == 1:
                    pe.wait_ge(wconv_ld, 16 * 10)
                    nc.tensor.matmul(PS[0:V2 + 1, 7, 0:V2 + 1], wa[:, :], wb[:, :], start=True, stop=True)
                    nc.tensor.transpose(PS[0:V2 + 1, 7, P:P + R2], wc[:, :], idn[0:R2, 0:R2]).then_inc(mab_done, 1)
                for n in range(NBR):
                    if t == 0 and n == 2 * TRI:
                        pe.wait_ge(qkv_rdy, 4)
                    if n < NDVE:
                        pe.wait_ge(prod_rdy, NDVE * t + n + 1)
                    else:
                        pe.wait_ge(gprod_rdy, (NBR - NDVE) * t + n - NDVE + 1)
                    for q in range(4):
                        last = nc.tensor.matmul(PS[32 * q:32 * q + 32, 4 + n // TRI, (n % TRI) * QS:(n % TRI + 1) * QS],
                                                hsum[:, t, :], prods[:, t, n, q * QS:(q + 1) * QS],
                                                start=(t == 0 and n % TRI == 0), stop=(t == T - 1), skip_group_check=True)
                    if t == T - 1 and n % TRI == TRI - 1:
                        last.then_inc(score_rdy, 1)
            qkv_product(4)
            qkv_product(5)

            pe.wait_ge(mab_copied, 1)
            for u in range(WIDE):
                t, m = divmod(u, NBR // TRI)
                base = WIDE_BANK[u % 2]
                if t == 0:
                    pe.wait_ge(sexp_rdy, m + 1)
                else:
                    pe.wait_ge(attn_rdy, 1)
                if u == 1:
                    pe.wait_ge(qkv_rdy, 6)
                if u >= 2:
                    pe.wait_ge(wide_used, u - 1)
                for q in (3, 0, 1, 2):
                    if u == 0 and q < NBR // TRI:
                        pe.wait_ge(sdiff_rdy, q + 1)
                    last = nc.tensor.matmul(PS[:, base + q, 0:TRI * QS], spread[:, t, q, :],
                                            (att, attn)[t][:, m * TRI:(m + 1) * TRI, :], start=True, stop=True)
                if u in (1, 2):
                    pe.wait_ge(ssum_rdy, 2)
                    for q in range(4):
                        last = nc.tensor.matmul(PS[:, base + q, TRI * QS:TRI * QS + QS // 2], spread[:, 0, q, :],
                                                srec[:, (u - 1) * QS // 2:u * QS // 2], start=True, stop=True, skip_group_check=True)
                last.then_inc(wide_rdy, 1)

            pe.wait_ge(wide_used, WIDE - 1)
            def centre_part(t, src, first=False, last=False):
                for g in range(2):
                    done = nc.tensor.matmul(PS[:, XB[1] + 2 * t + g, 0:HS], con("cen"), src[:, g * HS:(g + 1) * HS],
                                            start=first, stop=last, skip_group_check=True)
                    if last:
                        done.then_inc(xc_rdy, 1)

            centre_part(0, x_in[:, 0, :], first=True)
            pe.wait_ge(scaled_rdy, 1)
            centre_part(0, prods[:, 0, 0, :], last=True)
            pe.wait_ge(acc_rdy, 3)
            centre_part(1, prods[:, 1, 1, :], first=True)
            pe.wait_ge(tail_rdy, TRI)
            centre_part(1, prods[:, 1, NBR - 1, :])
            pe.wait_ge(total_rdy, 2)
            centre_part(1, prods[:, 1, 4, :], last=True)
            variances(1)
            widen(1)

            for t in range(T):
                pe.wait_ge(y_rdy, T + t + 1)
                for g in range(2):
                    last = nc.tensor.matmul(PS[64 * t:64 * t + 64, 4 + g, 0:HS], gate_bd[:, :], cut(y, t)[:, g, :],
                                            start=True, stop=True)
            last.then_inc(logit_done, 1)
            for c in range(FULL + 1):
                w = P if c < FULL else TAIL
                for t in range(T):
                    last = nc.tensor.transpose(PS[0:w, c // 2, ((c % 2) * T + t) * P:((c % 2) * T + t + 1) * P],
                                               y[:, t, c * P:c * P + w], idn)
                if c % 2 or c == FULL:
                    last.then_inc(yT_done, 1)
            keep_clock(6, 7)
            pe.wait_ge(pick_rdy, 1)
            for c in range(FULL + 1):
                w = P if c < FULL else TAIL
                last = nc.tensor.transpose(PS[0:w, 6 + c // FULL, (c % FULL) * P:(c % FULL + 1) * P], pick[:, c * P:c * P + w], idn)
                if c >= FULL - 1:
                    last.then_inc(pickT_done, 1)
            keep_clock(1, 3)
            pe.wait_ge(yT_rdy, 3)
            for t in range(T):
                for c in range(FULL + 1):
                    w = P if c < FULL else TAIL
                    pe.wait_ge(pickT_rdy, 1 + c // FULL)
                    last = nc.tensor.matmul(PS[:, 3, 64 * t:64 * t + 64], yT[0:w, c, t, :], pickT[0:w, c, 64 * t:64 * t + 64],
                                            start=(c == 0), stop=(c == FULL))
            last.then_inc(pool_done, 1)
            pe.wait_ge(ew_ld, 16 * 7)
            nc.tensor.matmul(PS[:, 0, 0:H1], con("ebias", E_), eb1[:, :], start=True, stop=False, skip_group_check=True)
            keep_clock(1, 4)
            pe.wait_ge(pool_dve, 1)
            pe.wait_ge(pool_act, 1)
            for g in range(TB):
                last = nc.tensor.matmul(PS[32 * g:32 * g + 32, 0, 0:H1], pool_bd[:, g, :], ew1[:, g, :],
                                        start=False, stop=True, skip_group_check=True)
            last.then_inc(hid_done, 1)
            nc.tensor.matmul(PS[0:C, 2, 0:P], eb2[:, :], con("obias", E_), start=True, stop=False, skip_group_check=True)
            keep_clock(1, 4)
            pe.wait_ge(hid_rdy, 1)
            nc.tensor.transpose(PS[:, 1, 0:P], hid[:, :], idn).then_inc(hidT_done, 1)
            keep_clock(1, 4)
            pe.wait_ge(hidT_rdy, 1)
            for e in range(E_):
                last = nc.tensor.matmul(PS[0:C, 2, e:e + E_ * (B - 1) + 1:E_], ew2[:, e, :], hidT[:, e * B:(e + 1) * B],
                                        start=False, stop=True, skip_group_check=True)
            last.then_inc(eo_done, 1)
            keep_clock(1, 4)
            pe.wait_ge(eo_rdy, 1)
            nc.tensor.transpose(PS[:, 3, 256:256 + C], eoutT[:, :], idn[0:C, 0:C]).then_inc(eoT_done, 1)
            keep_clock(1, 4)
            pe.wait_ge(eobd_rdy, 1)
            for t in range(T):
                rows = slice(TB * E_ * t, TB * E_ * (t + 1))
                for i in range(NP):
                    last = nc.tensor.matmul(band(4 + 2 * t, i), eout_bd[rows, :, :], patches(pick[rows, :], i), start=True, stop=True)
                last.then_inc(scat_done, 1)

            layernorm(2, xs[2])
            def pixels_out(i):
                for t in range(T):
                    pe.wait_ge(y_rdy, 2 * T + t + 1)
                    for p in range(2 * i, min(2 * i + 2, NPT)):
                        last = nc.tensor.matmul(PS[0:V2, i, ((p % 2) * T + t) * P:((p % 2) * T + t + 1) * P],
                                                y[:, t, p * V2:(p + 1) * V2], conv_bd[:, :],
                                                start=True, stop=True, skip_group_check=True)
                last.then_inc(pT_done, 1)

            def mab_product(i):
                pe.wait_ge(xT_rdy, i + 1)
                n = min(2, NPT - 2 * i)
                nc.tensor.matmul(PS[:, (5 + i) % 8, 0:n * T * P], mab[:, :], patch_pair(xT, i), start=True, stop=True).then_inc(u_done, 1)

            pixels_out(0)
            for i in range(1, PAIRS):
                pixels_out(i)
                mab_product(i - 1)
            mab_product(PAIRS - 1)

            def cval_products(k):
                g0, n = QUADS[k]
                for i in range(n):
                    w = gw_of(g0 + i)
                    cols = slice((g0 + i) * GW, (g0 + i) * GW + w)
                    nc.tensor.matmul(PS[0:w, CVAL_BANK[k], i * V2:(i + 1) * V2], xT[:, cols], wcT[:, :], start=True, stop=True)

            def gram_products(k):
                g0, n = QUADS[k]
                for i in range(n):
                    w = gw_of(g0 + i)
                    cols = slice((g0 + i) * GW, (g0 + i) * GW + w)
                    last = nc.tensor.matmul(PS[0:w, GRAM_BANK[k], i * GW:i * GW + w], xT[:, cols], uT[:, cols], start=True, stop=True)
                last.then_inc(gram_done, 1)

            def gram_quad(k):
                cval_products(k)
                gram_products(k)

            def yv_quad(k):
                g0, n = QUADS[k]
                pe.wait_ge(gram_rdy, k + 1)
                pe.wait_ge(cval_rdy, k + 1)
                for i in range(n):
                    w = gw_of(g0 + i)
                    last = nc.tensor.matmul(PS[0:V2, YV_BANK[k], i * GW:i * GW + w], cval[0:w, g0 + i, :],
                                            gram[0:w, g0 + i, 0:w], start=True, stop=True)
                last.then_inc(yv_done, 1)

            pe.wait_ge(u_rdy, 1)
            cval_products(0)
            pe.wait_ge(u_rdy, PAIRS)
            gram_products(0)
            for k in (1, 2):
                gram_quad(k)
            yv_quad(0)
            gram_quad(3)
            yv_quad(1)
            gram_quad(4)
            for k in (2, 3, 4):
                yv_quad(k)
            pe.wait_ge(yv_rdy, 5)
            yv3 = yvT[:, :].rearrange("k (b p) -> k b p", p=NPT)
            for t in range(T):
                for p in range(NPT):
                    last = nc.tensor.transpose(PS[:, BACK_BANK[t] + p // 6, (p % 6) * V2:(p % 6 + 1) * V2],
                                               yv3[:, t * P:(t + 1) * P, p], idn[0:V2, 0:V2])
                last.then_inc(back_done, 1)

            def first_token(h_, bank):
                nc.tensor.transpose(PS[0:1, bank, 0:C], h_[0:C, 0, 0:1], idn[0:C, 0:C]).then_inc(row_done, 1)

            pe.wait_ge(x3_rdy, 1)
            first_token(xs[3], 6)
            for t in range(T):
                centre(3, xs[3], t)
            variances(3)
            pe.wait_ge(ctl_step, 2)
            cr = pe.alloc_register("pe_code")
            pe.wait_ge(ctrl_rdy, 1)
            pe.reg_load(cr, ctrl[0:1, 0:1])
            widen(3)

            def second(t, nf):
                wait_for(pe, relu_rdy, nf * B + (t + 1) * TB)
                for i in range(NP):
                    for j in range(TB):
                        last = nc.tensor.matmul(PS[j * C:(j + 1) * C, 4 + 2 * t + i // 2, (i % 2) * BAND:(i % 2 + 1) * BAND], fw2[:, :],
                                                relu_h[:, t * TB + j, i * BAND:(i + 1) * BAND], start=True, stop=True,
                                                skip_group_check=True)
                last.then_inc(z_done, 1)

            runs_a, runs_f, steps = (pe.alloc_register(n) for n in ("pe_a", "pe_f", "pe_s"))
            for r in (runs_a, runs_f, steps):
                pe.reg_mov(r, 0)
            keep_clock(1, 1)
            pe.wait_ge(xc_copied, 4 * T)
            with pe.While(lambda: pe.snap(cr) < NONE):
                c_ = pe.snap(cr, min_val=0, max_val=4 * NB_ * NOPS - 1)
                with pe.If((c_ & 2) > 0):
                    na = pe.snap(runs_a, min_val=0, max_val=NB_)
                    wait_for(pe, aw_ld, na * 64 + 64)
                    with pe.Fori(0, B) as b:
                        d0 = na * ADVE_R + b * ADVE_B + 1
                        wait_for(pe, at_dve, d0 + 1)
                        for g in range(2):
                            for i in range(2):
                                nc.tensor.matmul(PS[0:C, 2 * i + g, 0:HS], aw[:, i, :], hb[:, g * HS:(g + 1) * HS], start=True, stop=True)
                        for c in range(NCH):
                            last = nc.tensor.matmul(PS[0:SC_, 4, c * C:(c + 1) * C], hb[:, c * SC_:(c + 1) * SC_], aw[:, 2, :],
                                                    start=True, stop=True)
                        last.then_inc(at_pe, 1)
                        with pe.Fori(0, NCH) as i:
                            di = d0 + i * ADVE_I + 2
                            wait_for(pe, at_dve, di + 1)
                            for g in range(2):
                                last = nc.tensor.matmul(PS[0:SC_, g, 0:HS], qi[:, :], kT_[:, g * HS:(g + 1) * HS], start=True, stop=True)
                            last.then_inc(at_pe, 1)
                            wait_for(pe, at_dve, di + 5)
                            for c in range(NCH):
                                last = nc.tensor.transpose(PS[0:SC_, 2 + c // 3, (c % 3) * SC_:(c % 3 + 1) * SC_],
                                                           arow[:, c * SC_:(c + 1) * SC_], idn[0:SC_, 0:SC_])
                            last.then_inc(at_pe, 1)
                            wait_for(pe, at_dve, di + 6)
                            for c in range(NCH):
                                last = nc.tensor.matmul(PS[0:C, 5, 0:SC_], vk[:, c, :], aT[:, c, :], start=(c == 0), stop=(c == NCH - 1))
                            last.then_inc(at_pe, 1)
                        wait_for(pe, at_dve, d0 + 2 + NCH * ADVE_I)
                        for g in range(2):
                            last = nc.tensor.matmul(PS[0:C, 6 + g, 0:HS], aw[:, 3, :], oT[:, g * HS:(g + 1) * HS], start=True, stop=True)
                        last.then_inc(at_pe, 1)
                    pe.reg_add(runs_a, runs_a, 1)
                with pe.If((c_ & 1) > 0):
                    na = pe.snap(runs_a, min_val=0, max_val=NB_)
                    nf = pe.snap(runs_f, min_val=0, max_val=NB_)
                    for t in range(T):
                        wait_for(pe, h_upd, na * T + nf * T + t + 1)
                        for j in range(TB):
                            k = t * TB + j
                            if t == 0:
                                wait_for(pe, fw1_ld[j], nf * 16 + 16)
                            if k == 2:
                                wait_for(pe, h_upd, na * T + nf * T + T)
                            if k >= 3:
                                wait_for(pe, relu_rdy, nf * B + k - 2)
                            for g in range(2):
                                nc.tensor.matmul(PS[:, HID_BANK[k % 3] + g, 0:HS], fw1[:, j, :], cut(h, t)[:, g, :],
                                                 start=True, stop=True).then_inc(f1_done, 1)
                            if k == TB:
                                wait_for(pe, fw_ld, nf * FW_DMAS + FW_DMAS)
                                second(0, nf)
                            if k == TB + 1:
                                wait_for(pe, h_upd, na * T + nf * T + T + 1)
                                first_token(h, 4)
                    second(1, nf)
                    pe.reg_add(runs_f, runs_f, 1)
                with pe.If((c_ & 1) < 1):
                    na = pe.snap(runs_a, min_val=0, max_val=NB_)
                    nf = pe.snap(runs_f, min_val=0, max_val=NB_)
                    wait_for(pe, h_upd, na * T + nf * T + T)
                    first_token(h, 4)
                pe.reg_add(steps, steps, 1)
                st = pe.snap(steps, min_val=1, max_val=NB_)
                wait_for(pe, ctrl_rdy, st + 1)
                pe.reg_load(cr, ctrl[0:1, 0:1])

        @block.scalar
        def _(act):
            act.dma_start(cst[:, 0:OFF["mean"][0]], consts[:, 0:OFF["mean"][0]]).then_inc(c0_in, 16)
            act.dma_start(x_in[:, 1, :], x[TB:B].rearrange("b c h w -> (b c) (h w)")).then_inc(x_ld[2], 16)
            def layernorm(i, eps):
                def squares(t):
                    for g in range(2):
                        act.wait_ge(xc_rdy, 2 * (T * i + t) + g + 1)
                        nc.scalar.activation(cut(sq, t)[:, g, :], PS[:, XB[i] + 2 * t + g, 0:HS], ACT.Square).then_inc(sq_rdy, 1)

                def keep(t):
                    nc.scalar.copy(cut(xc, t), half(t, XB[i])).then_inc(xc_copied, 1)

                squares(0)
                keep(0)
                squares(1)
                act.wait_ge(var_rdy, i + 1)
                nc.scalar.activation(std[:, :], PS[:, VB[i], 0:QS], ACT.Sqrt, bias=eps[:, :]).then_inc(std_rdy, 1)
                keep(1)

            def load_table(f):
                nc.scalar.activation(tab[:, :], tab[:, :], f)

            act.wait_ge(eps_set, 1)
            load_table(ACT.Sqrt)
            layernorm(0, eps6)
            load_table(ACT.Exp)
            act.wait_ge(border0, 1)
            def qkv_out(i):
                w, t, bank = QKV[i]
                act.wait_ge(qkv_done, i + 1)
                src = PS[:, bank:bank + 2, 0:HS]
                if w == 0:
                    nc.scalar.copy(cut(q_sb, t), src).then_inc(qkv_rdy, 1)
                else:
                    nc.scalar.copy(inner((kpad, vpad)[w - 1], t), rows24(src)).then_inc(qkv_rdy, 1)

            for i in range(4):
                qkv_out(i)
            for m in range(NBR // TRI):
                act.wait_ge(sdiff_rdy, m + 1)
                nc.scalar.activation(att[:, m * TRI:(m + 1) * TRI, :], att[:, m * TRI:(m + 1) * TRI, :], ACT.Exp,
                                     scale=HD ** -0.5).then_inc(sexp_rdy, 1)
            qkv_out(4)
            qkv_out(5)
            load_table(ACT.Sqrt)

            layernorm(1, eps5)
            load_table(ACT.Exp)
            act.wait_ge(logit_done, 1)
            act.wait_ge(gb_ld, 16)
            nc.scalar.activation(logit[:, :].rearrange("p (g s) -> p g s", g=2), PS[:, 4:6, 0:HS], ACT.Identity,
                                 bias=gb[:, :]).then_inc(logit_rdy, 1)
            act.wait_ge(ntop_rdy, 1)
            nc.scalar.activation(prob[:, :], logit[:, :], ACT.Exp, bias=ntop[:, :], accum_out=psum_[:, :]).then_inc(prob_rdy, 1)
            for c in range(0, FULL + 1, 2):
                act.wait_ge(yT_done, c // 2 + 1)
                n, w = (2, P) if c < FULL else (1, TAIL)
                nc.scalar.copy(yT[0:w, c:c + n, :, :].rearrange("k c t p -> k (c t p)"), PS[0:w, c // 2, 0:n * T * P]).then_inc(yT_rdy, 1)
            load_table(ACT.Gelu)
            act.wait_ge(pool_done, 1)
            act.wait_ge(border0, 1)
            for j in (2, 3):
                for e in range(TB):
                    last = nc.scalar.copy(pool_dst(j, e), pool_src(j, e))
            last.then_inc(pool_act, 1)
            act.wait_ge(hid_done, 1)
            nc.scalar.activation(hid[:, :], PS[:, 0, 0:H1], ACT.Gelu).then_inc(hid_rdy, 1)
            load_table(ACT.Sqrt)

            layernorm(2, eps6)
            for i in range(PAIRS):
                act.wait_ge(u_done, i + 1)
                n = min(2, NPT - 2 * i)
                nc.scalar.copy(patch_pair(uT, i), PS[:, (5 + i) % 8, 0:n * T * P].rearrange("k (p b) -> k p b", p=n)).then_inc(u_rdy, 1)

            def cval_quad(k):
                g0, n = QUADS[k]
                act.wait_ge(gram_done, k + 1)
                full = n if g0 + n < NGRP else n - 1
                last = nc.scalar.copy(cval[:, g0:g0 + full, :],
                                      PS[0:GW, CVAL_BANK[k], 0:full * V2].rearrange("p (g c) -> p g c", c=V2))
                if full < n:
                    last = nc.scalar.copy(cval[0:last_w, NGRP - 1, :], PS[0:last_w, CVAL_BANK[k], full * V2:n * V2])
                last.then_inc(cval_rdy, 1)

            def yv_copy(k):
                g0, n = QUADS[k]
                act.wait_ge(yv_done, k + 1)
                w = (n - 1) * GW + gw_of(g0 + n - 1)
                nc.scalar.copy(yvT[:, g0 * GW:g0 * GW + w], PS[0:V2, YV_BANK[k], 0:w]).then_inc(yv_rdy, 1)

            for k in range(4):
                cval_quad(k)
            yv_copy(0)
            cval_quad(4)
            for k in range(1, 5):
                yv_copy(k)

            layernorm(3, eps5)
            runs_a, runs_f, steps, cr = (act.alloc_register(n) for n in ("act_a", "act_f", "act_steps", "act_code"))
            for r in (runs_a, runs_f, steps):
                act.reg_mov(r, 0)
            act.wait_ge(ctrl_rdy, 1)
            act.reg_load(cr, ctrl[0:1, 0:1])
            with act.While(lambda: act.snap(cr) < NONE):
                c_ = act.snap(cr, min_val=0, max_val=4 * NB_ * NOPS - 1)
                with act.If((c_ & 2) > 0):
                    na = act.snap(runs_a, min_val=0, max_val=NB_)
                    with act.Fori(0, B) as b:
                        with act.Fori(0, NCH) as i:
                            wait_for(act, at_dve, na * ADVE_R + 1 + b * ADVE_B + 2 + i * ADVE_I + 3)
                            nc.scalar.activation(prow[:, :].rearrange("p (g s) -> p g s", g=2), PS[0:SC_, 0:2, 0:HS], ACT.Exp,
                                                 scale=C ** -0.5, bias=nmax[:, 1:2], accum_out=rsum[:, :]).then_inc(at_act, 1)
                    act.reg_add(runs_a, runs_a, 1)
                with act.If((c_ & 1) > 0):
                    nf = act.snap(runs_f, min_val=0, max_val=NB_)
                    load_table(ACT.Relu)
                    wait_for(act, fb1_ld, nf * 16 + 16)
                    for k in range(B):
                        for g in range(2):
                            wait_for(act, f1_done, nf * (2 * B) + 2 * k + g + 1)
                            last = nc.scalar.activation(relu_h[:, k, g * HS:(g + 1) * HS], PS[:, HID_BANK[k % 3] + g, 0:HS],
                                                        ACT.Relu, bias=fb1[:, :])
                        last.then_inc(relu_rdy, 1)
                    act.reg_add(runs_f, runs_f, 1)
                act.reg_add(steps, steps, 1)
                wait_for(act, ctrl_rdy, act.snap(steps, min_val=1, max_val=NB_) + 1)
                act.reg_load(cr, ctrl[0:1, 0:1])

        @block.vector
        def _(dve):
            nc.vector.memset(spread[:, :, :, :], 0.0).then_inc(spread_zero, 1)
            dve.wait_ge(spread_zero, 1)
            dve.wait_ge(c1_in, 16)
            for q in range(4):
                rows = slice(32 * q, 32 * q + 32)
                last = nc.vector.tensor_copy(spread[rows, :, q, :], con("heads", 32, 32 * q).rearrange("p (t m) -> p t m", t=T))
            last.then_inc(spread_rdy, 1)
            dve.wait_ge(bd_zero, 1)
            dve.wait_ge(wT_done, 1)
            for j in range(TB):
                rows = slice(j * C, (j + 1) * C)
                last = nc.vector.tensor_copy(qkv_bd[rows, :, j * C:(j + 1) * C], PS[0:C, 7, 0:96].rearrange("p (s o) -> p s o", s=3))
            last.then_inc(wT_copied, 1)

            def layernorm(i, dst):
                dve.wait_ge(std_rdy, i + 1)
                nc.vector.reciprocal(rstd[:, :], std[:, :]).then_inc(rstd_rdy, 1)
                if i == 0:
                    for j in range(TB):
                        rows = slice(j * C, (j + 1) * C)
                        nc.vector.tensor_copy(gate_bd[rows, j * E_:(j + 1) * E_], PS[0:C, 7, 96:96 + E_])
                        last = nc.vector.tensor_copy(conv_bd[rows, j * C:(j + 1) * C], PS[0:C, 7, 112:112 + C])
                    last.then_inc(wT_copied, 1)
                for t in range(T):
                    dve.wait_ge(xc_copied, T * i + t + 1)
                    dve.wait_ge(rwide_rdy, T * i + t + 1)
                    nc.vector.tensor_tensor(cut(dst, t), half(t, VB[i]), cut(xc, t), ALU.mult).then_inc(y_sem[i], 1)

            layernorm(0, y)

            for t in range(T):
                for n in range(NDVE):
                    dy, dx = divmod(n, 3)
                    if n == 0:
                        dve.wait_ge(qkv_rdy, 2 * t + 2)
                    nc.vector.tensor_tensor(prods[:, t, n, :].rearrange("p (r c) -> p r c", c=WW),
                                            q_sb[:, t, :].rearrange("p (r c) -> p r c", c=WW),
                                            kpad[:, t, dy:dy + HH, dx:dx + WW], ALU.mult).then_inc(prod_rdy, 1)
            dve.wait_ge(mab_done, 1)
            dve.wait_ge(xT_ones, 2)
            nc.vector.tensor_copy(mab[0:V2 + 1, 0:V2 + 1], PS[0:V2 + 1, 7, 0:V2 + 1])
            nc.vector.tensor_copy(wcT[0:V2 + 1, :].rearrange("k (r c) -> k r c", r=RV),
                                  PS[0:V2 + 1, 7, P:P + R2].rearrange("k (r c) -> k r c", r=R)[:, 0:RV, 0:RV]).then_inc(mab_copied, 1)
            dve.wait_ge(score_rdy, 2)
            nc.vector.tensor_reduce(smax2[:, 0, :], PS[:, 4:6, 0:TRI * QS].rearrange("p b (m s) -> p s b m", s=QS), AX.XY, ALU.max)
            dve.wait_ge(score_rdy, 3)
            nc.vector.tensor_reduce(smax2[:, 1, :], PS[:, 6, 0:TRI * QS].rearrange("p (m s) -> p s m", s=QS), AX.X,
                                    ALU.max).then_inc(smax_rdy, 1)
            dve.wait_ge(smax_rdy, 1)
            nc.vector.tensor_tensor(smax[:, :], smax2[:, 0, :], smax2[:, 1, :], ALU.max).then_inc(smax_rdy, 1)
            dve.wait_ge(smax_rdy, 2)
            part = [P, TRI, QS]
            for m in range(NBR // TRI):
                nc.vector.tensor_tensor(att[:, m * TRI:(m + 1) * TRI, :], PS[:, 4 + m, 0:TRI * QS].rearrange("p (m s) -> p m s", s=QS),
                                        smax[:, :].unsqueeze(1).to_broadcast(part), ALU.subtract).then_inc(sdiff_rdy, 1)
            dve.wait_ge(sexp_rdy, 3)
            nc.vector.tensor_reduce(ssum[:, :], att[:, :, :].rearrange("p n s -> p s n"), AX.X, ALU.add).then_inc(ssum_rdy, 1)
            dve.wait_ge(ssum_rdy, 1)
            nc.vector.reciprocal(srec[:, :], ssum[:, :]).then_inc(ssum_rdy, 1)
            dve.wait_ge(ssum_rdy, 2)
            def spread_product(u, m):
                t, m3 = divmod(u, NBR // TRI)
                dy, dx = divmod(m3 * TRI + m, 3)
                base = WIDE_BANK[u % 2]
                return nc.vector.tensor_tensor(
                    prods[:, t, m3 * TRI + m, :].rearrange("p (q r c) -> p q r c", q=4, c=WW),
                    PS[:, base:base + 4, m * QS:(m + 1) * QS].rearrange("p q (r c) -> p q r c", c=WW),
                    vpad[:, t, dy:dy + HH, dx:dx + WW].rearrange("p (q r) c -> p q r c", q=4), ALU.mult)

            dve.wait_ge(qkv_rdy, 6)
            for u in range(WIDE - 1):
                t, m3 = divmod(u, NBR // TRI)
                dve.wait_ge(wide_rdy, u + 1)
                for m in range(TRI):
                    last = spread_product(u, m)
                if u in (1, 2):
                    base = WIDE_BANK[u % 2]
                    last = nc.vector.tensor_copy(rtile[:, :, (u - 1) * QS // 2:u * QS // 2],
                                                 PS[:, base:base + 4, TRI * QS:TRI * QS + QS // 2])
                last.then_inc(wide_used, 1)
                dve.wait_ge(wide_used, u + 1)
                a, b = prods[:, t, m3 * TRI, :], prods[:, t, m3 * TRI + 1, :]
                nc.vector.tensor_tensor(a, a, b, ALU.add).then_inc(pair_rdy, 1)
                if u == NBR // TRI:
                    dve.wait_ge(acc_rdy, 2)
                    nc.vector.tensor_tensor(prods[:, 0, 0, :], prods[:, 0, 0, :], rtile[:, :, :].rearrange("p q s -> p (q s)"),
                                            ALU.mult).then_inc(scaled_rdy, 1)
            dve.wait_ge(wide_rdy, WIDE)
            for m in range(TRI):
                spread_product(WIDE - 1, m).then_inc(tail_rdy, 1)
            total = prods[:, 1, 4, :]
            a, b, c = (prods[:, 1, NBR - TRI + m, :] for m in range(TRI))
            dve.wait_ge(tail_rdy, TRI)
            dve.wait_ge(trio_rdy, 5)
            nc.vector.tensor_tensor(total, a, b, ALU.add).then_inc(total_rdy, 1)
            dve.wait_ge(total_rdy, 1)
            nc.vector.tensor_tensor(total, total, prods[:, 1, TRI, :], ALU.add).then_inc(total_rdy, 1)
            dve.wait_ge(acc_rdy, 3)
            nc.vector.tensor_tensor(xs[1][:, 1, :], c, prods[:, 1, 1, :], ALU.add).then_inc(total_rdy, 1)
            dve.wait_ge(total_rdy, 3)
            nc.vector.tensor_tensor(xs[1][:, 1, :], xs[1][:, 1, :], total, ALU.add).then_inc(x1_rdy, 1)

            layernorm(1, y)
            dve.wait_ge(logit_rdy, 1)
            nc.vector.max(top8[:, :], logit[:, :]).then_inc(top_rdy, 1)
            dve.wait_ge(top_rdy, 1)
            nc.vector.tensor_scalar(ntop[:, :], top8[:, 0:1], -1.0, None, ALU.mult).then_inc(ntop_rdy, 1)
            nc.vector.match_replace(rest[:, :], top8[:, :], logit[:, :], -3e38).then_inc(rest_rdy, 1)
            dve.wait_ge(rest_rdy, 1)
            nc.vector.tensor_tensor(ismine[:, :], logit[:, :], rest[:, :], ALU.not_equal).then_inc(mine_rdy, 1)
            dve.wait_ge(prob_rdy, 1)
            nc.vector.reciprocal(prec[:, :], psum_[:, :]).then_inc(prec_rdy, 1)
            dve.wait_ge(prec_rdy, 1)
            dve.wait_ge(mine_rdy, 1)
            nc.vector.scalar_tensor_tensor(pick[:, :], prob[:, :], prec[:, :], ismine[:, :], ALU.mult, ALU.mult).then_inc(pick_rdy, 1)
            for i, (n, w) in enumerate(((FULL, P), (1, TAIL))):
                dve.wait_ge(pickT_done, i + 1)
                nc.vector.tensor_copy(pickT[0:w, FULL * i:FULL * i + n, :].rearrange("k c p -> k (c p)"),
                                      PS[0:w, 6 + i, 0:n * P]).then_inc(pickT_rdy, 1)
            dve.wait_ge(border0, 1)
            dve.wait_ge(pool_done, 1)
            for j in (0, 1):
                for e in range(TB):
                    last = nc.vector.tensor_copy(pool_dst(j, e), pool_src(j, e))
            last.then_inc(pool_dve, 1)
            dve.wait_ge(hidT_done, 1)
            nc.vector.tensor_copy(hidT[:, :], PS[:, 1, 0:P]).then_inc(hidT_rdy, 1)
            dve.wait_ge(eo_done, 1)
            nc.vector.tensor_copy(eoutT[:, :], PS[0:C, 2, 0:P]).then_inc(eo_rdy, 1)
            dve.wait_ge(eoT_done, 1)
            nc.vector.tensor_tensor(eout_bd[:, :, :], PS[:, 3, 256:256 + C].unsqueeze(1).to_broadcast([P, TB, C]),
                                    con("own").unsqueeze(2).to_broadcast([P, TB, C]), ALU.mult).then_inc(eobd_rdy, 1)
            dve.wait_ge(x1_half, 1)
            dve.wait_ge(x1_rdy, 1)
            for t in range(T):
                dve.wait_ge(scat_done, t + 1)
                for i in range(NP):
                    last = nc.vector.tensor_tensor(xs[2][:, t, i * BAND:(i + 1) * BAND].rearrange("p (j r c) -> p j r c", j=NP, r=RV),
                                                   band(4 + 2 * t, i), patches(xs[1][:, t, :], i), ALU.add)
                last.then_inc(x2_rdy, 1)

            layernorm(2, y)
            xT4 = xT[0:V2, :].rearrange("k (t b p) -> k p t b", t=T, p=NPT)
            dve.wait_ge(wconv_ld, 16 * 10)
            dve.wait_ge(xT_ones, 3)
            for i in range(5):
                dve.wait_ge(pT_done, i + 1)
                n = min(2, NPT - 2 * i)
                nc.vector.tensor_tensor(xT4[:, 2 * i:2 * i + n, :, :],
                                        PS[0:V2, i, 0:n * T * P].rearrange("k (p t b) -> k p t b", p=n, t=T),
                                        bc_rows[:, :].unsqueeze(1).unsqueeze(1).to_broadcast([V2, n, T, P]), ALU.add).then_inc(xT_rdy, 1)
            for k, (g0, n) in enumerate(QUADS):
                dve.wait_ge(gram_done, k + 1)
                full = n if g0 + n < NGRP else n - 1
                last = nc.vector.tensor_tensor(gram[:, g0:g0 + full, :],
                                               PS[0:GW, GRAM_BANK[k], 0:full * GW].rearrange("p (g c) -> p g c", c=GW),
                                               con("blk", GW).unsqueeze(1).to_broadcast([GW, full, GW]), ALU.mult)
                if full < n:
                    last = nc.vector.tensor_tensor(gram[0:last_w, NGRP - 1, 0:last_w],
                                                   PS[0:last_w, GRAM_BANK[k], full * GW:full * GW + last_w],
                                                   con("blk", last_w)[:, 0:last_w], ALU.mult)
                last.then_inc(gram_rdy, 1)
            for t in range(T):
                dve.wait_ge(back_done, t + 1)
                for b, n in ((0, 2 * BAND), (1, BAND)):
                    px = slice(2 * BAND * b, 2 * BAND * b + n)
                    last = nc.vector.tensor_tensor(xs[3][:, t, px], PS[:, BACK_BANK[t] + b, 0:n], xs[2][:, t, px], ALU.add)
                last.then_inc(x3_rdy, 1)

            dve.wait_ge(code_st, 8)
            runs_a, runs_f, steps, cr = (dve.alloc_register(n) for n in ("dve_a", "dve_f", "dve_steps", "dve_code"))
            for r in (runs_a, runs_f, steps):
                dve.reg_mov(r, 0)

            CTL = 6

            def choose(n, bank, add_tile0=False):
                base = n * CTL
                wait_for(dve, row_done, n + 1)
                token = PS[0:1, bank, 0:NOPS]
                nc.vector.max(rmax[:, :], token).then_inc(ctl_step, 1)
                if add_tile0:
                    band_add(nc.vector, 0, 0)
                wait_for(dve, ctl_step, base + 1)
                nc.vector.max_index(ridx[:, :], rmax[:, :], token).then_inc(ctl_step, 1)
                if add_tile0:
                    band_add(nc.vector, 0, 1)
                wait_for(dve, ctl_step, base + 2)
                nc.vector.tensor_copy(opf[:, :], ridx[:, 0:1]).then_inc(ctl_step, 1)
                if add_tile0:
                    band_add(nc.vector, 0, 2).then_inc(fin_rdy, 1)
                wait_for(dve, ctl_step, base + 3)
                nc.vector.tensor_scalar(hot[:, :], con("iop", 1), opf[:, :], None, ALU.is_equal).then_inc(ctl_step, 1)
                wait_for(dve, ctl_step, base + 4)
                nc.vector.tensor_tensor(csel[:, :, :], code[:, :, :], hot[:, :].unsqueeze(1).to_broadcast([1, NB_, NOPS]),
                                        ALU.mult).then_inc(ctl_step, 1)
                wait_for(dve, ctl_step, base + 5)
                nc.vector.tensor_reduce(cand[:, :], csel[:, :, :], AX.X, ALU.add).then_inc(ctl_step, 1)
                wait_for(dve, ctl_step, base + 6)
                nc.vector.tensor_reduce(ctrl[:, 0:1], cand[:, :], AX.X, ALU.min).then_inc(ctrl_rdy, 1)
                nc.vector.tensor_reduce(nextf[:, :], cand[:, :], AX.X, ALU.min).then_inc(next_rdy, 1)

            def strike_out(n):
                wait_for(dve, next_rdy, n + 1)
                nc.vector.tensor_scalar(late[:, :], con("istep", 1), nextf[:, :], float(NONE), ALU.is_le, ALU.mult).then_inc(late_rdy, 1)
                wait_for(dve, late_rdy, 2 * n + 1)
                nc.vector.tensor_tensor(code[:, :, :], code[:, :, :], late[:, :].unsqueeze(2).to_broadcast([1, NB_, NOPS]),
                                        ALU.add).then_inc(late_rdy, 1)
                wait_for(dve, late_rdy, 2 * n + 2)

            dve.sem_inc(fw_free, 1)
            choose(0, 6)
            layernorm(3, h)
            dve.wait_ge(ctrl_rdy, 1)
            dve.reg_load(cr, ctrl[0:1, 0:1])

            def new_h(t):
                nf = dve.snap(runs_f, min_val=0, max_val=NB_)
                if t == 0:
                    dve.wait_ge(fin_rdy, T)
                wait_for(dve, z_done, nf * T + t + 1)
                if t == T - 1:
                    wait_for(dve, x3b_rdy, nf + 1)
                    for i in range(NP):
                        px = slice(i * BAND, (i + 1) * BAND)
                        last = nc.vector.tensor_tensor(patches(y[:, t, :], i), band(4 + 2 * t, i),
                                                       x3b[:, px].rearrange("p (j r c) -> p j r c", j=NP, r=RV), ALU.add)
                    last.then_inc(fin_rdy, 1)
                nc.vector.tensor_scalar(h[:, t, 0:2 * BAND], PS[:, 4 + 2 * t, 0:2 * BAND], fb2[:, :], None, ALU.add)
                nc.vector.tensor_scalar(h[:, t, 2 * BAND:S], PS[:, 5 + 2 * t, 0:BAND], fb2[:, :], None, ALU.add).then_inc(h_upd, 1)

            with dve.While(lambda: dve.snap(cr) < NONE):
                strike_out(dve.snap(steps, min_val=0, max_val=NB_))
                c_ = dve.snap(cr, min_val=0, max_val=4 * NB_ * NOPS - 1)
                with dve.If((c_ & 2) > 0):
                    na = dve.snap(runs_a, min_val=0, max_val=NB_)
                    wait_for(dve, h_upd, na * T + dve.snap(runs_f, min_val=0, max_val=NB_) * T + T)
                    for j in range(TB):
                        last = nc.vector.tensor_copy(h0[:, j::TB, :], h[j * C:(j + 1) * C, :, :])
                    last.then_inc(at_dve, 1)
                    with dve.Fori(0, B) as b:
                        d0 = na * ADVE_R + 1 + b * ADVE_B
                        p0 = na * (B * APE_B) + b * APE_B
                        wait_for(dve, at_dve, d0)
                        nc.vector.tensor_copy(hb[:, :], h0[:, bass.ds(b, 1), :].rearrange("c b s -> c (b s)")).then_inc(at_dve, 1)
                        wait_for(dve, at_pe, p0 + 1)
                        nc.vector.tensor_copy(qT_[:, :].rearrange("p (g s) -> p g s", g=2), PS[0:C, 0:2, 0:HS])
                        nc.vector.tensor_copy(kT_[:, :].rearrange("p (g s) -> p g s", g=2), PS[0:C, 2:4, 0:HS])
                        nc.vector.tensor_copy(vk[:, :, :].rearrange("k c d -> k (c d)"), PS[0:SC_, 4, 0:NCH * C]).then_inc(at_dve, 1)
                        with dve.Fori(0, NCH) as i:
                            di = d0 + 2 + i * ADVE_I
                            pi = p0 + 1 + i * APE_I
                            wait_for(dve, at_dve, di)
                            nc.vector.tensor_copy(qi[:, :], qT_[:, bass.ds(i * SC_, SC_)]).then_inc(at_dve, 1)
                            wait_for(dve, at_pe, pi + 1)
                            nc.vector.tensor_reduce(nmax[:, 0:1], PS[0:SC_, 0:2, 0:HS], AX.XY, ALU.max, negate=True).then_inc(at_dve, 1)
                            wait_for(dve, at_dve, di + 2)
                            nc.vector.tensor_scalar(nmax[:, 1:2], nmax[:, 0:1], C ** -0.5, None, ALU.mult).then_inc(at_dve, 1)
                            wait_for(dve, at_act, (na * B + b) * AACT_B + i + 1)
                            nc.vector.reciprocal(rrec[:, :], rsum[:, :]).then_inc(at_dve, 1)
                            wait_for(dve, at_dve, di + 4)
                            nc.vector.tensor_scalar(arow[:, :], prow[:, :], rrec[:, :], None, ALU.mult).then_inc(at_dve, 1)
                            wait_for(dve, at_pe, pi + 2)
                            nc.vector.tensor_copy(aT[:, :, :].rearrange("k (g c) q -> k g (c q)", g=2), PS[0:SC_, 2:4, 0:HS]).then_inc(at_dve, 1)
                            wait_for(dve, at_pe, pi + 3)
                            nc.vector.tensor_copy(oT[:, bass.ds(i * SC_, SC_)], PS[0:C, 5, 0:SC_]).then_inc(at_dve, 1)
                        wait_for(dve, at_pe, p0 + APE_B)
                        nc.vector.tensor_copy(h0[:, bass.ds(b, 1), :].rearrange("c b (g s) -> c (b g) s", g=2), PS[0:C, 6:8, 0:HS]).then_inc(at_dve, 1)
                    dve.wait_ge(fin_rdy, T)
                    wait_for(dve, at_dve, na * ADVE_R + ADVE_R)
                    for j in range(TB):
                        last = nc.vector.tensor_copy(h[j * C:(j + 1) * C, :, :], h0[:, j::TB, :])
                    last.then_inc(h_upd, T)
                    dve.reg_add(runs_a, runs_a, 1)
                with dve.If((c_ & 1) > 0):
                    nf = dve.snap(runs_f, min_val=0, max_val=NB_)
                    wait_for(dve, fw_ld, nf * FW_DMAS + FW_DMAS)
                    nc.vector.tensor_scalar(x3b[:, :], xs[3][:, T - 1, :], fb2[:, :], None, ALU.add).then_inc(x3b_rdy, 1)
                    new_h(0)
                dve.reg_add(steps, steps, 1)
                choose(dve.snap(steps, min_val=1, max_val=NB_), 4, add_tile0=True)
                with dve.If((c_ & 1) > 0):
                    new_h(1)
                    dve.reg_add(runs_f, runs_f, 1)
                with dve.If((c_ & 1) < 1):
                    final_add(nc.vector, 1)
                wait_for(dve, h_upd, T * (dve.snap(runs_a, min_val=0, max_val=NB_) + dve.snap(runs_f, min_val=0, max_val=NB_)) + T)
                dve.sem_inc(fw_free, 1)
                wait_for(dve, ctrl_rdy, dve.snap(steps, min_val=1, max_val=NB_) + 1)
                dve.reg_load(cr, ctrl[0:1, 0:1])


def kernel(**inputs):
    from concourse import bacc
    from concourse.bass_utils import run_bass_kernel_spmd

    nc = bacc.Bacc("TRN2", target_bir_lowering=False, num_devices=1)
    arrays, args = {}, {}
    for name, a in inputs.items():
        a = np.ascontiguousarray(a)
        if a.dtype == np.bool_:
            padded = np.zeros((1, 4 * MWORDS), np.bool_)
            padded[0, :a.size] = a.ravel()
            a = padded.view(np.int32)
        arrays["in_" + name] = a
        args[name] = nc.dram_tensor("in_" + name, a.shape, mybir.dt.from_np(a.dtype), kind="ExternalInput").ap()
    arrays["consts"] = constant_table()
    args["consts"] = nc.dram_tensor("consts", (P, NCST), mybir.dt.float32, kind="ExternalInput").ap()
    arrays["row_codes"] = row_table()
    args["row_codes"] = nc.dram_tensor("row_codes", (1, NB_ * NOPS), mybir.dt.float32, kind="ExternalInput").ap()
    args["out"] = nc.dram_tensor("result", (B, C, HH, WW), mybir.dt.float32, kind="ExternalOutput").ap()
    metaformer(nc, **args)
    return run_bass_kernel_spmd(nc, [arrays], core_ids=[0]).results[0]["result"]
```
